# Optimizing a Trainium2 kernel written in Bass

```python
import numpy as np
import jax
import jax.numpy as jnp

def _softmax(x, axis=-1):
    return jax.nn.softmax(x, axis=axis)

def _gelu(x):
    return jax.nn.gelu(x, approximate=True)

def _silu(x):
    return jax.nn.silu(x)

def _sigmoid(x):
    return jax.nn.sigmoid(x)

def _layernorm(x, axis=-1, eps=1e-05):
    m = jnp.mean(x, axis=axis, keepdims=True)
    v = jnp.var(x, axis=axis, keepdims=True)
    return (x - m) / jnp.sqrt(v + eps)

def _scatter_add(tgt, idx, src, axis=0):
    return tgt.at[idx].add(src)

def _segment_sum(src, seg, n):
    return jax.ops.segment_sum(src, seg, n)
kernel_name = 'mk_seq_preln_d4_jaxref_r8_3aa8cc'

def setup_inputs(seed: int=0):
    np.random.seed(seed)
    _w = jnp.asarray

    def _L0_attn_setup():
        import jax, jax.numpy as jnp
        import numpy as np
        B, N, DIM = (2, 256, 128)
        HEADS, DHEAD = (16, 64)
        GNN_DEPTH = 2
        EPS = 1e-05

        def layer_norm(x, gamma):
            mu = jnp.mean(x, axis=-1, keepdims=True)
            var = jnp.var(x, axis=-1, keepdims=True)
            return (x - mu) / jnp.sqrt(var + EPS) * gamma
        key = jax.random.key(seed)
        ks = jax.random.split(key, 12)
        hd = HEADS * DHEAD
        s = lambda fan: 1.0 / np.sqrt(fan)
        return {'x': jax.random.normal(ks[0], (B, N, DIM), dtype=jnp.float32), 'gamma_in': jnp.ones((DIM,), dtype=jnp.float32), 'Wq': jax.random.normal(ks[1], (DIM, hd), dtype=jnp.float32) * s(DIM), 'Wk': jax.random.normal(ks[2], (DIM, hd), dtype=jnp.float32) * s(DIM), 'Wv': jax.random.normal(ks[3], (DIM, hd), dtype=jnp.float32) * s(DIM), 'gnn_w': jax.random.normal(ks[4], (GNN_DEPTH, DHEAD, DHEAD), dtype=jnp.float32) * s(DHEAD), 'gnn_b': jnp.zeros((GNN_DEPTH, DHEAD), dtype=jnp.float32), 'lin_w': jax.random.normal(ks[5], (DHEAD, DHEAD), dtype=jnp.float32) * s(DHEAD), 'lin_b': jnp.zeros((DHEAD,), dtype=jnp.float32), 'Wo': jax.random.normal(ks[6], (hd, DIM), dtype=jnp.float32) * s(hd), 'gamma_out': jnp.ones((DIM,), dtype=jnp.float32)}
    _L0_attn_in = _L0_attn_setup()

    def _L0_ffn_setup():
        import jax, jax.numpy as jnp
        import numpy as np
        B, S, D_MODEL, D_FF = (4, 256, 128, 512)

        def _quantum_transform(hidden, theta, w_real, w_imag):
            imag = w_imag * jnp.sin(theta + hidden * 0.1)
            quantum_phase = jnp.cos(theta) * w_real + jnp.sin(theta) * w_imag
            return hidden + quantum_phase * imag * 0.1
        key = jax.random.key(seed)
        ks = jax.random.split(key, 8)
        return {'x': jax.random.normal(ks[0], (B, S, D_MODEL), dtype=jnp.float32), 'W1': jax.random.normal(ks[1], (D_MODEL, D_FF), dtype=jnp.float32) * (1.0 / np.sqrt(D_MODEL)), 'b1': jnp.zeros((D_FF,), dtype=jnp.float32), 'quantum_phases': jax.random.normal(ks[2], (D_FF,), dtype=jnp.float32) * (2.0 * np.pi), 'quantum_weights_real': jax.random.normal(ks[3], (D_FF,), dtype=jnp.float32) * 0.1, 'quantum_weights_imag': jax.random.normal(ks[4], (D_FF,), dtype=jnp.float32) * 0.1, 'W2': jax.random.normal(ks[5], (D_FF, D_MODEL), dtype=jnp.float32) * (1.0 / np.sqrt(D_FF)), 'b2': jnp.zeros((D_MODEL,), dtype=jnp.float32)}
    _L0_ffn_in = _L0_ffn_setup()

    def _L1_attn_setup():
        import jax, jax.numpy as jnp
        import numpy as np
        DIM_IN, DIM_OUT, DIM_INNER = (128, 128, 64)
        key = jax.random.key(seed)
        k1, k2, k3, k4 = jax.random.split(key, 4)
        x = jax.random.normal(k1, (4, 256, DIM_IN), dtype=jnp.float32)
        w_qkv = jax.random.uniform(k2, (DIM_INNER * 3, DIM_IN), dtype=jnp.float32, minval=-1.0, maxval=1.0) / np.sqrt(DIM_IN)
        w_out = jax.random.uniform(k3, (DIM_OUT, DIM_INNER), dtype=jnp.float32, minval=-1.0, maxval=1.0) / np.sqrt(DIM_INNER)
        b_out = jax.random.uniform(k4, (DIM_OUT,), dtype=jnp.float32, minval=-1.0, maxval=1.0) / np.sqrt(DIM_INNER)
        return {'x': x, 'w_qkv': w_qkv, 'w_out': w_out, 'b_out': b_out}
    _L1_attn_in = _L1_attn_setup()

    def _L1_ffn_setup():
        import jax, jax.numpy as jnp
        import numpy as np
        H = 128
        I = 128
        E = 8
        key = jax.random.key(seed)
        ks = jax.random.split(key, 8)
        s = 0.02
        x = jax.random.normal(ks[0], (4, 256, H), dtype=jnp.float32)
        Wg = jax.random.normal(ks[1], (H, E), dtype=jnp.float32) * s
        bg = jnp.zeros((E,), dtype=jnp.float32)
        W1 = jax.random.normal(ks[2], (E, H, I), dtype=jnp.float32) * s
        b1 = jnp.zeros((E, I), dtype=jnp.float32)
        W2 = jax.random.normal(ks[3], (E, I, H), dtype=jnp.float32) * s
        b2 = jnp.zeros((E, H), dtype=jnp.float32)
        return {'x': x, 'Wg': Wg, 'bg': bg, 'W1': W1, 'b1': b1, 'W2': W2, 'b2': b2}
    _L1_ffn_in = _L1_ffn_setup()

    def _L2_attn_setup():
        import jax, jax.numpy as jnp
        import numpy as np
        DIM = 128
        HEADS = 16
        HEAD_DIM = DIM // HEADS

        def feature_map(x):
            return jnp.where(x > 0, x + 1.0, jnp.exp(x))
        key = jax.random.key(seed)
        ks = jax.random.split(key, 11)
        B, N, D = (4, 1024, DIM)
        s = 1.0 / np.sqrt(D)
        inp = {'x': jax.random.normal(ks[0], (B, N, D), dtype=jnp.float32), 'wg_w': jax.random.normal(ks[1], (D, D), dtype=jnp.float32) * s, 'wg_b': jnp.zeros((D,), dtype=jnp.float32), 'wq_w': jax.random.normal(ks[2], (D, D), dtype=jnp.float32) * s, 'wq_b': jnp.zeros((D,), dtype=jnp.float32), 'wk_w': jax.random.normal(ks[3], (D, D), dtype=jnp.float32) * s, 'wk_b': jnp.zeros((D,), dtype=jnp.float32), 'wv_w': jax.random.normal(ks[4], (D, D), dtype=jnp.float32) * s, 'wv_b': jnp.zeros((D,), dtype=jnp.float32), 'out_w': jax.random.normal(ks[5], (D, D), dtype=jnp.float32) * s, 'out_b': jnp.zeros((D,), dtype=jnp.float32)}
        return inp
    _L2_attn_in = _L2_attn_setup()

    def _L2_ffn_setup():
        import jax, jax.numpy as jnp
        import numpy as np
        E = 8
        K = 2
        CF = 1.25
        key = jax.random.key(seed)
        kx, kr, kg, ku, kd = jax.random.split(key, 5)
        D, F = (128, 512)
        x = jax.random.normal(kx, (4, 256, D), dtype=jnp.float32)
        router_w = 0.02 * jax.random.normal(kr, (E, D), dtype=jnp.float32)
        wg = jax.random.normal(kg, (E, D, F), dtype=jnp.float32) / np.sqrt(D)
        wu = jax.random.normal(ku, (E, D, F), dtype=jnp.float32) / np.sqrt(D)
        wd = jax.random.normal(kd, (E, F, D), dtype=jnp.float32) / np.sqrt(F)
        return {'x': x, 'router_w': router_w, 'wg': wg, 'wu': wu, 'wd': wd}
    _L2_ffn_in = _L2_ffn_setup()

    def _L3_attn_setup():
        import jax, jax.numpy as jnp
        from jax import lax
        import numpy as np
        D_MODEL = 128
        D_STATE = 16
        D_CONV = 4
        EXPAND = 2
        D_INNER = D_MODEL * EXPAND
        DT_RANK = (D_MODEL + 15) // 16
        B, T = (2, 256)

        def _silu(v):
            return v * jax.nn.sigmoid(v)
        key = jax.random.key(seed)
        ks = jax.random.split(key, 8)

        def rn(k, shape, scale):
            return jax.random.normal(k, shape, dtype=jnp.float32) * scale
        x = rn(ks[0], (B, T, D_MODEL), 1.0)
        W_in = rn(ks[1], (D_MODEL, 2 * D_INNER), D_MODEL ** (-0.5))
        conv_w = rn(ks[2], (D_INNER, D_CONV), D_CONV ** (-0.5))
        conv_b = jnp.zeros((D_INNER,), jnp.float32)
        W_x = rn(ks[3], (D_INNER, DT_RANK + 2 * D_STATE), D_INNER ** (-0.5))
        W_dt = rn(ks[4], (DT_RANK, D_INNER), DT_RANK ** (-0.5))
        b_dt = jnp.log(jnp.expm1(jnp.full((D_INNER,), 0.01, jnp.float32)))
        A_log = jnp.log(jnp.broadcast_to(jnp.arange(1, D_STATE + 1, dtype=jnp.float32), (D_INNER, D_STATE)))
        Dp = jnp.ones((D_INNER,), jnp.float32)
        W_out = rn(ks[5], (D_INNER, D_MODEL), D_INNER ** (-0.5))
        return dict(x=x, W_in=W_in, conv_w=conv_w, conv_b=conv_b, W_x=W_x, W_dt=W_dt, b_dt=b_dt, A_log=A_log, D=Dp, W_out=W_out)
    _L3_attn_in = _L3_attn_setup()

    def _L3_ffn_setup():
        import jax, jax.numpy as jnp
        import numpy as np
        D_MODEL = 128
        D_FF = 512
        NUM_EXPERTS = 8
        key = jax.random.key(seed)
        ks = jax.random.split(key, 8)
        scale_in = 1.0 / np.sqrt(D_MODEL)
        scale_ff = 1.0 / np.sqrt(D_FF)
        x = jax.random.normal(ks[0], (4, 256, D_MODEL), dtype=jnp.float32)
        gate_w = jax.random.uniform(ks[1], (NUM_EXPERTS, D_MODEL), jnp.float32, -scale_in, scale_in)
        gate_b = jax.random.uniform(ks[2], (NUM_EXPERTS,), jnp.float32, -scale_in, scale_in)
        expert_bias = jnp.zeros((NUM_EXPERTS,), dtype=jnp.float32)
        w1 = jax.random.uniform(ks[3], (NUM_EXPERTS, D_MODEL, D_FF), jnp.float32, -scale_in, scale_in)
        b1 = jax.random.uniform(ks[4], (NUM_EXPERTS, D_FF), jnp.float32, -scale_in, scale_in)
        w2 = jax.random.uniform(ks[5], (NUM_EXPERTS, D_FF, D_MODEL), jnp.float32, -scale_ff, scale_ff)
        b2 = jax.random.uniform(ks[6], (NUM_EXPERTS, D_MODEL), jnp.float32, -scale_ff, scale_ff)
        return {'x': x, 'gate_w': gate_w, 'gate_b': gate_b, 'expert_bias': expert_bias, 'w1': w1, 'b1': b1, 'w2': w2, 'b2': b2}
    _L3_ffn_in = _L3_ffn_setup()
    _d = {'L0_attn_x': _L0_attn_in['x'], 'L0_attn_gamma_in': _L0_attn_in['gamma_in'], 'L0_attn_Wq': _L0_attn_in['Wq'], 'L0_attn_Wk': _L0_attn_in['Wk'], 'L0_attn_Wv': _L0_attn_in['Wv'], 'L0_attn_gnn_w': _L0_attn_in['gnn_w'], 'L0_attn_gnn_b': _L0_attn_in['gnn_b'], 'L0_attn_lin_w': _L0_attn_in['lin_w'], 'L0_attn_lin_b': _L0_attn_in['lin_b'], 'L0_attn_Wo': _L0_attn_in['Wo'], 'L0_attn_gamma_out': _L0_attn_in['gamma_out'], 'L0_ffn_W1': _L0_ffn_in['W1'], 'L0_ffn_b1': _L0_ffn_in['b1'], 'L0_ffn_quantum_phases': _L0_ffn_in['quantum_phases'], 'L0_ffn_quantum_weights_real': _L0_ffn_in['quantum_weights_real'], 'L0_ffn_quantum_weights_imag': _L0_ffn_in['quantum_weights_imag'], 'L0_ffn_W2': _L0_ffn_in['W2'], 'L0_ffn_b2': _L0_ffn_in['b2'], 'L1_attn_w_qkv': _L1_attn_in['w_qkv'], 'L1_attn_w_out': _L1_attn_in['w_out'], 'L1_attn_b_out': _L1_attn_in['b_out'], 'L1_ffn_Wg': _L1_ffn_in['Wg'], 'L1_ffn_bg': _L1_ffn_in['bg'], 'L1_ffn_W1': _L1_ffn_in['W1'], 'L1_ffn_b1': _L1_ffn_in['b1'], 'L1_ffn_W2': _L1_ffn_in['W2'], 'L1_ffn_b2': _L1_ffn_in['b2'], 'L2_attn_wg_w': _L2_attn_in['wg_w'], 'L2_attn_wg_b': _L2_attn_in['wg_b'], 'L2_attn_wq_w': _L2_attn_in['wq_w'], 'L2_attn_wq_b': _L2_attn_in['wq_b'], 'L2_attn_wk_w': _L2_attn_in['wk_w'], 'L2_attn_wk_b': _L2_attn_in['wk_b'], 'L2_attn_wv_w': _L2_attn_in['wv_w'], 'L2_attn_wv_b': _L2_attn_in['wv_b'], 'L2_attn_out_w': _L2_attn_in['out_w'], 'L2_attn_out_b': _L2_attn_in['out_b'], 'L2_ffn_router_w': _L2_ffn_in['router_w'], 'L2_ffn_wg': _L2_ffn_in['wg'], 'L2_ffn_wu': _L2_ffn_in['wu'], 'L2_ffn_wd': _L2_ffn_in['wd'], 'L3_attn_W_in': _L3_attn_in['W_in'], 'L3_attn_conv_w': _L3_attn_in['conv_w'], 'L3_attn_conv_b': _L3_attn_in['conv_b'], 'L3_attn_W_x': _L3_attn_in['W_x'], 'L3_attn_W_dt': _L3_attn_in['W_dt'], 'L3_attn_b_dt': _L3_attn_in['b_dt'], 'L3_attn_A_log': _L3_attn_in['A_log'], 'L3_attn_D': _L3_attn_in['D'], 'L3_attn_W_out': _L3_attn_in['W_out'], 'L3_ffn_gate_w': _L3_ffn_in['gate_w'], 'L3_ffn_gate_b': _L3_ffn_in['gate_b'], 'L3_ffn_expert_bias': _L3_ffn_in['expert_bias'], 'L3_ffn_w1': _L3_ffn_in['w1'], 'L3_ffn_b1': _L3_ffn_in['b1'], 'L3_ffn_w2': _L3_ffn_in['w2'], 'L3_ffn_b2': _L3_ffn_in['b2']}
    _x0 = _d['L0_attn_x']
    _d['L0_attn_x'] = jax.random.normal(jax.random.fold_in(jax.random.key(seed), 1), (2, 1024, 128), dtype=_x0.dtype)
    del _x0
    return _d

def reference(L0_attn_x, L0_attn_gamma_in, L0_attn_Wq, L0_attn_Wk, L0_attn_Wv, L0_attn_gnn_w, L0_attn_gnn_b, L0_attn_lin_w, L0_attn_lin_b, L0_attn_Wo, L0_attn_gamma_out, L0_ffn_W1, L0_ffn_b1, L0_ffn_quantum_phases, L0_ffn_quantum_weights_real, L0_ffn_quantum_weights_imag, L0_ffn_W2, L0_ffn_b2, L1_attn_w_qkv, L1_attn_w_out, L1_attn_b_out, L1_ffn_Wg, L1_ffn_bg, L1_ffn_W1, L1_ffn_b1, L1_ffn_W2, L1_ffn_b2, L2_attn_wg_w, L2_attn_wg_b, L2_attn_wq_w, L2_attn_wq_b, L2_attn_wk_w, L2_attn_wk_b, L2_attn_wv_w, L2_attn_wv_b, L2_attn_out_w, L2_attn_out_b, L2_ffn_router_w, L2_ffn_wg, L2_ffn_wu, L2_ffn_wd, L3_attn_W_in, L3_attn_conv_w, L3_attn_conv_b, L3_attn_W_x, L3_attn_W_dt, L3_attn_b_dt, L3_attn_A_log, L3_attn_D, L3_attn_W_out, L3_ffn_gate_w, L3_ffn_gate_b, L3_ffn_expert_bias, L3_ffn_w1, L3_ffn_b1, L3_ffn_w2, L3_ffn_b2):

    def _L0_attn_ref(x, gamma_in, Wq, Wk, Wv, gnn_w, gnn_b, lin_w, lin_b, Wo, gamma_out):
        import jax, jax.numpy as jnp
        import numpy as np
        B, N, DIM = (2, 256, 128)
        HEADS, DHEAD = (16, 64)
        GNN_DEPTH = 2
        EPS = 1e-05

        def layer_norm(x, gamma):
            mu = jnp.mean(x, axis=-1, keepdims=True)
            var = jnp.var(x, axis=-1, keepdims=True)
            return (x - mu) / jnp.sqrt(var + EPS) * gamma
        b, n, _ = x.shape
        scale = DHEAD ** (-0.5)
        xn = layer_norm(x, gamma_in)
        q = (xn @ Wq).reshape(b, n, HEADS, DHEAD).transpose(0, 2, 1, 3) * scale
        k = (xn @ Wk).reshape(b, n, HEADS, DHEAD).transpose(0, 2, 1, 3)
        v = (xn @ Wv).reshape(b, n, HEADS, DHEAD).transpose(0, 2, 1, 3)
        sim = jnp.einsum('bhid,bhjd->bhij', q, k)
        mask_value = -jnp.finfo(sim.dtype).max
        causal_mask = jnp.triu(jnp.ones((n, n), dtype=bool), k=1)
        sim = jnp.where(causal_mask, mask_value, sim)
        attn = jax.nn.softmax(sim.astype(jnp.float32), axis=-1)
        out = jnp.einsum('bhij,bhjd->bhid', attn, v)
        adj = attn.reshape(b * HEADS, n, n)
        adj = jnp.clip(adj + jnp.eye(n, dtype=adj.dtype), 0.0, 1.0)
        deg = jnp.sum(adj, axis=-1, keepdims=True)
        feats = v.reshape(b * HEADS, n, DHEAD)
        for l in range(GNN_DEPTH):
            h = feats @ gnn_w[l] + gnn_b[l]
            h = jnp.einsum('bij,bjd->bid', adj, h) / deg
            feats = jax.nn.gelu(h + feats, approximate=False)
        gnn_out = feats @ lin_w + lin_b
        out = out + gnn_out.reshape(b, HEADS, n, DHEAD)
        out = out.transpose(0, 2, 1, 3).reshape(b, n, HEADS * DHEAD)
        return layer_norm(out @ Wo, gamma_out)

    def _L0_ffn_ref(x, W1, b1, quantum_phases, quantum_weights_real, quantum_weights_imag, W2, b2):
        import jax, jax.numpy as jnp
        import numpy as np
        B, S, D_MODEL, D_FF = (4, 256, 128, 512)

        def _quantum_transform(hidden, theta, w_real, w_imag):
            imag = w_imag * jnp.sin(theta + hidden * 0.1)
            quantum_phase = jnp.cos(theta) * w_real + jnp.sin(theta) * w_imag
            return hidden + quantum_phase * imag * 0.1
        hidden = jnp.einsum('bsd,df->bsf', x, W1) + b1
        q = _quantum_transform(hidden, quantum_phases, quantum_weights_real, quantum_weights_imag)
        act = jax.nn.relu(q)
        return jnp.einsum('bsf,fd->bsd', act, W2) + b2

    def _L1_attn_ref(x, w_qkv, w_out, b_out):
        import jax, jax.numpy as jnp
        import numpy as np
        DIM_IN, DIM_OUT, DIM_INNER = (128, 128, 64)
        scale = DIM_INNER ** (-0.5)
        qkv = jnp.einsum('bnd,ed->bne', x, w_qkv)
        q, k, v = jnp.split(qkv, 3, axis=-1)
        sim = jnp.einsum('bid,bjd->bij', q, k) * scale
        n = sim.shape[-1]
        causal = jnp.tril(jnp.ones((n, n), dtype=bool))
        sim = jnp.where(causal[None], sim, -jnp.finfo(sim.dtype).max)
        attn = jax.nn.softmax(sim, axis=-1)
        out = jnp.einsum('bij,bjd->bid', attn, v)
        return jnp.einsum('bnd,od->bno', out, w_out) + b_out

    def _L1_ffn_ref(x, Wg, bg, W1, b1, W2, b2):
        import jax, jax.numpy as jnp
        import numpy as np
        H = 128
        I = 128
        E = 8
        B, S, Hd = x.shape
        xf = x.reshape(-1, Hd)
        logits = xf @ Wg + bg
        gates = jax.nn.softmax(logits, axis=-1)
        idx = jnp.argmax(gates, axis=-1)
        h = jax.nn.gelu(jnp.einsum('th,ehi->tei', xf, W1) + b1, approximate=False)
        y = jnp.einsum('tei,eih->teh', h, W2) + b2
        out = jnp.take_along_axis(y, idx[:, None, None], axis=1)[:, 0, :]
        return out.reshape(B, S, Hd)

    def _L2_attn_ref(x, wg_w, wg_b, wq_w, wq_b, wk_w, wk_b, wv_w, wv_b, out_w, out_b):
        import jax, jax.numpy as jnp
        import numpy as np
        DIM = 128
        HEADS = 16
        HEAD_DIM = DIM // HEADS

        def feature_map(x):
            return jnp.where(x > 0, x + 1.0, jnp.exp(x))
        B, N, D = x.shape
        H, Hd = (HEADS, HEAD_DIM)
        q = (x @ wq_w + wq_b).reshape(B, N, H, Hd)
        k = (x @ wk_w + wk_b).reshape(B, N, H, Hd)
        v = (x @ wv_w + wv_b).reshape(B, N, H, Hd)
        gate = jax.nn.sigmoid(x @ wg_w + wg_b)
        q = feature_map(q)
        k = feature_map(k)
        kv = jnp.einsum('bnhd,bnhe->bhde', k, v)
        z = 1.0 / (jnp.einsum('bnhd,bhd->bnh', q, k.sum(axis=1)) + 1e-06)
        scores = jnp.einsum('bnhd,bhde,bnh->bnhe', q, kv, z)
        out = scores.reshape(B, N, D)
        return gate * out @ out_w + out_b

    def _L2_ffn_ref(x, router_w, wg, wu, wd):
        import jax, jax.numpy as jnp
        import numpy as np
        E = 8
        K = 2
        CF = 1.25
        B, L, D = x.shape
        xf = x.reshape(-1, D)
        N = xf.shape[0]
        capacity = max(1, int(CF * N / E))
        logits = xf @ router_w.T
        probs = jax.nn.softmax(logits, axis=-1)
        topw, topi = jax.lax.top_k(probs, K)
        topw = topw / (topw.sum(-1, keepdims=True) + 1e-06)
        fe = topi.reshape(-1)
        fw = topw.reshape(-1)
        ft = jnp.repeat(jnp.arange(N), K)
        order = jnp.lexsort((-fw, fe))
        se, sw, st = (fe[order], fw[order], ft[order])
        counts = jax.ops.segment_sum(jnp.ones_like(se), se, num_segments=E)
        starts = jnp.cumsum(counts) - counts
        rank = jnp.arange(N * K) - starts[se]
        keep = rank < capacity
        pos = jnp.where(keep, rank, capacity)
        disp = jnp.zeros((E, capacity + 1, D), x.dtype).at[se, pos].set(xf[st])
        disp = disp[:, :capacity]
        g = jnp.einsum('ecd,edf->ecf', disp, wg)
        u = jnp.einsum('ecd,edf->ecf', disp, wu)
        eo = jnp.einsum('ecf,efd->ecd', jax.nn.silu(g) * u, wd)
        gathered = eo[se, jnp.minimum(pos, capacity - 1)]
        contrib = gathered * (sw * keep.astype(x.dtype))[:, None]
        out = jnp.zeros_like(xf).at[st].add(contrib)
        return out.reshape(B, L, D)

    def _L3_attn_ref(x, W_in, conv_w, conv_b, W_x, W_dt, b_dt, A_log, D, W_out):
        import jax, jax.numpy as jnp
        from jax import lax
        import numpy as np
        D_MODEL = 128
        D_STATE = 16
        D_CONV = 4
        EXPAND = 2
        D_INNER = D_MODEL * EXPAND
        DT_RANK = (D_MODEL + 15) // 16
        B, T = (2, 256)

        def _silu(v):
            return v * jax.nn.sigmoid(v)
        Bb, Tt, _ = x.shape
        xz = x @ W_in
        xi, z = jnp.split(xz, 2, axis=-1)
        xi_nch = jnp.transpose(xi, (0, 2, 1))
        xc = lax.conv_general_dilated(xi_nch, conv_w[:, None, :], (1,), [(D_CONV - 1, 0)], feature_group_count=D_INNER, dimension_numbers=('NCH', 'OIH', 'NCH'))
        xc = _silu(jnp.transpose(xc, (0, 2, 1)) + conv_b)
        x_dbl = xc @ W_x
        dt, Bm, Cm = jnp.split(x_dbl, [DT_RANK, DT_RANK + D_STATE], axis=-1)
        delta = jax.nn.softplus(dt @ W_dt + b_dt)
        A = -jnp.exp(A_log)
        dA = jnp.exp(delta[..., None] * A)
        dBu = delta[..., None] * Bm[:, :, None, :] * xc[..., None]

        def step(h, inp):
            dA_t, dBu_t, C_t = inp
            h = dA_t * h + dBu_t
            y = jnp.einsum('bdn,bn->bd', h, C_t)
            return (h, y)
        h0 = jnp.zeros((Bb, D_INNER, D_STATE), x.dtype)
        _, ys = lax.scan(step, h0, (jnp.transpose(dA, (1, 0, 2, 3)), jnp.transpose(dBu, (1, 0, 2, 3)), jnp.transpose(Cm, (1, 0, 2))))
        y = jnp.transpose(ys, (1, 0, 2)) + xc * D
        return y * _silu(z) @ W_out

    def _L3_ffn_ref(x, gate_w, gate_b, expert_bias, w1, b1, w2, b2):
        import jax, jax.numpy as jnp
        import numpy as np
        D_MODEL = 128
        D_FF = 512
        NUM_EXPERTS = 8
        gate_logits = jnp.einsum('bsd,ed->bse', x, gate_w) + gate_b + expert_bias
        top_idx = jnp.argmax(gate_logits, axis=-1)
        out = jnp.zeros_like(x)
        for e in range(NUM_EXPERTS):
            mask = (top_idx == e)[..., None].astype(x.dtype)
            h = jax.nn.relu(jnp.einsum('bsd,df->bsf', x, w1[e]) + b1[e])
            y = jnp.einsum('bsf,fd->bsd', h, w2[e]) + b2[e]
            out = out + mask * y
        return out
    x = L0_attn_x
    x = x + _L0_attn_ref(_layernorm(x, axis=-1), L0_attn_gamma_in, L0_attn_Wq, L0_attn_Wk, L0_attn_Wv, L0_attn_gnn_w, L0_attn_gnn_b, L0_attn_lin_w, L0_attn_lin_b, L0_attn_Wo, L0_attn_gamma_out)
    x = x + _L0_ffn_ref(_layernorm(x, axis=-1), L0_ffn_W1, L0_ffn_b1, L0_ffn_quantum_phases, L0_ffn_quantum_weights_real, L0_ffn_quantum_weights_imag, L0_ffn_W2, L0_ffn_b2)
    x = x + _L1_attn_ref(_layernorm(x, axis=-1), L1_attn_w_qkv, L1_attn_w_out, L1_attn_b_out)
    x = x + _L1_ffn_ref(_layernorm(x, axis=-1), L1_ffn_Wg, L1_ffn_bg, L1_ffn_W1, L1_ffn_b1, L1_ffn_W2, L1_ffn_b2)
    x = x + _L2_attn_ref(_layernorm(x, axis=-1), L2_attn_wg_w, L2_attn_wg_b, L2_attn_wq_w, L2_attn_wq_b, L2_attn_wk_w, L2_attn_wk_b, L2_attn_wv_w, L2_attn_wv_b, L2_attn_out_w, L2_attn_out_b)
    x = x + _L2_ffn_ref(_layernorm(x, axis=-1), L2_ffn_router_w, L2_ffn_wg, L2_ffn_wu, L2_ffn_wd)
    x = x + _L3_attn_ref(_layernorm(x, axis=-1), L3_attn_W_in, L3_attn_conv_w, L3_attn_conv_b, L3_attn_W_x, L3_attn_W_dt, L3_attn_b_dt, L3_attn_A_log, L3_attn_D, L3_attn_W_out)
    x = x + _L3_ffn_ref(_layernorm(x, axis=-1), L3_ffn_gate_w, L3_ffn_gate_b, L3_ffn_expert_bias, L3_ffn_w1, L3_ffn_b1, L3_ffn_w2, L3_ffn_b2)
    return x

_drawn_inputs = setup_inputs


def setup_inputs(seed=0):
    import zlib

    import numpy as np

    out = dict(_drawn_inputs(seed))
    spreads = {'L0_attn_gamma_in': (1.0, 0.2),
     'L0_attn_gnn_b': (0.0, 0.1),
     'L0_attn_lin_b': (0.0, 0.1),
     'L0_attn_gamma_out': (1.0, 0.2),
     'L0_ffn_b1': (0.0, 0.1),
     'L0_ffn_b2': (0.0, 0.1),
     'L1_ffn_bg': (0.0, 0.1),
     'L1_ffn_b1': (0.0, 0.325),
     'L1_ffn_b2': (0.0, 0.1),
     'L2_attn_wg_b': (0.0, 0.342),
     'L2_attn_wq_b': (0.0, 2.0),
     'L2_attn_wk_b': (0.0, 2.0),
     'L2_attn_wv_b': (0.0, 0.1),
     'L2_attn_out_b': (0.0, 0.1),
     'L3_attn_conv_b': (0.0, 0.269),
     'L3_attn_b_dt': (-4.600166320800781, 0.6),
     'L3_attn_D': (1.0, 0.2),
     'L3_ffn_expert_bias': (0.0, 0.1)}
    factors = {'L0_ffn_quantum_phases': 8.0,
     'L0_ffn_quantum_weights_real': 8.0,
     'L0_ffn_quantum_weights_imag': 8.0,
     'L2_attn_wq_w': 4.638,
     'L2_attn_wk_w': 3.311,
     'L3_attn_W_dt': 5.858,
     'L3_attn_A_log': 2.74,
     'L3_ffn_b1': 4.779,
     'L3_ffn_b2': 3.894}
    for name, (base, spread) in spreads.items():
        noise = np.random.default_rng([zlib.crc32(name.encode()), seed]).standard_normal(out[name].shape)
        drawn = base * np.exp(spread * noise) if base else spread * noise
        out[name] = jnp.asarray(drawn.astype(out[name].dtype))
    for name, factor in factors.items():
        out[name] = (out[name] * factor).astype(out[name].dtype)
    return out
```

```python
from contextlib import ExitStack

import concourse.bass as bass
from concourse import mybir

ALU = mybir.AluOpType
ACT = mybir.ActivationFunctionType
F32 = mybir.dt.float32
F32R = mybir.dt.float32r
BF16 = mybir.dt.bfloat16
I32 = mybir.dt.int32
AX_X = mybir.AxisListType.X

P = 128
NB = 2
SEQ = 1024
TOK = NB * SEQ
TT = TOK // P
ST = SEQ // P
EPS = 1e-5


class Count:

    def __init__(self, sem, start=0):
        self.sem = sem
        self.n = start

    def mark(self, ins, by=1):
        ins.then_inc(self.sem, by)
        self.n = self.n + by

    def then_wait(self, eng, ins):
        self.mark(ins)
        eng.wait_ge(self.sem, self.n)


def wait(eng, sem, value):
    if not (isinstance(value, int) and value <= 0):
        eng.wait_ge(sem, value)


def spread(ap, shape):
    return ap.unsqueeze(len(ap.shape)).broadcast_to(shape)


def ln_stats(dve, step, work, src, tiles, waits=None):
    st, mv, ve = work["stats"], work["mv"], work["ve"]
    for t in range(tiles):
        if waits:
            waits(t)
        step.mark(dve.bn_stats(st[:, t, :], src[:, t, :]))
    dve.wait_ge(step.sem, step.n)
    for t in range(tiles):
        step.mark(dve.bn_aggr(mv[:, t, :], st[:, t, :]))
    dve.wait_ge(step.sem, step.n)
    return dve.tensor_scalar(ve[:, 0:tiles], mv[:, 0:tiles, 1], EPS, None, ALU.add)


def ln_rstd(dve, step, work, tiles):
    ve, sd, y, z = work["ve"], work["sd"], work["rstd"], work["newton"]
    step.then_wait(dve, dve.reciprocal(y[:, 0:tiles], sd[:, 0:tiles]))
    step.then_wait(dve, dve.tensor_tensor(z[:, 0:tiles], y[:, 0:tiles], y[:, 0:tiles], ALU.mult))
    step.then_wait(dve, dve.tensor_tensor(z[:, 0:tiles], z[:, 0:tiles], ve[:, 0:tiles], ALU.mult))
    step.then_wait(dve, dve.tensor_scalar(z[:, 0:tiles], z[:, 0:tiles], -0.5, 1.5, ALU.mult, ALU.add))
    step.then_wait(dve, dve.tensor_tensor(y[:, 0:tiles], y[:, 0:tiles], z[:, 0:tiles], ALU.mult))


def ln_work(sb, name, tiles):
    return {
        "stats": sb(name + "_stats", [P, tiles, 6], F32), "mv": sb(name + "_mv", [P, tiles, 2], F32),
        "ve": sb(name + "_ve", [P, tiles], F32), "sd": sb(name + "_sd", [P, tiles], F32),
        "rstd": sb(name + "_rstd", [P, tiles], F32), "newton": sb(name + "_newton", [P, tiles], F32),
    }


def scope(nc, ctx, name):
    used = []

    def clear():
        nc.clear_and_free_semaphores(used)
        nc.all_engine_barrier()

    ctx.callback(clear)

    def sb(n, shape, dt=F32):
        return ctx.enter_context(nc.sbuf_tensor(f"{name}_{n}", shape, dt))

    def pb(n, shape, dt=F32):
        return ctx.enter_context(nc.psum_tensor(f"{name}_{n}", shape, dt))

    def sem(n):
        used.append(nc.alloc_semaphore(f"{name}_{n}"))
        return used[-1]

    return sb, pb, sem


def prenorm(nc, name, x, xnT, ident, rounds=1, gamma=None, xn_keep=None):
    with ExitStack() as ctx:
        sb, pb, sem = scope(nc, ctx, name)
        xn = xn_keep if xn_keep is not None else sb("xn", [P, TT, P])
        work = ln_work(sb, name, TT)
        bank = [pb(f"turned{n}", [P, 4, P]) for n in range(4)]
        step_done, ve_ready, root_ready = sem("step"), sem("ve_ready"), sem("root_ready")
        xn_ready, turned_ready, kept = sem("xn_ready"), sem("turned_ready"), sem("kept")
        block = ctx.enter_context(nc.Block(no_gpsimd_drain=True))

        @block.vector
        def _(dve):
            step = Count(step_done)
            src = x
            for r in range(rounds):
                ln_stats(dve, step, work, src, TT).then_inc(ve_ready, 1)
                dve.wait_ge(root_ready, r + 1)
                ln_rstd(dve, step, work, TT)
                for t in range(TT):
                    ins = dve.tensor_scalar(xn[:, t, :], src[:, t, :], work["mv"][:, t, 0:1],
                                            work["rstd"][:, t:t + 1], ALU.subtract, ALU.mult)
                    if r == rounds - 1:
                        ins.then_inc(xn_ready, 1)
                    else:
                        step.mark(ins)
                src = xn
                dve.wait_ge(step.sem, step.n)

        @block.scalar
        def _(act):
            for r in range(rounds):
                act.wait_ge(ve_ready, r + 1)
                act.activation(work["sd"][:, :], work["ve"][:, :], ACT.Sqrt).then_inc(root_ready, 1)
            for g in range(4):
                act.wait_ge(turned_ready, g + 1)
                act.activation(xnT[:, g * 512:(g + 1) * 512], bank[g][:, :, :].rearrange("p a b -> p (a b)"),
                               ACT.Copy, scale=1.0 if gamma is None else gamma).then_inc(kept, 1)

        @block.tensor
        def _(pe):
            for g in range(4):
                for j in range(4):
                    pe.wait_ge(xn_ready, 4 * g + j + 1)
                    mm = pe.transpose(bank[g][:, j, :], xn[:, 4 * g + j, :], ident[:, :])
                mm.then_inc(turned_ready, 1)
HEADS, DH = 16, 64
PAIRS = HEADS // 2
SCALE0 = DH ** -0.5


def l0_attention(nc, d, x, xnT, ident, const):
    with ExitStack() as ctx:
        sb, pb, sem = scope(nc, ctx, "l0a")
        wp = sb("wp", [P, 4 * P])
        wv2 = sb("wv2", [P, 2, 2, DH])
        gnn0 = sb("gnn0", [P, P])
        gnn1 = sb("gnn1", [P, P])
        lin = sb("lin", [P, P])
        linb = sb("linb", [P, 1])
        vbias = sb("vbias", [P, 2, 2, DH])
        h1bias = sb("h1bias", [P, 2, DH])
        mask = sb("mask", [P, P], BF16)
        identb = sb("identb", [P, P], BF16)
        maskf = sb("maskf", [P, P])
        caps = sb("caps", [P, P])
        qa = sb("qa", [DH + 1, 2, SEQ])
        ka = sb("ka", [DH + 1, 2, SEQ])
        qr = sb("qr", [DH, 2, SEQ], F32R)
        kr = sb("kr", [DH, 2, SEQ], F32R)
        E = sb("E", [P, 2, 36 * P])
        VH = sb("VH", [P, ST, 2, 2 * DH + 1])
        F1 = sb("F1", [P, ST, 2, DH])
        F2 = sb("F2", [P, ST, 2, DH])
        H1 = sb("H1", [P, ST, 2, DH])
        U1 = sb("U1", [P, ST, 2, DH])
        AO = sb("AO", [P, ST, 2, DH])
        FT = sb("FT", [P, 4 * P])
        OT = sb("OT", [P, PAIRS, SEQ])
        wo = sb("wo", [P, PAIRS, P])
        go = sb("go", [P, P])
        eii = sb("eii", [P, 2, ST])
        mx = sb("mx", [P, 2, ST])
        mh = sb("mh", [P, 2, ST], BF16)
        ml = sb("ml", [P, 2, ST], BF16)
        small = sb("small", [P, ST, 10])
        scrap = sb("scrap", [P, P])
        tmp = sb("tmp", [P, 2, DH])
        Y = sb("Y", [P, ST, P])
        work = ln_work(sb, "l0o", ST)
        ring = [pb(f"ring{n}", [P, SEQ]) for n in range(2)]
        agg = [pb(f"agg{n}", [P, 512]) for n in range(2)]
        turn = pb("turn", [P, 4 * P])
        prod = pb("prod", [P, 4 * P])

        const_in, w_in = sem("const_in"), sem("w_in")
        wv0_ready, wv_ready = sem("wv0_ready"), sem("wv_ready")
        q_ready, k_ready, v_ready = sem("q_ready"), sem("k_ready"), sem("v_ready")
        q_kept, k_kept, v_kept, rounded = sem("q_kept"), sem("k_kept"), sem("v_kept"), sem("rounded")
        rowmax_ready, max_done, mparts = sem("rowmax_ready"), sem("max_done"), sem("mparts")
        mrow_ready, mrow_kept = sem("mrow_ready"), sem("mrow_kept")
        score_ready, exp_done, masked = sem("score_ready"), sem("exp_done"), sem("masked")
        agg1_ready, post1_done, gelu1_done = sem("agg1_ready"), sem("post1_done"), sem("gelu1_done")
        t1_ready, t1_kept, h1_ready, h1_kept = sem("t1_ready"), sem("t1_kept"), sem("h1_ready"), sem("h1_kept")
        u1_ready = sem("u1_ready")
        agg2_ready, post2_done, gelu2_done = sem("agg2_ready"), sem("post2_done"), sem("gelu2_done")
        t2_ready, t2_kept, ot_ready, ot_kept = sem("t2_ready"), sem("t2_kept"), sem("ot_ready"), sem("ot_kept")
        dve_step, dve_out, y_ready, y_kept = sem("dve_step"), sem("dve_out"), sem("y_ready"), sem("y_kept")
        ve_ready, root_ready, pool_step = sem("ve_ready"), sem("root_ready"), sem("pool_step")

        ecol = [sum(SEQ - P * k for k in range(jt)) for jt in range(ST)]

        def e_tile(h, jt, it):
            at = ecol[jt] + (it - jt) * P
            return E[:, h, at:at + P]

        block = ctx.enter_context(nc.Block(no_gpsimd_drain=True))

        def for_units(eng, first, body, last):
            first()
            for b in range(NB):
                with eng.Fori(0, PAIRS - 1) as i:
                    body(i + b * PAIRS if b else i, b, i, b)
                if b < NB - 1:
                    body(PAIRS * (b + 1) - 1, b, PAIRS - 1, b + 1)
                else:
                    body(PAIRS * (b + 1) - 1, b, PAIRS - 1, None)
                last(b)

        @block.sync
        def _(sp):
            for dst, src in ((maskf, d["cmask"]), (caps, d["caps"]), (wo, d["wo"]), (go, d["gout"].partition_broadcast(P))):
                sp.dma_start(dst[:], src).then_inc(const_in, 16)
            sp.wait_ge(pool_step, 6)
            for h in range(2):
                r = slice(h * DH, (h + 1) * DH)
                sp.dma_start(gnn0[r, r], d["gnn_w"][0]).then_inc(const_in, 16)
                sp.dma_start(gnn1[r, r], d["gnn_w"][1]).then_inc(const_in, 16)
                sp.dma_start(lin[r, r], d["lin_w"]).then_inc(const_in, 16)
                sp.dma_start(linb[r, :], d["lin_b"]).then_inc(const_in, 16)
                sp.dma_start(vbias[:, h, 1, :], d["gnn_b"][0:1, :].partition_broadcast(P)).then_inc(const_in, 16)
                sp.dma_start(h1bias[:, h, :], d["gnn_b"][1:2, :].partition_broadcast(P)).then_inc(const_in, 16)
            sp.dma_start(wp[:, :], d["wqkv"][0:P, :]).then_inc(w_in, 16)
            for b in range(NB):
                with sp.Fori(0, PAIRS - 1) as i:
                    g = i + b * PAIRS
                    sp.wait_ge(k_ready, g + 1)
                    sp.dma_start(wp[:, :], d["wqkv"][bass.ds((i + 1) * P, P), :]).then_inc(w_in, 16)
                if b < NB - 1:
                    sp.wait_ge(k_ready, PAIRS * (b + 1))
                    sp.dma_start(wp[:, :], d["wqkv"][0:P, :]).then_inc(w_in, 16)

        NCONST = 16 * (4 + 12)

        @block.gpsimd
        def _(pool):
            for n, t in enumerate((gnn0, gnn1, lin)):
                pool.memset(t[:, :], 0.0).then_inc(pool_step, 1)
            pool.memset(vbias[:, :, :, :], 0.0).then_inc(pool_step, 1)
            pool.memset(VH[:, :, :, 2 * DH:2 * DH + 1], 1.0).then_inc(pool_step, 1)
            pool.wait_ge(pool_step, 5)
            pool.memset(ka[DH:DH + 1, :, :], 1.0).then_inc(pool_step, 1)
            pool.wait_ge(pool_step, 6)

            pool.wait_ge(const_in, NCONST)

            def body(g, b, pair, nb):
                for c in range(2):
                    g4 = slice(4 * c, 4 * c + 4)
                    pool.wait_ge(h1_kept, g * 2 + (c + 1))
                    pool.wait_ge(gelu1_done, g * 8 + (4 * c + 4))
                    for t in range(4 * c, 4 * c + 4):
                        pool.tensor_tensor(U1[:, t, :, :], H1[:, t, :, :],
                                           spread(small[:, t, 6:8], [P, 2, DH]), ALU.mult).then_inc(pool_step, 1)
                    pool.wait_ge(pool_step, g * 8 + (6 + 4 * (c + 1)))
                    pool.tensor_tensor(U1[:, g4, :, :], U1[:, g4, :, :], F1[:, g4, :, :], ALU.add).then_inc(u1_ready, 1)

            for_units(pool, lambda: None, body, lambda b: None)

        @block.scalar
        def _(act):
            def keep_q(u):
                act.wait_ge(q_ready, u + 1)
                for h in range(2):
                    act.activation(qa[0:DH, h, :], ring[0][h * DH:(h + 1) * DH, :], ACT.Copy, scale=SCALE0)
                    ins = act.activation(qr[:, h, :], ring[0][h * DH:(h + 1) * DH, :], ACT.Copy, scale=SCALE0)
                ins.then_inc(q_kept, 1)

            def keep_mrows(u):
                for h in range(2):
                    act.wait_ge(mrow_ready, u * 2 + (h + 1))
                    act.activation(qa[DH:DH + 1, h, :], ring[h][0:1, :], ACT.Copy, scale=-1.0).then_inc(mrow_kept, 1)

            def first():
                keep_q(0)
                keep_mrows(0)

            def body(g, b, pair, nb):
                for h in range(2):
                    for jt in range(ST):
                        n = ST * h + jt
                        act.wait_ge(score_ready, g * 16 + (n + 1))
                        w = SEQ - P * jt
                        act.activation(E[:, h, ecol[jt]:ecol[jt] + w], ring[n % 2][:, 0:w], ACT.Exp).then_inc(exp_done, 1)
                for it in range(ST):
                    act.wait_ge(post1_done, g * 8 + (it + 1))
                    act.activation(F1[:, it, :, :], F1[:, it, :, :], ACT.Gelu).then_inc(gelu1_done, 1)
                    if it == 3:
                        act.wait_ge(t1_ready, g * 2 + 1)
                        act.activation(FT[:, :], turn[:, :], ACT.Copy).then_inc(t1_kept, 1)
                if nb is not None:
                    keep_q(g + 1)
                act.wait_ge(t1_ready, g * 2 + 2)
                act.activation(FT[:, :], turn[:, :], ACT.Copy).then_inc(t1_kept, 1)
                for it in range(ST):
                    act.wait_ge(post2_done, g * 8 + (it + 1))
                    act.activation(F2[:, it, :, :], F2[:, it, :, :], ACT.Gelu).then_inc(gelu2_done, 1)
                for c in range(2):
                    act.wait_ge(t2_ready, g * 2 + (c + 1))
                    act.activation(FT[:, :], turn[:, :], ACT.Copy).then_inc(t2_kept, 1)
                    if c == 0 and nb is not None:
                        keep_mrows(g + 1)

            def last(b):
                act.wait_ge(ve_ready, b + 1)
                act.activation(work["sd"][:, :], work["ve"][:, :], ACT.Sqrt).then_inc(root_ready, 1)

            for_units(act, first, body, last)

        @block.tensor
        def _(pe):
            pe.wait_ge(const_in, NCONST)
            pe.wait_ge(wv_ready, 1)

            def project(u, b):
                cols = b * SEQ
                pe.wait_ge(wv_ready, u * 1 + 2)
                for c in range(2):
                    mm = pe.matmul(ring[0][:, c * 512:(c + 1) * 512], wp[:, 0:P],
                                   xnT[:, cols + c * 512:cols + (c + 1) * 512], start=True, stop=True)
                mm.then_inc(q_ready, 1)
                for c in range(2):
                    mm = pe.matmul(ring[1][:, c * 512:(c + 1) * 512], wp[:, P:2 * P],
                                   xnT[:, cols + c * 512:cols + (c + 1) * 512], start=True, stop=True)
                mm.then_inc(k_ready, 1)

            def values(u, b, half):
                if half == 0:
                    pe.wait_ge(q_kept, u + 1)
                else:
                    pe.wait_ge(k_kept, u + 1)
                for t in range(4):
                    tok = b * SEQ + (4 * half + t) * P
                    mm = pe.matmul(ring[half][:, t * 256:(t + 1) * 256], xnT[:, tok:tok + P],
                                   wv2[:, :, :, :].rearrange("p a b c -> p (a b c)"), start=True, stop=True)
                mm.then_inc(v_ready, 1)

            def row_scores(u, n):
                it, h = n // 2, n % 2
                if n < 2:
                    pe.wait_ge(v_kept, u * 2 + (n + 1))
                else:
                    pe.wait_ge(max_done, u * 16 + (n - 1))
                if n == 0:
                    pe.wait_ge(rounded, u + 1)
                w = (it + 1) * P
                for c0 in range(0, w, 512):
                    c1 = min(w, c0 + 512)
                    mm = pe.matmul(ring[n % 2][:, c0:c1], qr[:, h, it * P:(it + 1) * P], kr[:, h, c0:c1],
                                   start=True, stop=c1 < w)
                mm = pe.matmul(ring[n % 2][:, it * P:w], identb[:, :], mask[:, :], start=False, stop=True)
                mm.then_inc(rowmax_ready, 1)

            def max_rows(u, h):
                pe.wait_ge(mparts, u * 2 + (h + 1))
                for it in range(ST):
                    pe.matmul(ring[h][0:1, it * P:(it + 1) * P], mh[:, h, it:it + 1], identb[:, :],
                              start=True, stop=False)
                    mm = pe.matmul(ring[h][0:1, it * P:(it + 1) * P], ml[:, h, it:it + 1], identb[:, :],
                                   start=False, stop=True)
                mm.then_inc(mrow_ready, 1)

            def fuse_wv(u):
                pe.wait_ge(w_in, (u + 1) * 16)
                pe.matmul(prod[:, 0:P], wp[:, 3 * P:4 * P], gnn0[:, :], start=True, stop=True).then_inc(wv0_ready, 1)

            def first():
                fuse_wv(0)
                project(0, 0)
                values(0, 0, 0)
                values(0, 0, 1)
                for n in range(2 * ST):
                    row_scores(0, n)
                max_rows(0, 0)
                max_rows(0, 1)

            def body(g, b, pair, nb):
                for h in range(2):
                    for jt in range(ST):
                        n = ST * h + jt
                        if n < 2:
                            pe.wait_ge(mrow_kept, g * 2 + (n + 1))
                        else:
                            pe.wait_ge(exp_done, g * 16 + (n - 1))
                        w = SEQ - P * jt
                        for c0 in range(0, w, 512):
                            c1 = min(w, c0 + 512)
                            mm = pe.matmul(ring[n % 2][:, c0:c1], ka[:, h, jt * P:(jt + 1) * P],
                                           qa[:, h, P * jt + c0:P * jt + c1], start=True, stop=True)
                        mm.then_inc(score_ready, 1)
                if nb is not None:
                    pe.wait_ge(masked, g * 16 + 1)
                    fuse_wv(g + 1)
                for it in range(ST):
                    if it == 0 and b:
                        pe.wait_ge(y_kept, ST * b)
                    if it >= 2:
                        pe.wait_ge(post1_done, g * 8 + (it - 1))
                    pe.wait_ge(masked, g * 16 + (ST + it + 1))
                    for h in range(2):
                        for jt in range(it + 1):
                            mm = pe.matmul(agg[it % 2][:, h * 129:(h + 1) * 129], e_tile(h, jt, it),
                                           VH[:, jt, h, :], start=(jt == 0), stop=(jt == it))
                    mm.then_inc(agg1_ready, 1)
                    if it == 5:
                        turn_f(g, 0, F1, gelu1_done, t1_ready)
                pe.wait_ge(t1_kept, g * 2 + 1)
                if nb is not None:
                    pe.wait_ge(wv_ready, g + 3)
                graph_linear(g, 0)
                if nb is not None:
                    project(g + 1, nb)
                turn_f(g, 1, F1, gelu1_done, t1_ready)
                if nb is not None:
                    values(g + 1, nb, 0)
                pe.wait_ge(t1_kept, g * 2 + 2)
                pe.wait_ge(h1_kept, g * 2 + 1)
                graph_linear(g, 1)
                if nb is not None:
                    values(g + 1, nb, 1)
                for it in range(ST):
                    if it < 2:
                        pe.wait_ge(post1_done, g * 8 + (it + 7))
                    else:
                        pe.wait_ge(post2_done, g * 8 + (it - 1))
                    if it in (0, 4):
                        pe.wait_ge(h1_kept, g * 2 + (it // 4 + 1))
                    for h in range(2):
                        for jt in range(it + 1):
                            mm = pe.matmul(agg[it % 2][:, h * DH:(h + 1) * DH], e_tile(h, jt, it),
                                           H1[:, jt, h, :], start=(jt == 0), stop=(jt == it))
                    mm.then_inc(agg2_ready, 1)
                    if nb is not None:
                        row_scores(g + 1, 2 * it)
                        row_scores(g + 1, 2 * it + 1)
                turn_f(g, 0, F2, gelu2_done, t2_ready)
                if nb is not None:
                    max_rows(g + 1, 0)
                    max_rows(g + 1, 1)
                mix(g, 0)
                turn_f(g, 1, F2, gelu2_done, t2_ready)
                mix(g, 1)

            def turn_f(g, c, src, done, ready):
                pe.wait_ge(done, g * 8 + (4 * c + 4))
                for t in range(4):
                    mm = pe.transpose(turn[:, t * P:(t + 1) * P],
                                      src[:, 4 * c + t, :, :].rearrange("p a b -> p (a b)"), ident[:, :])
                mm.then_inc(ready, 1)

            def graph_linear(g, c):
                for t in range(4):
                    mm = pe.matmul(prod[:, t * P:(t + 1) * P], FT[:, t * P:(t + 1) * P], gnn1[:, :],
                                   start=True, stop=True)
                mm.then_inc(h1_ready, 1)

            def mix(g, c):
                pe.wait_ge(t2_kept, g * 2 + (c + 1))
                if c == 1:
                    pe.wait_ge(ot_kept, g * 2 + 1)
                for t in range(4):
                    pe.matmul(prod[:, t * P:(t + 1) * P],
                              AO[:, 4 * c + t, :, :].rearrange("p a b -> p (a b)"), ident[:, :],
                              start=(t == 0), stop=False, skip_group_check=True)
                mm = pe.matmul(prod[:, :], lin[:, :], FT[:, :], start=False, stop=True, skip_group_check=True)
                mm.then_inc(ot_ready, 1)

            def last(b):
                pe.wait_ge(ot_kept, 2 * PAIRS * (b + 1))
                for it in range(ST):
                    if it >= 2:
                        pe.wait_ge(y_kept, ST * b + it - 1)
                    for q in range(PAIRS):
                        mm = pe.matmul(agg[it % 2][:, 0:P], OT[:, q, it * P:(it + 1) * P], wo[:, q, :],
                                       start=(q == 0), stop=(q == PAIRS - 1))
                    mm.then_inc(y_ready, 1)

            for_units(pe, first, body, last)

        LAST = 2 * ST + 5 + ST + 2

        @block.vector
        def _(dve):
            step = Count(dve_step)
            dve.wait_ge(const_in, NCONST)
            step.then_wait(dve, dve.tensor_copy(mask[:, :], maskf[:, :]))
            dve.tensor_copy(identb[:, :], ident[:, :]).then_inc(wv_ready, 1)

            def keep_wv(u):
                dve.wait_ge(wv0_ready, u + 1)
                for h in range(2):
                    dve.tensor_copy(wv2[:, h, 0, :], wp[:, 2 * P + h * DH:2 * P + (h + 1) * DH])
                    ins = dve.tensor_copy(wv2[:, h, 1, :], prod[:, h * DH:(h + 1) * DH])
                ins.then_inc(wv_ready, 1)

            def keep_k(u):
                dve.wait_ge(k_ready, u + 1)
                for h in range(2):
                    ins = dve.tensor_copy(ka[0:DH, h, :], ring[1][h * DH:(h + 1) * DH, :])
                ins.then_inc(k_kept, 1)
                dve.wait_ge(k_kept, u + 1)
                dve.tensor_copy(kr[:, :, :], ka[0:DH, :, :]).then_inc(rounded, 1)

            def keep_v(u, half):
                dve.wait_ge(v_ready, u * 2 + (half + 1))
                for h in range(2):
                    src = ring[half][:, :].rearrange("p (t h w) -> p t h w", t=4, h=2)[:, :, h, :]
                    bias = vbias[:, h, :, :].rearrange("p a b -> p (a b)").unsqueeze(1).broadcast_to([P, 4, P])
                    ins = dve.tensor_tensor(VH[:, 4 * half:4 * half + 4, h, 0:2 * DH], src, bias, ALU.add)
                ins.then_inc(v_kept, 1)

            def row_max(u, n):
                it, h = n // 2, n % 2
                dve.wait_ge(rowmax_ready, u * 16 + (n + 1))
                dve.tensor_reduce(mx[:, h, it:it + 1], ring[n % 2][:, 0:(it + 1) * P], AX_X, ALU.max).then_inc(max_done, 1)

            def max_parts(u, step):
                dve.wait_ge(max_done, u * 16 + 16)
                for h in range(2):
                    step.then_wait(dve, dve.tensor_copy(mh[:, h, :], mx[:, h, :]))
                    dve.tensor_tensor(ml[:, h, :], mx[:, h, :], mh[:, h, :], ALU.subtract).then_inc(mparts, 1)

            def first():
                keep_wv(0)
                keep_k(0)
                keep_v(0, 0)
                keep_v(0, 1)
                for n in range(2 * ST):
                    row_max(0, n)
                max_parts(0, step)

            done = {}

            def body(g, b, pair, nb):
                full = done.get("per_unit", 0)
                step = Count(dve_step, done["start"] + g * full)
                at0 = 0
                n0 = 0
                for h in range(2):
                    for jt in range(ST):
                        dve.wait_ge(exp_done, g * 16 + (ST * h + jt + 1))
                        dve.tensor_tensor(e_tile(h, jt, jt), e_tile(h, jt, jt), caps[:, :], ALU.min).then_inc(masked, 1)
                        dve.wait_ge(masked, g * 16 + (ST * h + jt + 1))
                        step.then_wait(dve, dve.scalar_tensor_tensor(
                            scrap[:, :], e_tile(h, jt, jt), 1.0, ident[:, :], ALU.mult, ALU.mult,
                            accum_out=eii[:, h, jt:jt + 1]))
                        n0 += 1
                    if h == 1 and nb is not None:
                        keep_wv(g + 1)
                for it in range(ST):
                    dve.wait_ge(agg1_ready, g * 8 + (it + 1))
                    a = agg[it % 2][:, 0:258].rearrange("p (h w) -> p h w", h=2)
                    s, row = a[:, :, 128], small[:, it, :]
                    step.then_wait(dve, dve.tensor_tensor(row[:, 4:6], s, eii[:, :, it], ALU.subtract))
                    step.mark(dve.tensor_tensor(row[:, 0:2], s, row[:, 4:6], ALU.add))
                    step.then_wait(dve, dve.tensor_copy(row[:, 2:4], s))
                    step.then_wait(dve, dve.reciprocal(row[:, 0:4], row[:, 0:4]))
                    step.mark(dve.tensor_tensor(row[:, 6:8], row[:, 4:6], row[:, 0:2], ALU.mult))
                    step.mark(dve.tensor_tensor(AO[:, it, :, :], a[:, :, 0:DH], spread(row[:, 2:4], [P, 2, DH]), ALU.mult))
                    step.then_wait(dve, dve.tensor_tensor(F1[:, it, :, :], a[:, :, DH:2 * DH],
                                                          spread(row[:, 0:2], [P, 2, DH]), ALU.mult))
                    step.then_wait(dve, dve.tensor_tensor(tmp[:, :, :], VH[:, it, :, DH:2 * DH],
                                                          spread(row[:, 6:8], [P, 2, DH]), ALU.mult))
                    step.then_wait(dve, dve.tensor_tensor(F1[:, it, :, :], F1[:, it, :, :], tmp[:, :, :], ALU.add))
                    dve.tensor_tensor(F1[:, it, :, :], F1[:, it, :, :], VH[:, it, :, 0:DH], ALU.add).then_inc(post1_done, 1)
                    n0 += 9
                def keep_h1(c):
                    dve.wait_ge(h1_ready, g * 2 + (c + 1))
                    bias = h1bias[:, :, :].rearrange("p a b -> p (a b)").unsqueeze(1).broadcast_to([P, 4, P])
                    dve.tensor_tensor(H1[:, 4 * c:4 * c + 4, :, :].rearrange("p t a b -> p t (a b)"),
                                      prod[:, :].rearrange("p (t w) -> p t w", t=4), bias, ALU.add).then_inc(h1_kept, 1)
                keep_h1(0)
                if nb is not None:
                    keep_k(g + 1)
                    keep_v(g + 1, 0)
                keep_h1(1)
                if nb is not None:
                    keep_v(g + 1, 1)
                for it in range(ST):
                    dve.wait_ge(agg2_ready, g * 8 + (it + 1))
                    if it in (0, 4):
                        dve.wait_ge(u1_ready, g * 2 + (it // 4 + 1))
                    a = agg[it % 2][:, 0:P].rearrange("p (h w) -> p h w", h=2)
                    step.then_wait(dve, dve.tensor_tensor(F2[:, it, :, :], a, spread(small[:, it, 0:2], [P, 2, DH]), ALU.mult))
                    dve.tensor_tensor(F2[:, it, :, :], F2[:, it, :, :], U1[:, it, :, :], ALU.add).then_inc(post2_done, 1)
                    n0 += 1
                    if nb is not None:
                        row_max(g + 1, 2 * it)
                        row_max(g + 1, 2 * it + 1)
                if nb is not None:
                    max_parts(g + 1, step)
                    n0 += 2
                for c in range(2):
                    dve.wait_ge(ot_ready, g * 2 + (c + 1))
                    at = pair * SEQ + c * 512
                    flat = OT[:, :, :].rearrange("p a b -> p (a b)")
                    dst = flat[:, bass.ds(at, 512)]
                    dve.tensor_scalar(dst, prod[:, :], linb[:, :], None, ALU.add).then_inc(ot_kept, 1)
                done["n"] = n0

            def last(b):
                step = Count(dve_out)
                step.n = b * LAST
                start = step.n
                for it in range(ST):
                    dve.wait_ge(y_ready, ST * b + it + 1)
                    dve.tensor_copy(Y[:, it, :], agg[it % 2][:, 0:P]).then_inc(y_kept, 1)
                dve.wait_ge(y_kept, ST * (b + 1))
                ln_stats(dve, step, work, Y, ST).then_inc(ve_ready, 1)
                dve.wait_ge(root_ready, b + 1)
                ln_rstd(dve, step, work, ST)
                for it in range(ST):
                    step.mark(dve.tensor_scalar(Y[:, it, :], Y[:, it, :], work["mv"][:, it, 0:1],
                                                  work["rstd"][:, it:it + 1], ALU.subtract, ALU.mult))
                dve.wait_ge(step.sem, step.n)
                gam = go[:, :].unsqueeze(1).broadcast_to([P, ST, P])
                step.then_wait(dve, dve.tensor_tensor(Y[:, :, :], Y[:, :, :], gam, ALU.mult))
                xb = x[:, b * ST:(b + 1) * ST, :]
                step.then_wait(dve, dve.tensor_tensor(xb, xb, Y[:, :, :], ALU.add))
                assert step.n - start == LAST

            done["per_unit"] = 16 + 9 * ST + ST + 2
            first()
            done["start"] = step.n
            for b in range(NB):
                with dve.Fori(0, PAIRS - 1) as i:
                    body(i + b * PAIRS if b else i, b, i, b)
                    assert done["n"] == done["per_unit"]
                body(PAIRS * (b + 1) - 1, b, PAIRS - 1, b + 1 if b < NB - 1 else None)
                last(b)
TWO_PI_PARTS = (6.28125, 0.0019350051879882812, 3.0199159819e-07)
ROUND = 1.5 * 2.0 ** 23
PI_IN = 3.1415925


def turns_removed(dve, step, y, m):
    step.then_wait(dve, dve.tensor_scalar(m, y, 0.15915494309189535, ROUND, ALU.mult, ALU.add))
    step.then_wait(dve, dve.tensor_scalar(m, m, ROUND, None, ALU.subtract))
    for part in TWO_PI_PARTS:
        step.then_wait(dve, dve.scalar_tensor_tensor(y, m, -part, y, ALU.mult, ALU.add))
    return dve.tensor_scalar(y, y, PI_IN, -PI_IN, ALU.min, ALU.max)


def l0_ffn(nc, d, x, xnT):
    F = d["f0_w1"].shape[1]
    FC = F // P
    with ExitStack() as ctx:
        sb, pb, sem = scope(nc, ctx, "l0f")
        w1, w2 = sb("w1", [P, F]), sb("w2", [P, FC, P])
        vec = sb("vec", [P, 4, FC])
        b2 = sb("b2", [P, P])
        coef, cosr, sinr, room = (sb(n, [P, FC]) for n in ("coef", "cosr", "sinr", "room"))
        h, y, m = sb("h", [P, 3, 512]), sb("y", [P, 3, 512]), sb("m", [P, 512])
        a = sb("a", [P, 2, FC, 512])
        hid = [pb(f"hid{n}", [P, 512]) for n in range(2)]
        outp = [pb(f"outp{n}", [P, 4, P]) for n in range(2)]
        w_in, bias_added = sem("w_in"), sem("bias_added")
        hid_ready, hid_kept, y_ready, sine_done = sem("hid_ready"), sem("hid_kept"), sem("y_ready"), sem("sine_done")
        q_ready, act_ready, out_ready, out_kept = sem("q_ready"), sem("act_ready"), sem("out_ready"), sem("out_kept")
        dve_step, angle_ready, trig_ready = sem("dve_step"), sem("angle_ready"), sem("trig_ready")
        items = [(g, c) for g in range(4) for c in range(FC)]
        block = ctx.enter_context(nc.Block(no_gpsimd_drain=True))

        @block.sync
        def _(sp):
            for dst, src in ((w1, d["f0_w1"]), (vec, d["f0_vec"]), (w2, d["f0_w2"]), (b2, d["f0_b2"].partition_broadcast(P))):
                sp.dma_start(dst[:], src).then_inc(w_in, 16)

        @block.gpsimd
        def _(pool):
            pool.wait_ge(w_in, 64)
            pool.tensor_tensor(x[:, :, :], x[:, :, :], b2[:, :].unsqueeze(1).broadcast_to([P, TT, P]),
                               ALU.add).then_inc(bias_added, 1)

        @block.scalar
        def _(act):
            act.wait_ge(angle_ready, 1)
            act.activation(sinr[:, :], vec[:, 1, :], ACT.Sin).then_inc(trig_ready, 1)
            act.activation(cosr[:, :], vec[:, 1, :], ACT.Sin, scale=0.5).then_inc(trig_ready, 1)

            def keep(n):
                g, c = items[n]
                act.wait_ge(hid_ready, n + 1)
                if n >= 3:
                    act.wait_ge(act_ready, n - 2)
                act.activation(h[:, n % 3, :], hid[n % 2][:, :], ACT.Identity, bias=vec[:, 0, c:c + 1]).then_inc(hid_kept, 1)

            def sine(n):
                act.wait_ge(y_ready, n + 1)
                act.activation(y[:, n % 3, :], y[:, n % 3, :], ACT.Sin).then_inc(sine_done, 1)

            def relu(n):
                g, c = items[n]
                act.wait_ge(q_ready, n + 1)
                if g >= 2:
                    act.wait_ge(out_ready, g - 1)
                act.activation(a[:, g % 2, c, :], h[:, n % 3, :], ACT.Relu).then_inc(act_ready, 1)

            keep(0)
            for n in range(len(items)):
                if n + 1 < len(items):
                    keep(n + 1)
                sine(n)
                if n >= 1:
                    relu(n - 1)
            relu(len(items) - 1)

        @block.vector
        def _(dve):
            step = Count(dve_step)
            dve.wait_ge(w_in, 64)
            turns_removed(dve, step, vec[:, 1, :], room[:, :]).then_inc(angle_ready, 1)
            dve.wait_ge(trig_ready, 2)
            step.then_wait(dve, dve.tensor_tensor(cosr[:, :], cosr[:, :], cosr[:, :], ALU.mult))
            step.then_wait(dve, dve.tensor_scalar(cosr[:, :], cosr[:, :], -2.0, 1.0, ALU.mult, ALU.add))
            step.then_wait(dve, dve.tensor_tensor(cosr[:, :], cosr[:, :], vec[:, 2, :], ALU.mult))
            step.then_wait(dve, dve.tensor_tensor(coef[:, :], sinr[:, :], vec[:, 3, :], ALU.mult))
            step.then_wait(dve, dve.tensor_tensor(coef[:, :], coef[:, :], cosr[:, :], ALU.add))
            step.then_wait(dve, dve.tensor_tensor(coef[:, :], coef[:, :], vec[:, 3, :], ALU.mult))
            step.then_wait(dve, dve.tensor_scalar(coef[:, :], coef[:, :], 0.1, None, ALU.mult))

            def angle(n):
                g, c = items[n]
                dve.wait_ge(hid_kept, n + 1)
                s = y[:, n % 3, :]
                step.then_wait(dve, dve.tensor_scalar(s, h[:, n % 3, :], 0.1, vec[:, 1, c:c + 1], ALU.mult, ALU.add))
                turns_removed(dve, step, s, m[:, :]).then_inc(y_ready, 1)

            def combine(n):
                g, c = items[n]
                dve.wait_ge(sine_done, n + 1)
                dve.scalar_tensor_tensor(h[:, n % 3, :], y[:, n % 3, :], coef[:, c:c + 1], h[:, n % 3, :],
                                         ALU.mult, ALU.add).then_inc(q_ready, 1)

            def add(g):
                dve.wait_ge(out_ready, g + 1)
                dve.wait_ge(bias_added, 1)
                s = x[:, 4 * g:4 * g + 4, :]
                dve.tensor_tensor(s, outp[g % 2][:, :, :], s, ALU.add).then_inc(out_kept, 1)

            for n in range(len(items)):
                angle(n)
                if n >= 1:
                    combine(n - 1)
                if n % FC == 1 and n > FC:
                    add(n // FC - 1)
            combine(len(items) - 1)
            add(3)

        @block.tensor
        def _(pe):
            pe.wait_ge(w_in, 64)

            def down(g):
                if g >= 2:
                    pe.wait_ge(out_kept, g - 1)
                for c in range(FC):
                    pe.wait_ge(act_ready, FC * g + c + 1)
                    for t in range(4):
                        mm = pe.matmul(outp[g % 2][:, t, :], a[:, g % 2, c, t * P:(t + 1) * P], w2[:, c, :],
                                       start=(c == 0 and t == 0), stop=(c == FC - 1), skip_group_check=True)
                mm.then_inc(out_ready, 1)

            for n, (g, c) in enumerate(items):
                if n >= 2:
                    pe.wait_ge(hid_kept, n - 1)
                pe.matmul(hid[n % 2][:, :], w1[:, c * P:(c + 1) * P], xnT[:, g * 512:(g + 1) * 512],
                          start=True, stop=True).then_inc(hid_ready, 1)
                if c == 1 and g >= 1:
                    down(g - 1)
            down(3)
def l1_attention(nc, d, x, xnT, ident):
    DI = d["a1_out"].shape[0]
    scale = DI ** -0.5
    with ExitStack() as ctx:
        sb, pb, sem = scope(nc, ctx, "l1a")
        wqkv, wout, bout = sb("wqkv", [P, 3 * DI]), sb("wout", [2 * DI, P]), sb("bout", [P, P])
        maskf, mask, identb = sb("maskf", [P, P]), sb("mask", [P, P], BF16), sb("identb", [P, P], BF16)
        qa, ka = sb("qa", [DI + 1, 2, SEQ]), sb("ka", [DI + 1, 2, SEQ])
        qr, kr = sb("qr", [DI, 2, SEQ], F32R), sb("kr", [DI, 2, SEQ], F32R)
        E = sb("E", [P, 2, 36 * P])
        V1 = sb("V1", [P, ST, 2, DI + 1])
        AO, AT = sb("AO", [P, ST, 2, DI]), sb("AT", [P, ST, P])
        mx, mh, ml = sb("mx", [P, 2, ST]), sb("mh", [P, 2, ST], BF16), sb("ml", [P, 2, ST], BF16)
        rs = sb("rs", [P, ST, 2])
        ring = [pb(f"ring{n}", [P, SEQ]) for n in range(2)]
        agg = [pb(f"agg{n}", [P, 512]) for n in range(4)]
        w_in, pool_step, dve_step, bf_ready = sem("w_in"), sem("pool_step"), sem("dve_step"), sem("bf_ready")
        q_ready, k_ready, v_ready = sem("q_ready"), sem("k_ready"), sem("v_ready")
        q_kept, k_kept, v_kept, rounded = sem("q_kept"), sem("k_kept"), sem("v_kept"), sem("rounded")
        rowmax_ready, max_done, mparts = sem("rowmax_ready"), sem("max_done"), sem("mparts")
        mrow_ready, mrow_kept = sem("mrow_ready"), sem("mrow_kept")
        score_ready, exp_done, masked = sem("score_ready"), sem("exp_done"), sem("masked")
        agg_ready, ao_ready, at_ready, at_kept = sem("agg_ready"), sem("ao_ready"), sem("at_ready"), sem("at_kept")
        y_ready, y_added = sem("y_ready"), sem("y_added")
        ecol = [sum(SEQ - P * k for k in range(jt)) for jt in range(ST)]

        def e_tile(b, jt, it):
            at = ecol[jt] + (it - jt) * P
            return E[:, b, at:at + P]

        block = ctx.enter_context(nc.Block(no_gpsimd_drain=True))

        @block.sync
        def _(sp):
            for dst, src in ((wqkv[:, :], d["a1_qkv"]), (maskf[:, :], d["cmask"]), (wout[0:DI, :], d["a1_out"]),
                             (wout[DI:2 * DI, :], d["a1_out"]), (bout[:, :], d["a1_bout"].partition_broadcast(P))):
                sp.dma_start(dst, src).then_inc(w_in, 16)

        @block.gpsimd
        def _(pool):
            pool.memset(V1[:, :, :, DI:DI + 1], 1.0).then_inc(pool_step, 1)
            pool.wait_ge(pool_step, 1)
            pool.memset(ka[DI:DI + 1, :, :], 1.0).then_inc(pool_step, 1)
            pool.wait_ge(pool_step, 2)
            pool.wait_ge(w_in, 80)
            pool.tensor_tensor(x[:, :, :], x[:, :, :], bout[:, :].unsqueeze(1).broadcast_to([P, TT, P]),
                               ALU.add).then_inc(pool_step, 1)
            for b in range(2):
                for jt in range(ST):
                    pool.wait_ge(exp_done, ST * b + jt + 1)
                    tile = e_tile(b, jt, jt)
                    pool.affine_select(out=tile, in_=tile, compare_op=ALU.is_ge, fill=0.0, base=0,
                                       pattern=[[1, P]], channel_multiplier=-1).then_inc(masked, 1)

        @block.scalar
        def _(act):
            for b in range(2):
                act.wait_ge(q_ready, b + 1)
                act.activation(qa[0:DI, b, :], ring[b][0:DI, :], ACT.Copy, scale=scale).then_inc(q_kept, 1)
            for b in range(2):
                act.wait_ge(mrow_ready, b + 1)
                act.activation(qa[DI:DI + 1, b, :], ring[b][0:1, :], ACT.Copy, scale=-1.0).then_inc(mrow_kept, 1)
            for n in range(2 * ST):
                b, jt = n // ST, n % ST
                act.wait_ge(score_ready, n + 1)
                w = SEQ - P * jt
                act.activation(E[:, b, ecol[jt]:ecol[jt] + w], ring[n % 2][:, 0:w], ACT.Exp).then_inc(exp_done, 1)
            for it in range(ST):
                act.wait_ge(at_ready, it + 1)
                act.activation(AT[:, it, :], agg[2 + it % 2][:, 0:P], ACT.Copy).then_inc(at_kept, 1)

        @block.tensor
        def _(pe):
            pe.wait_ge(w_in, 80)
            for b in range(2):
                for c in range(2):
                    mm = pe.matmul(ring[b][0:DI, c * 512:(c + 1) * 512], wqkv[:, 0:DI],
                                   xnT[:, b * SEQ + c * 512:b * SEQ + (c + 1) * 512], start=True, stop=True)
                mm.then_inc(q_ready, 1)
            for b in range(2):
                pe.wait_ge(q_kept, b + 1)
                for c in range(2):
                    mm = pe.matmul(ring[b][0:DI, c * 512:(c + 1) * 512], wqkv[:, DI:2 * DI],
                                   xnT[:, b * SEQ + c * 512:b * SEQ + (c + 1) * 512], start=True, stop=True)
                mm.then_inc(k_ready, 1)
            for b in range(2):
                for t in range(ST):
                    mm = pe.matmul(agg[b][:, t * DI:(t + 1) * DI], xnT[:, b * SEQ + t * P:b * SEQ + (t + 1) * P],
                                   wqkv[:, 2 * DI:3 * DI], start=True, stop=True)
                mm.then_inc(v_ready, 1)
            pe.wait_ge(bf_ready, 1)
            for n in range(2 * ST):
                it, b = n // 2, n % 2
                if n < 2:
                    pe.wait_ge(k_kept, n + 1)
                    pe.wait_ge(rounded, 2 * (n + 1))
                else:
                    pe.wait_ge(max_done, n - 1)
                w = (it + 1) * P
                for c0 in range(0, w, 512):
                    c1 = min(w, c0 + 512)
                    pe.matmul(ring[n % 2][:, c0:c1], qr[:, b, it * P:(it + 1) * P], kr[:, b, c0:c1],
                              start=True, stop=c1 < w)
                pe.matmul(ring[n % 2][:, it * P:w], identb[:, :], mask[:, :], start=False,
                          stop=True).then_inc(rowmax_ready, 1)
            for b in range(2):
                pe.wait_ge(mparts, b + 1)
                for it in range(ST):
                    pe.matmul(ring[b][0:1, it * P:(it + 1) * P], mh[:, b, it:it + 1], identb[:, :], start=True, stop=False)
                    mm = pe.matmul(ring[b][0:1, it * P:(it + 1) * P], ml[:, b, it:it + 1], identb[:, :],
                                   start=False, stop=True)
                mm.then_inc(mrow_ready, 1)
            for n in range(2 * ST):
                b, jt = n // ST, n % ST
                if n == 0:
                    pe.wait_ge(pool_step, 2)
                if n < 2:
                    pe.wait_ge(mrow_kept, n + 1)
                else:
                    pe.wait_ge(exp_done, n - 1)
                w = SEQ - P * jt
                for c0 in range(0, w, 512):
                    c1 = min(w, c0 + 512)
                    mm = pe.matmul(ring[n % 2][:, c0:c1], ka[:, b, jt * P:(jt + 1) * P],
                                   qa[:, b, P * jt + c0:P * jt + c1], start=True, stop=True)
                mm.then_inc(score_ready, 1)
            pe.wait_ge(v_kept, 2)

            def turn(it):
                pe.wait_ge(ao_ready, it + 1)
                if it >= 2:
                    pe.wait_ge(at_kept, it - 1)
                pe.transpose(agg[2 + it % 2][:, 0:P], AO[:, it, :, :].rearrange("p a b -> p (a b)"),
                             ident[:, :]).then_inc(at_ready, 1)

            for it in range(ST):
                if it >= 2:
                    pe.wait_ge(ao_ready, it - 1)
                pe.wait_ge(masked, ST + it + 1)
                for b in range(2):
                    for jt in range(it + 1):
                        mm = pe.matmul(agg[it % 2][:, b * 65:(b + 1) * 65], e_tile(b, jt, it), V1[:, jt, b, :],
                                       start=(jt == 0), stop=(jt == it))
                mm.then_inc(agg_ready, 1)
                if it >= 1:
                    turn(it - 1)
            turn(ST - 1)
            for g in range(4):
                b = g // 2
                if g < 2:
                    pe.wait_ge(at_kept, ST)
                    pe.wait_ge(ao_ready, ST)
                else:
                    pe.wait_ge(y_added, g - 1)
                for t in range(4):
                    mm = pe.matmul(agg[g % 2][:, t * P:(t + 1) * P], AT[b * DI:(b + 1) * DI, 4 * (g % 2) + t, :],
                                   wout[b * DI:(b + 1) * DI, :], start=True, stop=True)
                mm.then_inc(y_ready, 1)

        @block.vector
        def _(dve):
            step = Count(dve_step)
            dve.wait_ge(w_in, 80)
            step.then_wait(dve, dve.tensor_copy(mask[:, :], maskf[:, :]))
            dve.tensor_copy(identb[:, :], ident[:, :]).then_inc(bf_ready, 1)
            for b in range(2):
                dve.wait_ge(k_ready, b + 1)
                dve.tensor_copy(ka[0:DI, b, :], ring[b][0:DI, :]).then_inc(k_kept, 1)
            for b in range(2):
                dve.wait_ge(v_ready, b + 1)
                dve.tensor_copy(V1[:, :, b, 0:DI], agg[b][:, :].rearrange("p (t w) -> p t w", t=ST)).then_inc(v_kept, 1)
            for b in range(2):
                dve.wait_ge(q_kept, b + 1)
                dve.wait_ge(k_kept, b + 1)
                dve.tensor_copy(qr[:, b, :], qa[0:DI, b, :]).then_inc(rounded, 1)
                dve.tensor_copy(kr[:, b, :], ka[0:DI, b, :]).then_inc(rounded, 1)
            for n in range(2 * ST):
                it, b = n // 2, n % 2
                dve.wait_ge(rowmax_ready, n + 1)
                dve.tensor_reduce(mx[:, b, it:it + 1], ring[n % 2][:, 0:(it + 1) * P], AX_X, ALU.max).then_inc(max_done, 1)
            dve.wait_ge(max_done, 2 * ST)
            for b in range(2):
                step.then_wait(dve, dve.tensor_copy(mh[:, b, :], mx[:, b, :]))
                dve.tensor_tensor(ml[:, b, :], mx[:, b, :], mh[:, b, :], ALU.subtract).then_inc(mparts, 1)
            for it in range(ST):
                dve.wait_ge(agg_ready, it + 1)
                a = agg[it % 2][:, 0:130].rearrange("p (h w) -> p h w", h=2)
                step.then_wait(dve, dve.reciprocal(rs[:, it, :], a[:, :, DI]))
                dve.tensor_tensor(AO[:, it, :, :], a[:, :, 0:DI], spread(rs[:, it, :], [P, 2, DI]), ALU.mult).then_inc(ao_ready, 1)
            dve.wait_ge(pool_step, 3)
            for g in range(4):
                dve.wait_ge(y_ready, g + 1)
                s = x[:, 4 * g:4 * g + 4, :]
                dve.tensor_tensor(s, agg[g % 2][:, :].rearrange("p (t w) -> p t w", t=4), s, ALU.add).then_inc(y_added, 1)
NE = 8


def first_best(dve, step, pick, score, best, rank, prio, shape):
    step.then_wait(dve, dve.tensor_reduce(best, score, AX_X, ALU.max))
    step.then_wait(dve, dve.tensor_tensor(rank, score, spread(best, shape), ALU.is_ge))
    step.then_wait(dve, dve.tensor_tensor(rank, rank, prio, ALU.mult))
    step.then_wait(dve, dve.tensor_reduce(best, rank, AX_X, ALU.max))
    step.then_wait(dve, dve.tensor_tensor(pick, rank, spread(best, shape), ALU.is_equal))


def gate_top1(nc, name, d, keys, x, xnT, ident, pick):
    wkey, bkeys, b2key = keys
    with ExitStack() as ctx:
        sb, pb, sem = scope(nc, ctx, name)
        wg, b2 = sb("wg", [P, NE]), sb("b2", [NE, P])
        bias = [sb(f"bias{n}", [P, NE]) for n in range(len(bkeys))]
        prio = sb("prio", [P, NE])
        score, rank, best = sb("score", [P, TT, NE]), sb("rank", [P, TT, NE]), sb("best", [P, TT])
        pickT = sb("pickT", [NE, TT, P])
        lg = pb("lg", [P, TT, NE])
        pt = [pb(f"pt{n}", [NE, 4, P]) for n in range(2)]
        bb = [pb(f"bb{n}", [P, 4, P]) for n in range(2)]
        w_in, lg_ready, dve_step, pick_ready = sem("w_in"), sem("lg_ready"), sem("dve_step"), sem("pick_ready")
        pt_ready, pt_kept, bb_ready, bb_added = sem("pt_ready"), sem("pt_kept"), sem("bb_ready"), sem("bb_added")
        block = ctx.enter_context(nc.Block(no_gpsimd_drain=True))
        NW = 16 * (3 + len(bkeys))

        @block.sync
        def _(sp):
            sp.dma_start(wg[:, :], d[wkey]).then_inc(w_in, 16)
            sp.dma_start(b2[:, :], d[b2key]).then_inc(w_in, 16)
            sp.dma_start(prio[:, :], d["prio"].partition_broadcast(P)).then_inc(w_in, 16)
            for t, k in zip(bias, bkeys):
                sp.dma_start(t[:, :], d[k].partition_broadcast(P)).then_inc(w_in, 16)

        @block.tensor
        def _(pe):
            pe.wait_ge(w_in, NW)
            for t in range(TT):
                mm = pe.matmul(lg[:, t, :], xnT[:, t * P:(t + 1) * P], wg[:, :], start=True, stop=True)
            mm.then_inc(lg_ready, 1)
            pe.wait_ge(pick_ready, 1)
            for g in range(4):
                if g >= 2:
                    pe.wait_ge(pt_kept, g - 1)
                for t in range(4):
                    mm = pe.transpose(pt[g % 2][:, t, :], pick[:, 4 * g + t, :], ident[:, :])
                mm.then_inc(pt_ready, 1)
                pe.wait_ge(pt_kept, g + 1)
                if g >= 2:
                    pe.wait_ge(bb_added, g - 1)
                for t in range(4):
                    mm = pe.matmul(bb[g % 2][:, t, :], pickT[:, 4 * g + t, :], b2[:, :], start=True, stop=True)
                mm.then_inc(bb_ready, 1)

        @block.scalar
        def _(act):
            for g in range(4):
                act.wait_ge(pt_ready, g + 1)
                act.activation(pickT[:, 4 * g:4 * g + 4, :], pt[g % 2][:, :, :], ACT.Copy).then_inc(pt_kept, 1)

        @block.vector
        def _(dve):
            step = Count(dve_step)
            shape = [P, TT, NE]
            dve.wait_ge(lg_ready, 1)
            src = lg
            for t in bias:
                step.then_wait(dve, dve.tensor_tensor(score[:, :, :], src[:, :, :],
                                                      t[:, :].unsqueeze(1).broadcast_to(shape), ALU.add))
                src = score
            first_best(dve, step, pick[:, :, :], score[:, :, :], best[:, :], rank[:, :, :],
                       prio[:, :].unsqueeze(1).broadcast_to(shape), shape)
            dve.engine_nop().then_inc(pick_ready, 1)
            for g in range(4):
                dve.wait_ge(bb_ready, g + 1)
                s = x[:, 4 * g:4 * g + 4, :]
                dve.tensor_tensor(s, bb[g % 2][:, :, :], s, ALU.add).then_inc(bb_added, 1)


def experts_dense(nc, name, kind, d, keys, x, xnT, cw):
    upkeys, b1key, downkey = keys
    NU = len(upkeys)
    F = d[upkeys[0]].shape[1]
    FC = F // P
    with ExitStack() as ctx:
        sb, pb, sem = scope(nc, ctx, name)
        up = [[sb(f"up{j}_{u}", [P, F]) for u in range(NU)] for j in range(2)]
        down = [sb(f"down{j}", [P, FC, P]) for j in range(2)]
        b1 = [sb(f"b1_{j}", [P, FC]) for j in range(2)]
        a = sb("a", [P, 2, FC, 512])
        gate = sb("gate", [P, 2, 512])
        hid = [pb(f"hid{n}", [P, 512]) for n in range(2 * NU)]
        outp = [pb(f"outp{n}", [P, 4, P]) for n in range(2)]
        w_in = [sem("w_in0"), sem("w_in1")]
        hid_ready, gate_done, act_ready = sem("hid_ready"), sem("gate_done"), sem("act_ready")
        out_ready, out_added = sem("out_ready"), sem("out_added")
        per_w = 16 * (NU + 1 + (b1key is not None))
        func = {"gelu": ACT.Gelu, "relu": ACT.Relu, "silu": ACT.Silu}[kind]
        block = ctx.enter_context(nc.Block(no_gpsimd_drain=True))

        @block.sync
        def _(sp):
            def load(e, j):
                for u, k in enumerate(upkeys):
                    sp.dma_start(up[j][u][:, :], d[k][bass.ds(e * P, P), :]).then_inc(w_in[j], 16)
                sp.dma_start(down[j][:, :, :].rearrange("p a b -> p (a b)"), d[downkey][bass.ds(e * P, P), :]).then_inc(w_in[j], 16)
                if b1key is not None:
                    sp.dma_start(b1[j][:, :], d[b1key][bass.ds(e * P, P), :]).then_inc(w_in[j], 16)
            load(0, 0)
            load(1, 1)
            with sp.Fori(0, NE // 2 - 1) as i:
                for j in range(2):
                    sp.wait_ge(out_ready, i * 8 + 4 * (j + 1))
                    load(i * 2 + 2 + j, j)

        def experts(eng, body):
            for j in range(2):
                body(0, j)
            with eng.Fori(1, NE // 2) as i:
                for j in range(2):
                    body(i, j)

        def each(upf, downf):
            for g in range(4):
                upf(g)
                if g >= 1:
                    downf(g - 1)
            downf(3)

        @block.tensor
        def _(pe):
            def body(i, j):
                pe.wait_ge(w_in[j], (i + 1) * per_w)

                def upf(g):
                    for c in range(FC):
                        n = (4 * j + g) * FC + c
                        wait(pe, act_ready, i * 8 * FC + n - 1)
                        for u in range(NU):
                            mm = pe.matmul(hid[(n % 2) * NU + u][:, :], up[j][u][:, c * P:(c + 1) * P],
                                           xnT[:, g * 512:(g + 1) * 512], start=True, stop=True)
                        mm.then_inc(hid_ready, 1)

                def downf(g):
                    m = 4 * j + g
                    wait(pe, out_added, i * 8 + m - 1)
                    for c in range(FC):
                        pe.wait_ge(act_ready, i * 8 * FC + m * FC + c + 1)
                        for t in range(4):
                            mm = pe.matmul(outp[g % 2][:, t, :], a[:, g % 2, c, t * P:(t + 1) * P], down[j][:, c, :],
                                           start=(c == 0 and t == 0), stop=(c == FC - 1), skip_group_check=True)
                    mm.then_inc(out_ready, 1)

                each(upf, downf)

            experts(pe, body)

        @block.scalar
        def _(act):
            def body(i, j):
                if b1key is not None:
                    act.wait_ge(w_in[j], (i + 1) * per_w)
                for g in range(4):
                    for c in range(FC):
                        n = (4 * j + g) * FC + c
                        act.wait_ge(hid_ready, i * 8 * FC + n + 1)
                        m = 4 * j + g
                        if NU == 1:
                            wait(act, out_ready, i * 8 + m - 1)
                            act.activation(a[:, g % 2, c, :], hid[n % 2][:, :], func, bias=b1[j][:, c:c + 1]).then_inc(act_ready, 1)
                        else:
                            wait(act, act_ready, i * 8 * FC + n - 1)
                            act.activation(gate[:, n % 2, :], hid[(n % 2) * NU][:, :], func).then_inc(gate_done, 1)

            experts(act, body)

        @block.vector
        def _(dve):
            def body(i, j):
                def upf(g):
                    if NU == 1:
                        return
                    for c in range(FC):
                        n = (4 * j + g) * FC + c
                        m = 4 * j + g
                        dve.wait_ge(gate_done, i * 8 * FC + n + 1)
                        wait(dve, out_ready, i * 8 + m - 1)
                        dve.tensor_tensor(a[:, g % 2, c, :], gate[:, n % 2, :], hid[(n % 2) * NU + 1][:, :],
                                          ALU.mult).then_inc(act_ready, 1)

                def downf(g):
                    m = 4 * j + g
                    dve.wait_ge(out_ready, i * 8 + m + 1)
                    for t in range(4):
                        s = x[:, 4 * g + t, :]
                        w = cw[:, 4 * g + t, :][:, bass.ds(i * 2 + j, 1)]
                        ins = dve.scalar_tensor_tensor(s, outp[g % 2][:, t, :], w, s, ALU.mult, ALU.add)
                    ins.then_inc(out_added, 1)

                each(upf, downf)

            experts(dve, body)
def l2_attention(nc, d, x, xnT, ident):
    NH = 16
    W = 3 * P + 1
    with ExitStack() as ctx:
        sb, pb, sem = scope(nc, ctx, "l2a")
        wkgv, wq, wo = sb("wkgv", [P, 3 * P]), sb("wq", [P, P]), sb("wo", [P, P])
        bkgv, bq, bo = sb("bkgv", [P, 3 * P]), sb("bq", [P, 1]), sb("bo", [P, P])
        heads = sb("heads", [P, P + NH])
        KGV = sb("KGV", [P, TT, W])
        room = sb("room", [P, ST, P])
        QT, qroom = sb("QT", [P, TOK]), sb("qroom", [P, TOK])
        RK = sb("RK", [P, NB, P + NH])
        z = sb("z", [P, TT, NH])
        O, OT = sb("O", [P, TT, P]), sb("OT", [P, TT, P])
        ring = [pb(f"ring{n}", [P, 512]) for n in range(2)]
        qp = [pb(f"qp{n}", [P, 512]) for n in range(2)]
        kv = pb("kv", [P, NB, 256])
        outp = [pb(f"outp{n}", [P, 4, P]) for n in range(2)]
        w_in, one_set, bo_added = sem("w_in"), sem("one_set"), sem("bo_added")
        kgv_ready, kgv_kept, q_ready, q_kept = sem("kgv_ready"), sem("kgv_kept"), sem("q_ready"), sem("q_kept")
        low_ready, exp_done, k_ready, g_exp, g_ready = (sem(n) for n in ("low_ready", "exp_done", "k_ready", "g_exp", "g_ready"))
        qlow_ready, qexp_done, qT_ready = sem("qlow_ready"), sem("qexp_done"), sem("qT_ready")
        kv_ready, rk_ready, num_ready, o_ready = sem("kv_ready"), sem("rk_ready"), sem("num_ready"), sem("o_ready")
        ot_ready, ot_kept, out_ready, out_added = sem("ot_ready"), sem("ot_kept"), sem("out_ready"), sem("out_added")
        dve_step = sem("dve_step")
        block = ctx.enter_context(nc.Block(no_gpsimd_drain=True))

        @block.sync
        def _(sp):
            for dst, src in ((wkgv, d["a2_wkgv"]), (bkgv, d["a2_bkgv"].partition_broadcast(P)), (wq, d["a2_wq"]),
                             (bq, d["a2_bq"]), (heads, d["heads"]), (wo, d["a2_wo"]), (bo, d["a2_bo"].partition_broadcast(P))):
                sp.dma_start(dst[:], src).then_inc(w_in, 16)

        @block.gpsimd
        def _(pool):
            pool.memset(KGV[:, :, 3 * P:W], 1.0).then_inc(one_set, 1)
            pool.wait_ge(w_in, 7 * 16)
            pool.tensor_tensor(x[:, :, :], x[:, :, :], bo[:, :].unsqueeze(1).broadcast_to([P, TT, P]),
                               ALU.add).then_inc(bo_added, 1)

        @block.tensor
        def _(pe):
            pe.wait_ge(w_in, 7 * 16)
            for t in range(TT):
                if t >= 2:
                    pe.wait_ge(kgv_kept, t - 1)
                pe.matmul(ring[t % 2][:, 0:3 * P], xnT[:, t * P:(t + 1) * P], wkgv[:, :], start=True,
                          stop=True).then_inc(kgv_ready, 1)
                if t % 4 == 3:
                    g = t // 4
                    if g >= 2:
                        pe.wait_ge(q_kept, g - 1)
                    pe.matmul(qp[g % 2][:, :], wq[:, :], xnT[:, g * 512:(g + 1) * 512], start=True,
                              stop=True).then_inc(q_ready, 1)
            for b in range(NB):
                pe.wait_ge(k_ready, b + 1)
                pe.wait_ge(one_set, 1)
                for t in range(b * ST, (b + 1) * ST):
                    mm = pe.matmul(kv[:, b, 0:P + 1], KGV[:, t, 0:P], KGV[:, t, 2 * P:W],
                                   start=(t == b * ST), stop=(t == (b + 1) * ST - 1))
                mm.then_inc(kv_ready, 1)

            def turn(g):
                pe.wait_ge(o_ready, 2 * (g + 1))
                if g >= 2:
                    pe.wait_ge(ot_kept, g - 1)
                for t in range(4):
                    mm = pe.transpose(qp[g % 2][:, t * P:(t + 1) * P], O[:, 4 * g + t, :], ident[:, :])
                mm.then_inc(ot_ready, 1)

            def project(g):
                pe.wait_ge(ot_kept, g + 1)
                if g >= 2:
                    pe.wait_ge(out_added, g - 1)
                for t in range(4):
                    mm = pe.matmul(outp[g % 2][:, t, :], OT[:, 4 * g + t, :], wo[:, :], start=True, stop=True)
                mm.then_inc(out_ready, 1)

            pe.wait_ge(qT_ready, 1)
            pe.wait_ge(q_kept, 4)
            for n in range(TT // 2):
                if n * 2 % ST == 0:
                    pe.wait_ge(rk_ready, n * 2 // ST + 1)
                if n >= 2:
                    pe.wait_ge(o_ready, n - 1)
                for j in range(2):
                    t = 2 * n + j
                    mm = pe.matmul(ring[n % 2][:, j * (P + NH):(j + 1) * (P + NH)], QT[:, t * P:(t + 1) * P],
                                   RK[:, t // ST, :], start=True, stop=True)
                mm.then_inc(num_ready, 1)
                if n % 2 == 0 and n >= 2:
                    turn(n // 2 - 1)
                if n % 2 == 1 and n >= 3:
                    project(n // 2 - 1)
            turn(3)
            project(3)

        @block.scalar
        def _(act):
            act.wait_ge(w_in, 7 * 16)
            for b in range(NB):
                for g in (2 * b, 2 * b + 1):
                    act.wait_ge(q_ready, g + 1)
                    act.activation(QT[:, g * 512:(g + 1) * 512], qp[g % 2][:, :], ACT.Identity, bias=bq[:, :]).then_inc(q_kept, 1)
                s = slice(b * ST, (b + 1) * ST)
                act.wait_ge(low_ready, b + 1)
                act.activation(room[:, :, :], room[:, :, :], ACT.Exp).then_inc(exp_done, 1)
                act.activation(KGV[:, s, P:2 * P], KGV[:, s, P:2 * P], ACT.Exp, scale=-1.0).then_inc(g_exp, 1)
            act.wait_ge(qlow_ready, 1)
            act.activation(qroom[:, :], qroom[:, :], ACT.Exp).then_inc(qexp_done, 1)
            for g in range(4):
                act.wait_ge(ot_ready, g + 1)
                act.activation(OT[:, 4 * g:4 * g + 4, :], qp[g % 2][:, :].rearrange("p (t w) -> p t w", t=4),
                               ACT.Copy).then_inc(ot_kept, 1)

        @block.vector
        def _(dve):
            step = Count(dve_step)
            dve.wait_ge(w_in, 7 * 16)
            for b in range(NB):
                s = slice(b * ST, (b + 1) * ST)
                for t in range(b * ST, (b + 1) * ST):
                    dve.wait_ge(kgv_ready, t + 1)
                    dve.tensor_tensor(KGV[:, t, 0:3 * P], ring[t % 2][:, 0:3 * P], bkgv[:, :], ALU.add).then_inc(kgv_kept, 1)
                dve.wait_ge(kgv_kept, (b + 1) * ST)
                dve.tensor_scalar(room[:, :, :], KGV[:, s, 0:P], 0.0, None, ALU.min).then_inc(low_ready, 1)
                dve.wait_ge(exp_done, b + 1)
                dve.scalar_tensor_tensor(KGV[:, s, 0:P], KGV[:, s, 0:P], 0.0, room[:, :, :], ALU.max, ALU.add).then_inc(k_ready, 1)
                dve.wait_ge(k_ready, b + 1)
                if b == NB - 1:
                    dve.wait_ge(q_kept, 4)
                    dve.tensor_scalar(qroom[:, :], QT[:, :], 0.0, None, ALU.min).then_inc(qlow_ready, 1)
                dve.wait_ge(g_exp, b + 1)
                step.then_wait(dve, dve.tensor_scalar(KGV[:, s, P:2 * P], KGV[:, s, P:2 * P], 1.0, None, ALU.add))
                step.then_wait(dve, dve.reciprocal(KGV[:, s, P:2 * P], KGV[:, s, P:2 * P]))
            dve.wait_ge(qexp_done, 1)
            dve.scalar_tensor_tensor(QT[:, :], QT[:, :], 0.0, qroom[:, :], ALU.max, ALU.add).then_inc(qT_ready, 1)
            for b in range(NB):
                dve.wait_ge(kv_ready, 2)
                dve.tensor_tensor(RK[:, b, 0:P], kv[:, b, 0:P], heads[:, 0:P], ALU.mult)
                dve.tensor_scalar(RK[:, b, P:P + NH], heads[:, P:P + NH], kv[:, b, P:P + 1], None, ALU.mult).then_inc(rk_ready, 1)

            def add(g):
                dve.wait_ge(out_ready, g + 1)
                s = x[:, 4 * g:4 * g + 4, :]
                dve.tensor_tensor(s, outp[g % 2][:, :, :], s, ALU.add).then_inc(out_added, 1)

            dve.wait_ge(bo_added, 1)
            for n in range(TT // 2):
                dve.wait_ge(num_ready, n + 1)
                ps = ring[n % 2][:, 0:2 * (P + NH)].rearrange("p (j w) -> p j w", j=2)
                s = slice(2 * n, 2 * n + 2)
                step.then_wait(dve, dve.tensor_scalar(z[:, s, :], ps[:, :, P:P + NH], 1e-6, None, ALU.add))
                step.then_wait(dve, dve.reciprocal(z[:, s, :], z[:, s, :]))
                for t in range(2):
                    ins = dve.tensor_tensor(O[:, 2 * n + t, :].rearrange("p (h w) -> p h w", h=NH),
                                            ps[:, t, 0:P].rearrange("p (h w) -> p h w", h=NH),
                                            spread(z[:, 2 * n + t, :], [P, NH, P // NH]), ALU.mult)
                    step.mark(ins)
                dve.wait_ge(step.sem, step.n)
                dve.tensor_tensor(O[:, s, :], O[:, s, :], KGV[:, s, P:2 * P], ALU.mult).then_inc(o_ready, 1)
                if n % 2 == 1 and n >= 5:
                    add(n // 2 - 2)
            add(2)
            add(3)
def route_top2(nc, d, x, xnT, ident, cw):
    CAP = int(1.25 * TOK / NE)
    R = P // NE
    DIGITS = 8
    with ExitStack() as ctx:
        sb, pb, sem = scope(nc, ctx, "rt")
        wr, prio = sb("wr", [P, NE]), sb("prio", [P, NE])
        digits = sb("digits", [P, DIGITS], I32)
        same = sb("same", [P, P])
        pickrow = sb("pickrow", [P, NE])
        prob, rank, one, two = (sb(n, [P, TT, NE]) for n in ("prob", "rank", "one", "two"))
        best, tot = sb("best", [P, TT]), sb("tot", [P, TT])
        wide = sb("wide", [P, TT, P])
        WR, keep, eq, cum = (sb(n, [P, TOK]) for n in ("WR", "keep", "eq", "cum"))
        zeros = sb("zeros", [P, TOK])
        T, cand, inc = sb("T", [P, 1], I32), sb("cand", [P, 1], I32), sb("inc", [P, 1], I32)
        cnt, flag, need = sb("cnt", [P, 1]), sb("flag", [P, 1]), sb("need", [P, 1])
        lg = pb("lg", [P, TT, NE])
        wt = [pb(f"wt{n}", [P, 512]) for n in range(4)]
        votes = pb("votes", [P, 512])
        cwp = pb("cwp", [P, TT, NE])
        w_in, lg_ready, exp_in, exp_done, wide_ready = (sem(n) for n in ("w_in", "lg_ready", "exp_in", "exp_done", "wide_ready"))
        wt_ready, wr_kept, flag_ready, votes_ready = sem("wt_ready"), sem("wr_kept"), sem("flag_ready"), sem("votes_ready")
        kept_ready, cwp_ready, dve_step, zero_set = sem("kept_ready"), sem("cwp_ready"), sem("dve_step"), sem("zero_set")
        block = ctx.enter_context(nc.Block(no_gpsimd_drain=True))

        @block.sync
        def _(sp):
            for dst, src in ((wr, d["f2_router"]), (prio, d["prio"].partition_broadcast(P)), (digits, d["digits"]),
                             (same, d["same16"]), (pickrow, d["pickrow"])):
                sp.dma_start(dst[:], src).then_inc(w_in, 16)

        @block.gpsimd
        def _(pool):
            pool.memset(zeros[:, :], 0.0).then_inc(zero_set, 1)
            pool.memset(T[:, :], 0).then_inc(zero_set, 1)

        @block.tensor
        def _(pe):
            pe.wait_ge(w_in, 80)
            for t in range(TT):
                mm = pe.matmul(lg[:, t, :], xnT[:, t * P:(t + 1) * P], wr[:, :], start=True, stop=True)
            mm.then_inc(lg_ready, 1)
            pe.wait_ge(wide_ready, 1)
            for g in range(4):
                for t in range(4):
                    mm = pe.transpose(wt[g][:, t * P:(t + 1) * P], wide[:, 4 * g + t, :], ident[:, :])
                mm.then_inc(wt_ready, 1)
            for k in range(DIGITS):
                pe.wait_ge(flag_ready, k + 1)
                pe.matmul(votes[:, 0:1], same[:, :], flag[:, :], start=True, stop=True).then_inc(votes_ready, 1)
            pe.wait_ge(kept_ready, 1)
            for t in range(TT):
                mm = pe.matmul(cwp[:, t, :], keep[:, t * P:(t + 1) * P], pickrow[:, :], start=True, stop=True)
            mm.then_inc(cwp_ready, 1)

        @block.scalar
        def _(act):
            act.wait_ge(exp_in, 1)
            act.activation(prob[:, :, :], prob[:, :, :], ACT.Exp).then_inc(exp_done, 1)
            for g in range(4):
                act.wait_ge(wt_ready, g + 1)
                act.activation(WR[:, g * 512:(g + 1) * 512], wt[g][:, :], ACT.Copy).then_inc(wr_kept, 1)

        @block.vector
        def _(dve):
            step = Count(dve_step)
            shape = [P, TT, NE]
            dve.wait_ge(w_in, 80)
            pr = prio[:, :].unsqueeze(1).broadcast_to(shape)
            dve.wait_ge(lg_ready, 1)
            step.then_wait(dve, dve.tensor_reduce(best[:, :], lg[:, :, :], AX_X, ALU.max))
            dve.tensor_tensor(prob[:, :, :], lg[:, :, :], spread(best[:, :], shape), ALU.subtract).then_inc(exp_in, 1)
            dve.wait_ge(exp_done, 1)
            step.then_wait(dve, dve.tensor_reduce(tot[:, :], prob[:, :, :], AX_X, ALU.add))
            step.then_wait(dve, dve.reciprocal(tot[:, :], tot[:, :]))
            step.then_wait(dve, dve.tensor_tensor(prob[:, :, :], prob[:, :, :], spread(tot[:, :], shape), ALU.mult))
            first_best(dve, step, one[:, :, :], prob[:, :, :], best[:, :], rank[:, :, :], pr, shape)
            step.then_wait(dve, dve.scalar_tensor_tensor(two[:, :, :], one[:, :, :], -2.0, prob[:, :, :], ALU.mult, ALU.add))
            first_best(dve, step, two[:, :, :], two[:, :, :], best[:, :], rank[:, :, :], pr, shape)
            step.then_wait(dve, dve.tensor_tensor(one[:, :, :], one[:, :, :], two[:, :, :], ALU.add))
            step.then_wait(dve, dve.tensor_tensor(prob[:, :, :], prob[:, :, :], one[:, :, :], ALU.mult))
            step.then_wait(dve, dve.tensor_reduce(tot[:, :], prob[:, :, :], AX_X, ALU.add))
            step.then_wait(dve, dve.tensor_scalar(tot[:, :], tot[:, :], 1e-6, None, ALU.add))
            step.then_wait(dve, dve.reciprocal(tot[:, :], tot[:, :]))
            step.then_wait(dve, dve.tensor_tensor(prob[:, :, :], prob[:, :, :], spread(tot[:, :], shape), ALU.mult))
            dve.tensor_copy(wide[:, :, :].rearrange("p t (e r) -> p (t e) r", r=R),
                            spread(prob[:, :, :].rearrange("p t e -> p (t e)"), [P, TT * NE, R])).then_inc(wide_ready, 1)
            dve.wait_ge(wr_kept, 4)
            dve.wait_ge(zero_set, 2)
            for k in range(DIGITS):
                step.then_wait(dve, dve.tensor_tensor(cand[:, :], T[:, :], digits[:, k:k + 1], ALU.bitwise_or))
                step.then_wait(dve, dve.tensor_scalar(keep[:, :], WR[:, :], cand[:, :].bitcast(F32), 0.0, ALU.is_ge,
                                                      ALU.add, accum_out=cnt[:, :]))
                dve.tensor_scalar(flag[:, :], cnt[:, :], CAP - 0.5, None, ALU.is_ge).then_inc(flag_ready, 1)
                dve.wait_ge(votes_ready, k + 1)
                step.then_wait(dve, dve.tensor_scalar(inc[:, :], votes[:, 0:1], 1.0, float(2 ** (28 - 4 * k)),
                                                      ALU.subtract, ALU.mult))
                step.then_wait(dve, dve.tensor_tensor(T[:, :], T[:, :], inc[:, :], ALU.bitwise_or))
            cut = T[:, :].bitcast(F32)
            step.then_wait(dve, dve.tensor_scalar(keep[:, :], WR[:, :], cut, 0.0, ALU.is_gt, ALU.add, accum_out=cnt[:, :]))
            step.then_wait(dve, dve.tensor_scalar(need[:, :], cnt[:, :], -1.0, CAP + 0.5, ALU.mult, ALU.add))
            step.then_wait(dve, dve.tensor_scalar(eq[:, :], WR[:, :], cut, None, ALU.is_equal))
            step.then_wait(dve, dve.tensor_tensor_scan(cum[:, :], eq[:, :], zeros[:, :], 0.0, ALU.add, ALU.add))
            step.then_wait(dve, dve.scalar_tensor_tensor(eq[:, :], cum[:, :], need[:, :], eq[:, :], ALU.is_le, ALU.mult))
            step.then_wait(dve, dve.tensor_tensor(keep[:, :], keep[:, :], eq[:, :], ALU.add))
            dve.tensor_tensor(keep[:, :], keep[:, :], WR[:, :], ALU.mult).then_inc(kept_ready, 1)
            dve.wait_ge(cwp_ready, 1)
            dve.tensor_copy(cw[:, :, :], cwp[:, :, :]).then_inc(dve_step, 1)
def l3_mixer(nc, d, x, xnT, ident):
    DI = d["m_conv"].shape[0]
    HALF = DI // P
    NS = d["m_alog"].shape[1]
    RK = d["m_wdt"].shape[0]
    KC = d["m_conv"].shape[1]
    PAD = KC - 1
    with ExitStack() as ctx:
        sb, pb, sem = scope(nc, ctx, "mx")
        win = sb("win", [P, 2 * DI])
        conv, convb = sb("conv", [P, HALF, KC]), sb("convb", [P, HALF])
        wdt8, wbc = sb("wdt8", [P, HALF, RK]), sb("wbc", [P, HALF, 2 * NS])
        wdt = sb("wdt", [RK, DI])
        bdt, A, Dp = sb("bdt", [P, HALF]), sb("A", [P, HALF, NS]), sb("Dp", [P, HALF])
        wout = sb("wout", [P, HALF, P])
        sel1 = sb("sel1", [96, 2 * NS])
        sel = sb("sel", [96, 2 * NS, P], BF16)
        XI = sb("XI", [P, HALF, NB, PAD + SEQ])
        XC, SZ, DT = (sb(n, [P, HALF, TOK]) for n in ("XC", "SZ", "DT"))
        V, Ex = sb("V", [P, TOK]), sb("Ex", [P, TOK])
        dt8 = sb("dt8", [RK, TOK])
        bc, rest = sb("bc", [96, TOK], BF16), sb("rest", [32, TOK])
        dA, dBu, hst = sb("dA", [P, 2, HALF, SEQ]), sb("dBu", [P, 2, HALF, SEQ]), sb("hst", [P, 2, HALF, SEQ])
        BB = sb("BB", [P, 2, SEQ])
        Bp, Cp = pb("Bp", [P, SEQ]), pb("Cp", [P, SEQ])
        ysum = [pb(f"ysum{h}", [P, SEQ]) for h in range(HALF)]
        work = [Bp, Cp, ysum[0], ysum[1]]
        w_in, pads, proj_ready, proj_kept = sem("w_in"), sem("pads"), sem("proj_ready"), sem("proj_kept")
        tap_done, conv_ready, xc_ready = sem("tap_done"), sem("conv_ready"), sem("xc_ready")
        dbl_ready, dbl_kept, step_ready, v_kept = sem("dbl_ready"), sem("dbl_kept"), sem("step_ready"), sem("v_kept")
        abs_ready, e_ready, u_ready, ln_ready, dt_ready = (sem(n) for n in ("abs_ready", "e_ready", "u_ready", "ln_ready", "dt_ready"))
        a_exp, a_ready, du_ready, dve_step = sem("a_exp"), sem("a_ready"), sem("du_ready"), sem("dve_step")
        b_ready, b_kept, c_ready, dA_ready, dBu_ready = (sem(n) for n in ("b_ready", "b_kept", "c_ready", "dA_ready", "dBu_ready"))
        scanned, hc_ready, summed, y_ready = sem("scanned"), sem("hc_ready"), sem("summed"), sem("y_ready")
        rest_kept = sem("rest_kept")
        out_ready, out_added, bc_ready, ysum_ready = sem("out_ready"), sem("out_added"), sem("bc_ready"), sem("ysum_ready")
        block = ctx.enter_context(nc.Block(no_gpsimd_drain=True))
        loads = ((win, "m_win"), (conv, "m_conv3"), (convb, "m_convb"), (wdt8, "m_wx_dt"), (wbc, "m_wx_bc"), (wdt, "m_wdt"),
                 (bdt, "m_bdt"), (A, "m_alog3"), (Dp, "m_D"), (wout, "m_wout"), (sel1, "sel32"))
        NW = 16 * len(loads)
        du = XI

        def du_of(h, b):
            return du[:, h, b, 0:SEQ]

        @block.sync
        def _(sp):
            for dst, k in loads:
                sp.dma_start(dst[:], d[k]).then_inc(w_in, 16)

        @block.tensor
        def _(pe):
            pe.wait_ge(w_in, NW)
            items = [(p, h, b) for p in range(2) for h in range(HALF) for b in range(NB)]
            for n, (p, h, b) in enumerate(items):
                if n >= 4:
                    pe.wait_ge(proj_kept, n - 3)
                for c in range(2):
                    mm = pe.matmul(work[n % 4][:, c * 512:(c + 1) * 512], win[:, p * DI + h * P:p * DI + (h + 1) * P],
                                   xnT[:, b * SEQ + c * 512:b * SEQ + (c + 1) * 512], start=True, stop=True)
                mm.then_inc(proj_ready, 1)
            for b in range(NB):
                pe.wait_ge(proj_kept, 8)
                pe.wait_ge(xc_ready, HALF * NB)
                for m, (wt, rows) in enumerate(((wbc, 2 * NS), (wdt8, RK))):
                    for c in range(2):
                        for h in range(HALF):
                            mm = pe.matmul(work[2 * b + m][0:rows, c * 512:(c + 1) * 512], wt[:, h, :],
                                           XC[:, h, b * SEQ + c * 512:b * SEQ + (c + 1) * 512],
                                           start=(h == 0), stop=(h == HALF - 1))
                    mm.then_inc(dbl_ready, 1)
            for n, (h, b) in enumerate((h, b) for h in range(HALF) for b in range(NB)):
                pe.wait_ge(dbl_kept, NB)
                pe.wait_ge(rest_kept, NB)
                for c in range(2):
                    mm = pe.matmul(work[n][:, c * 512:(c + 1) * 512], wdt[:, h * P:(h + 1) * P],
                                   dt8[:, b * SEQ + c * 512:b * SEQ + (c + 1) * 512], start=True, stop=True)
                mm.then_inc(step_ready, 1)
            pe.wait_ge(bc_ready, 1)
            pe.wait_ge(v_kept, 4)

            def rows(out, r, b, ready):
                for c in range(2):
                    mm = pe.matmul(out[:, c * 512:(c + 1) * 512], sel[:, r, :],
                                   bc[:, b * SEQ + c * 512:b * SEQ + (c + 1) * 512], start=True, stop=True)
                mm.then_inc(ready, 1)

            def total(b, i, j, first, last):
                for h in range(HALF):
                    pe.wait_ge(hc_ready, NS * HALF * b + i * 2 * HALF + j * HALF + h + 1)
                    for c in range(2):
                        mm = pe.matmul(ysum[h][:, c * 512:(c + 1) * 512], ident[:, :],
                                       hst[:, j, h, c * 512:(c + 1) * 512], start=first, stop=last,
                                       skip_group_check=True)
                mm.then_inc(summed, 1)

            for b in range(NB):
                if b:
                    pe.wait_ge(y_ready, HALF * b)
                def states(i, first, last):
                    for j in range(2):
                        n = NS * b + i * 2 + j
                        wait(pe, b_kept, n)
                        wait(pe, hc_ready, n * HALF)
                        rows(Bp, i * 2 + j, b, b_ready)
                        rows(Cp, i * 2 + j + NS, b, c_ready)
                        if j == 1:
                            total(b, i, 0, first, False)
                    total(b, i, 1, False, last)
                states(0, True, False)
                with pe.Fori(1, NS // 2 - 1) as i:
                    states(i, False, False)
                states(NS // 2 - 1, False, True)
                pe.wait_ge(ysum_ready, HALF * (b + 1))
                for g in range(2):
                    for t in range(4):
                        for h in range(HALF):
                            tok = b * SEQ + (4 * g + t) * P
                            mm = pe.matmul(ysum[g][:, t * P:(t + 1) * P], XC[:, h, tok:tok + P], wout[:, h, :],
                                           start=(h == 0), stop=(h == HALF - 1))
                    mm.then_inc(out_ready, 1)

        @block.scalar
        def _(act):
            act.wait_ge(w_in, NW)
            items = [(p, h, b) for p in range(2) for h in range(HALF) for b in range(NB)]
            for n, (p, h, b) in enumerate(items):
                act.wait_ge(proj_ready, n + 1)
                if p == 0:
                    act.wait_ge(pads, 1)
                    act.activation(XI[:, h, b, PAD:PAD + SEQ], work[n % 4][:, :], ACT.Copy).then_inc(proj_kept, 1)
                else:
                    act.activation(SZ[:, h, b * SEQ:(b + 1) * SEQ], work[n % 4][:, :], ACT.Silu).then_inc(proj_kept, 1)
            for n, (h, b) in enumerate((h, b) for h in range(HALF) for b in range(NB)):
                s = XC[:, h, b * SEQ:(b + 1) * SEQ]
                act.wait_ge(conv_ready, n + 1)
                act.activation(s, s, ACT.Silu, bias=convb[:, h:h + 1]).then_inc(xc_ready, 1)
            for b in range(NB):
                act.wait_ge(dbl_ready, 2 * b + 2)
                act.activation(dt8[:, b * SEQ:(b + 1) * SEQ], work[2 * b + 1][0:RK, :], ACT.Copy).then_inc(dbl_kept, 1)
            act.activation(A[:, :, :], A[:, :, :], ACT.Exp).then_inc(a_exp, 1)
            for h in range(HALF):
                if h:
                    act.wait_ge(dt_ready, h)
                for b in range(NB):
                    act.wait_ge(step_ready, NB * h + b + 1)
                    act.activation(Ex[:, b * SEQ:(b + 1) * SEQ], work[NB * h + b][:, :], ACT.Abs,
                                   bias=bdt[:, h:h + 1]).then_inc(abs_ready, 1)
                    act.activation(V[:, b * SEQ:(b + 1) * SEQ], work[NB * h + b][:, :], ACT.Identity,
                                   bias=bdt[:, h:h + 1]).then_inc(v_kept, 1)
                act.wait_ge(abs_ready, NB * (h + 1))
                act.activation(Ex[:, :], Ex[:, :], ACT.Exp, scale=-1.0).then_inc(e_ready, 1)
                act.wait_ge(u_ready, h + 1)
                act.activation(DT[:, h, :], DT[:, h, :], ACT.Ln).then_inc(ln_ready, 1)
            act.wait_ge(a_ready, 1)
            act.wait_ge(dt_ready, HALF)
            for b in range(NB):
                def states(i):
                    for j in range(2):
                        n = i * 2 + j + NS * b
                        act.wait_ge(b_ready, n + 1)
                        wait(act, dBu_ready, (n - 1) * HALF)
                        act.activation(BB[:, j, :], Bp[:, :], ACT.Copy).then_inc(b_kept, 1)
                        for h in range(HALF):
                            wait(act, scanned, (n - 1) * HALF)
                            act.activation(dA[:, j, h, :], DT[:, h, b * SEQ:(b + 1) * SEQ], ACT.Exp,
                                           scale=A[:, h, :][:, bass.ds(i * 2 + j, 1)]).then_inc(dA_ready, 1)

                states(0)
                with act.Fori(1, NS // 2) as i:
                    states(i)

        @block.gpsimd
        def _(pool):
            pool.memset(XI[:, :, :, 0:PAD], 0.0).then_inc(pads, 1)
            pool.wait_ge(du_ready, HALF * NB)
            for b in range(NB):
                def states(i):
                    for j in range(2):
                        n = i * 2 + j + NS * b
                        pool.wait_ge(b_kept, n + 1)
                        for h in range(HALF):
                            wait(pool, scanned, (n - 1) * HALF)
                            pool.tensor_tensor(dBu[:, j, h, :], du_of(h, b), BB[:, j, :], ALU.mult).then_inc(dBu_ready, 1)

                states(0)
                with pool.Fori(1, NS // 2) as i:
                    states(i)

        @block.vector
        def _(dve):
            step = Count(dve_step)
            dve.wait_ge(w_in, NW)
            dve.wait_ge(pads, 1)
            step.then_wait(dve, dve.tensor_copy(sel[:, :, :], spread(sel1[:, :], [96, 2 * NS, P])))
            for n, (h, b) in enumerate((h, b) for h in range(HALF) for b in range(NB)):
                dve.wait_ge(proj_kept, n + 1)
                s = XC[:, h, b * SEQ:(b + 1) * SEQ]
                step.then_wait(dve, dve.tensor_scalar(s, XI[:, h, b, 0:SEQ], conv[:, h, 0:1], None, ALU.mult))
                for k in range(1, KC):
                    ins = dve.scalar_tensor_tensor(s, XI[:, h, b, k:k + SEQ], conv[:, h, k:k + 1], s, ALU.mult, ALU.add)
                    if k < KC - 1:
                        step.then_wait(dve, ins)
                ins.then_inc(conv_ready, 1)
            for b in range(NB):
                c = slice(b * SEQ, (b + 1) * SEQ)
                dve.wait_ge(dbl_ready, 2 * b + 1)
                dve.tensor_copy(rest[:, c], work[2 * b][0:32, :]).then_inc(rest_kept, 1)
            dve.wait_ge(rest_kept, NB)
            for b in range(NB):
                c = slice(b * SEQ, (b + 1) * SEQ)
                step.then_wait(dve, dve.tensor_copy(bc[0:32, c], rest[:, c]))
                step.then_wait(dve, dve.tensor_tensor(rest[:, c], rest[:, c], bc[0:32, c], ALU.subtract))
                step.then_wait(dve, dve.tensor_copy(bc[32:64, c], rest[:, c]))
                step.then_wait(dve, dve.tensor_copy(bc[64:96, c], bc[32:64, c]))
                step.then_wait(dve, dve.tensor_tensor(rest[:, c], rest[:, c], bc[32:64, c], ALU.subtract))
                ins = dve.tensor_copy(bc[64:96, c], rest[:, c])
                if b == NB - 1:
                    ins.then_inc(bc_ready, 1)
                else:
                    step.then_wait(dve, ins)
            dve.wait_ge(a_exp, 1)
            dve.tensor_scalar(A[:, :, :], A[:, :, :], -1.0, None, ALU.mult).then_inc(a_ready, 1)
            for h in range(HALF):
                dve.wait_ge(v_kept, NB * (h + 1))
                dve.wait_ge(e_ready, h + 1)
                dve.tensor_scalar(DT[:, h, :], Ex[:, :], 1.0, None, ALU.add).then_inc(u_ready, 1)
                dve.wait_ge(u_ready, h + 1)
                step.then_wait(dve, dve.tensor_scalar(hst[:, 0, :, :].rearrange("p a b -> p (a b)"), Ex[:, :], 1.0, 1.0, ALU.add, ALU.subtract))
                step.then_wait(dve, dve.tensor_tensor(Ex[:, :], Ex[:, :], hst[:, 0, :, :].rearrange("p a b -> p (a b)"), ALU.subtract))
                step.then_wait(dve, dve.scalar_tensor_tensor(Ex[:, :], V[:, :], 0.0, Ex[:, :], ALU.max, ALU.add))
                dve.wait_ge(ln_ready, h + 1)
                dve.tensor_tensor(DT[:, h, :], DT[:, h, :], Ex[:, :], ALU.add).then_inc(dt_ready, 1)
            dve.wait_ge(dt_ready, HALF)
            dve.wait_ge(xc_ready, HALF * NB)
            for h in range(HALF):
                for b in range(NB):
                    c = slice(b * SEQ, (b + 1) * SEQ)
                    dve.tensor_tensor(du_of(h, b), DT[:, h, c], XC[:, h, c], ALU.mult).then_inc(du_ready, 1)

            def add(b):
                for g in range(2):
                    dve.wait_ge(out_ready, NB * b + g + 1)
                    s = x[:, b * ST + 4 * g:b * ST + 4 * g + 4, :]
                    dve.tensor_tensor(s, ysum[g][:, 0:512].rearrange("p (t w) -> p t w", t=4), s, ALU.add).then_inc(y_ready, 1)

            for b in range(NB):
                c = slice(b * SEQ, (b + 1) * SEQ)
                def states(i):
                    for j in range(2):
                        n = i * 2 + j + NS * b
                        wait(dve, summed, n - 1)
                        for h in range(HALF):
                            dve.wait_ge(dA_ready, n * HALF + h + 1)
                            dve.wait_ge(dBu_ready, n * HALF + h + 1)
                            dve.tensor_tensor_scan(hst[:, j, h, :], dA[:, j, h, :], dBu[:, j, h, :], 0.0,
                                                   ALU.mult, ALU.add).then_inc(scanned, 1)
                        dve.wait_ge(c_ready, n + 1)
                        for h in range(HALF):
                            dve.wait_ge(scanned, n * HALF + h + 1)
                            dve.tensor_tensor(hst[:, j, h, :], hst[:, j, h, :], Cp[:, :], ALU.mult).then_inc(hc_ready, 1)

                states(0)
                with dve.Fori(1, NS // 2) as i:
                    states(i)
                dve.wait_ge(summed, NS * (b + 1))
                for h in range(HALF):
                    step.then_wait(dve, dve.scalar_tensor_tensor(XC[:, h, c], XC[:, h, c], Dp[:, h:h + 1], ysum[h][:, :],
                                                                 ALU.mult, ALU.add))
                    dve.tensor_tensor(XC[:, h, c], XC[:, h, c], SZ[:, h, c], ALU.mult).then_inc(ysum_ready, 1)
                add(b)
def more_layouts(a, out):
    import numpy as np

    def chunks(w):
        return w.reshape(-1, P, w.shape[-1]).transpose(1, 0, 2)

    def experts(w):
        e, r, c = w.shape
        return w.reshape(e, r // P, P, c).transpose(0, 2, 1, 3).reshape(e * P, r // P * c)

    out["f0_w1"], out["f0_w2"] = a["L0_ffn_W1"], chunks(a["L0_ffn_W2"])
    vec = np.stack([a["L0_ffn_b1"], a["L0_ffn_quantum_phases"], a["L0_ffn_quantum_weights_real"],
                    a["L0_ffn_quantum_weights_imag"]])
    out["f0_vec"] = vec.reshape(4, -1, P).transpose(2, 0, 1)
    out["f0_b2"] = a["L0_ffn_b2"].reshape(1, P)
    out["a1_qkv"], out["a1_out"] = a["L1_attn_w_qkv"].T, a["L1_attn_w_out"].T
    out["a1_bout"] = a["L1_attn_b_out"].reshape(1, P)
    out["f1_wg"], out["f1_bg"] = a["L1_ffn_Wg"], a["L1_ffn_bg"].reshape(1, NE)
    out["f1_w1"], out["f1_w2"], out["f1_b2"] = experts(a["L1_ffn_W1"]), experts(a["L1_ffn_W2"]), a["L1_ffn_b2"]
    out["f1_b1"] = experts(a["L1_ffn_b1"][:, :, None])
    kgv = ("wk", "wg", "wv")
    out["a2_wkgv"] = np.concatenate([a[f"L2_attn_{n}_w"] for n in kgv], 1)
    out["a2_bkgv"] = np.concatenate([a[f"L2_attn_{n}_b"] for n in kgv]).reshape(1, 3 * P)
    out["a2_wq"], out["a2_bq"] = a["L2_attn_wq_w"], a["L2_attn_wq_b"].reshape(P, 1)
    out["a2_wo"], out["a2_bo"] = a["L2_attn_out_w"], a["L2_attn_out_b"].reshape(1, P)
    out["f2_router"] = a["L2_ffn_router_w"].T
    for n in ("wg", "wu", "wd"):
        out["f2_" + n] = experts(a["L2_ffn_" + n])
    out["m_win"], out["m_conv"], out["m_wdt"] = a["L3_attn_W_in"], a["L3_attn_conv_w"], a["L3_attn_W_dt"]
    out["m_conv3"] = chunks(a["L3_attn_conv_w"])
    for n, k in (("convb", "conv_b"), ("bdt", "b_dt"), ("D", "D")):
        out["m_" + n] = a["L3_attn_" + k].reshape(-1, P).T
    rk = a["L3_attn_W_dt"].shape[0]
    out["m_wx_dt"], out["m_wx_bc"] = chunks(a["L3_attn_W_x"][:, :rk]), chunks(a["L3_attn_W_x"][:, rk:])
    out["m_alog"], out["m_alog3"] = a["L3_attn_A_log"], chunks(a["L3_attn_A_log"])
    out["m_wout"] = chunks(a["L3_attn_W_out"])
    out["f3_wg"] = a["L3_ffn_gate_w"].T
    out["f3_bg"], out["f3_be"] = a["L3_ffn_gate_b"].reshape(1, NE), a["L3_ffn_expert_bias"].reshape(1, NE)
    out["f3_w1"], out["f3_w2"], out["f3_b2"] = experts(a["L3_ffn_w1"]), experts(a["L3_ffn_w2"]), a["L3_ffn_b2"]
    out["f3_b1"] = experts(a["L3_ffn_b1"][:, :, None])
    i = np.arange(P)
    f = np.float32
    out["heads"] = np.concatenate([i[:, None] // 8 == i[None] // 8, i[:, None] // 8 == np.arange(16)[None]], 1).astype(f)
    out["prio"] = np.arange(NE, 0, -1).reshape(1, NE).astype(f)
    out["same16"] = (i[:, None] // 16 == i[None] // 16).astype(f)
    out["pickrow"] = (i[:, None] == 16 * np.arange(NE)[None]).astype(f)
    dig = (i[:, None] % 16) << (28 - 4 * np.arange(8))[None]
    dig[:, 0] = np.minimum(i % 16, 7) << 28
    out["digits"] = dig.astype(np.int32)
    out["sel32"] = (np.arange(96)[:, None] % 32 == np.arange(32)[None]).astype(f)


def program(nc, d, out, upto=99, start=0):
    with ExitStack() as ctx:
        sb, pb, sem = scope(nc, ctx, "main")
        x = sb("x", [P, TT, P])
        xnT = sb("xnT", [P, TOK])
        ident = sb("ident", [P, P])
        gin = sb("gin", [P, 1])
        pick = sb("pick", [P, TT, NE])
        first_in, out_done = sem("first_in"), sem("out_done")
        with nc.Block(no_gpsimd_drain=True) as block:
            @block.sync
            def _(sp):
                sp.dma_start(ident[:, :], d["eye"]).then_inc(first_in, 16)
                sp.dma_start(gin[:, :], d["gin"]).then_inc(first_in, 16)
                for t in range(4):
                    sp.dma_start(x[:, 4 * t:4 * t + 4, :], d["x"][:, 4 * t:4 * t + 4, :]).then_inc(first_in, 16)
                sp.wait_ge(first_in, 6 * 16)

        def layer(n, name, f, **k):
            if start <= n < upto:
                prenorm(nc, "n" + name, x, xnT, ident, **k)
                f()

        layer(0, "0", lambda: l0_attention(nc, d, x, xnT, ident, None), rounds=2, gamma=gin[:, :])
        layer(1, "1", lambda: l0_ffn(nc, d, x, xnT))
        layer(2, "2", lambda: l1_attention(nc, d, x, xnT, ident))

        def l1_ffn():
            gate_top1(nc, "g1", d, ("f1_wg", ("f1_bg",), "f1_b2"), x, xnT, ident, pick)
            experts_dense(nc, "e1", "gelu", d, (("f1_w1",), "f1_b1", "f1_w2"), x, xnT, pick)

        def l2_ffn():
            route_top2(nc, d, x, xnT, ident, pick)
            experts_dense(nc, "e2", "silu", d, (("f2_wg", "f2_wu"), None, "f2_wd"), x, xnT, pick)

        def l3_ffn():
            gate_top1(nc, "g3", d, ("f3_wg", ("f3_bg", "f3_be"), "f3_b2"), x, xnT, ident, pick)
            experts_dense(nc, "e3", "relu", d, (("f3_w1",), "f3_b1", "f3_w2"), x, xnT, pick)

        layer(3, "3", l1_ffn)
        layer(4, "4", lambda: l2_attention(nc, d, x, xnT, ident))
        layer(5, "5", l2_ffn)
        layer(6, "6", lambda: l3_mixer(nc, d, x, xnT, ident))
        layer(7, "7", l3_ffn)
        with nc.Block(no_gpsimd_drain=True) as block:
            @block.sync
            def _(sp):
                for t in range(4):
                    sp.dma_start(out[:, 4 * t:4 * t + 4, :], x[:, 4 * t:4 * t + 4, :]).then_inc(out_done, 16)
                sp.wait_ge(out_done, 4 * 16)


def layouts(inputs):
    import numpy as np

    a = {k: np.ascontiguousarray(np.asarray(v)) for k, v in inputs.items()}
    out = {}
    out["x"] = a["L0_attn_x"].reshape(TT, P, P).transpose(1, 0, 2)
    wq, wk, wv = (a["L0_attn_" + n].reshape(P, PAIRS, P) for n in ("Wq", "Wk", "Wv"))
    out["wqkv"] = np.stack([wq, wk, wv, wv.transpose(2, 1, 0)], 2).transpose(1, 0, 2, 3).reshape(PAIRS * P, 4 * P)
    out["wo"] = a["L0_attn_Wo"].reshape(PAIRS, P, P).transpose(1, 0, 2)
    out["gnn_w"], out["gnn_b"] = a["L0_attn_gnn_w"], a["L0_attn_gnn_b"]
    out["lin_w"], out["lin_b"] = a["L0_attn_lin_w"], a["L0_attn_lin_b"].reshape(DH, 1)
    out["gin"], out["gout"] = a["L0_attn_gamma_in"].reshape(P, 1), a["L0_attn_gamma_out"].reshape(1, P)
    more_layouts(a, out)
    out["eye"] = np.eye(P, dtype=np.float32)
    out["caps"] = np.triu(np.full((P, P), 3e38, np.float32))
    out["cmask"] = np.triu(np.full((P, P), -1e38, np.float32), 1)
    return {k: np.ascontiguousarray(v) for k, v in out.items()}


def kernel(**inputs):
    import numpy as np
    import concourse.bacc as bacc
    from concourse.bass_utils import run_bass_kernel_spmd

    arrays = layouts(inputs)
    nc = bacc.Bacc("TRN2", target_bir_lowering=False, num_devices=1)
    d = {n: nc.dram_tensor(f"in_{n}", v.shape, mybir.dt.from_np(v.dtype), kind="ExternalInput").ap()
         for n, v in arrays.items()}
    out = nc.dram_tensor("out_x", (P, TT, P), F32, kind="ExternalOutput").ap()
    program(nc, d, out)
    r = run_bass_kernel_spmd(nc, [{f"in_{n}": v for n, v in arrays.items()}], core_ids=[0])
    got = np.asarray(r.results[0]["out_x"])
    return got.transpose(1, 0, 2).reshape(NB, SEQ, P)
```

```python
from contextlib import ExitStack

import concourse.bass as bass
from concourse import mybir

ALU = mybir.AluOpType
ACT = mybir.ActivationFunctionType
F32 = mybir.dt.float32
F32R = mybir.dt.float32r
BF16 = mybir.dt.bfloat16
I32 = mybir.dt.int32
AX_X = mybir.AxisListType.X

P = 128
NB = 2
SEQ = 1024
TOK = NB * SEQ
TT = TOK // P
ST = SEQ // P
EPS = 1e-5


class Count:

    def __init__(self, sem, start=0):
        self.sem = sem
        self.n = start

    def mark(self, ins, by=1):
        ins.then_inc(self.sem, by)
        self.n = self.n + by

    def then_wait(self, eng, ins):
        self.mark(ins)
        eng.wait_ge(self.sem, self.n)


def wait(eng, sem, value):
    if not (isinstance(value, int) and value <= 0):
        eng.wait_ge(sem, value)


def spread(ap, shape):
    return ap.unsqueeze(len(ap.shape)).broadcast_to(shape)


def ln_stats(dve, step, work, src, tiles, waits=None):
    st, mv, ve = work["stats"], work["mv"], work["ve"]
    for t in range(tiles):
        if waits:
            waits(t)
        step.mark(dve.bn_stats(st[:, t, :], src[:, t, :]))
    dve.wait_ge(step.sem, step.n)
    for t in range(tiles):
        step.mark(dve.bn_aggr(mv[:, t, :], st[:, t, :]))
    dve.wait_ge(step.sem, step.n)
    return dve.tensor_scalar(ve[:, 0:tiles], mv[:, 0:tiles, 1], EPS, None, ALU.add)


def ln_rstd(dve, step, work, tiles):
    ve, sd, y, z = work["ve"], work["sd"], work["rstd"], work["newton"]
    step.then_wait(dve, dve.reciprocal(y[:, 0:tiles], sd[:, 0:tiles]))
    step.then_wait(dve, dve.tensor_tensor(z[:, 0:tiles], y[:, 0:tiles], y[:, 0:tiles], ALU.mult))
    step.then_wait(dve, dve.tensor_tensor(z[:, 0:tiles], z[:, 0:tiles], ve[:, 0:tiles], ALU.mult))
    step.then_wait(dve, dve.tensor_scalar(z[:, 0:tiles], z[:, 0:tiles], -0.5, 1.5, ALU.mult, ALU.add))
    step.then_wait(dve, dve.tensor_tensor(y[:, 0:tiles], y[:, 0:tiles], z[:, 0:tiles], ALU.mult))


def ln_work(sb, name, tiles):
    return {
        "stats": sb(name + "_stats", [P, tiles, 6], F32), "mv": sb(name + "_mv", [P, tiles, 2], F32),
        "ve": sb(name + "_ve", [P, tiles], F32), "sd": sb(name + "_sd", [P, tiles], F32),
        "rstd": sb(name + "_rstd", [P, tiles], F32), "newton": sb(name + "_newton", [P, tiles], F32),
    }


def scope(nc, ctx, name):
    used = []

    def clear():
        nc.clear_and_free_semaphores(used)
        nc.all_engine_barrier()

    ctx.callback(clear)

    def sb(n, shape, dt=F32):
        return ctx.enter_context(nc.sbuf_tensor(f"{name}_{n}", shape, dt))

    def pb(n, shape, dt=F32):
        return ctx.enter_context(nc.psum_tensor(f"{name}_{n}", shape, dt))

    def sem(n):
        used.append(nc.alloc_semaphore(f"{name}_{n}"))
        return used[-1]

    return sb, pb, sem


def prenorm(nc, name, x, xnT, ident, rounds=1, gamma=None, xn_keep=None):
    with ExitStack() as ctx:
        sb, pb, sem = scope(nc, ctx, name)
        xn = xn_keep if xn_keep is not None else sb("xn", [P, TT, P])
        work = ln_work(sb, name, TT)
        bank = [pb(f"turned{n}", [P, 4, P]) for n in range(4)]
        step_done, ve_ready, root_ready = sem("step"), sem("ve_ready"), sem("root_ready")
        xn_ready, turned_ready, kept = sem("xn_ready"), sem("turned_ready"), sem("kept")
        block = ctx.enter_context(nc.Block(no_gpsimd_drain=True))

        @block.vector
        def _(dve):
            step = Count(step_done)
            src = x
            for r in range(rounds):
                ln_stats(dve, step, work, src, TT).then_inc(ve_ready, 1)
                dve.wait_ge(root_ready, r + 1)
                ln_rstd(dve, step, work, TT)
                for t in range(TT):
                    ins = dve.tensor_scalar(xn[:, t, :], src[:, t, :], work["mv"][:, t, 0:1],
                                            work["rstd"][:, t:t + 1], ALU.subtract, ALU.mult)
                    if r == rounds - 1:
                        ins.then_inc(xn_ready, 1)
                    else:
                        step.mark(ins)
                src = xn
                dve.wait_ge(step.sem, step.n)

        @block.scalar
        def _(act):
            for r in range(rounds):
                act.wait_ge(ve_ready, r + 1)
                act.activation(work["sd"][:, :], work["ve"][:, :], ACT.Sqrt).then_inc(root_ready, 1)
            for g in range(4):
                act.wait_ge(turned_ready, g + 1)
                act.activation(xnT[:, g * 512:(g + 1) * 512], bank[g][:, :, :].rearrange("p a b -> p (a b)"),
                               ACT.Copy, scale=1.0 if gamma is None else gamma).then_inc(kept, 1)

        @block.tensor
        def _(pe):
            for g in range(4):
                for j in range(4):
                    pe.wait_ge(xn_ready, 4 * g + j + 1)
                    mm = pe.transpose(bank[g][:, j, :], xn[:, 4 * g + j, :], ident[:, :])
                mm.then_inc(turned_ready, 1)
HEADS, DH = 16, 64
PAIRS = HEADS // 2
SCALE0 = DH ** -0.5


class Passed:

    n = 0


def l0_attention(nc, d, x, xnT, ident, const):
    with ExitStack() as ctx:
        sb, pb, sem = scope(nc, ctx, "l0a")
        wp = sb("wp", [P, 3 * P])
        gnn = [sb(f"gnn{l}", [P, P]) for l in range(2)]
        gnnb = [sb(f"gnnb{l}", [P, 1]) for l in range(2)]
        lin = sb("lin", [P, P])
        linb = sb("linb", [P, 1])
        mask = sb("mask", [P, P], BF16)
        identb = sb("identb", [P, P], BF16)
        identr = sb("identr", [P, P], F32R)
        maskf = sb("maskf", [P, P])
        Q1 = sb("Q1", [P, 2, SEQ], F32R)
        K1 = sb("K1", [P, 2, SEQ], F32R)
        Q2 = sb("Q2", [DH + 1, 2, SEQ], F32R)
        K2 = sb("K2", [DH + 1, 2, SEQ], F32R)
        E = sb("E", [P, 2, 36 * P])
        VT = sb("VT", [P, SEQ])
        VN = sb("VN", [P, SEQ])
        VH = sb("VH", [P, ST * 2, DH + 1])
        F1 = sb("F1", [P, ST * 2, DH])
        F1T = sb("F1T", [P, SEQ])
        S = sb("S", [P, SEQ])
        ZT = sb("ZT", [P, SEQ])
        Z = sb("Z", [P, ST * 2, DH])
        T = sb("T", [P, ST * 2, DH])
        AO = sb("AO", [P, ST * 2, DH])
        OT = sb("OT", [P, PAIRS, SEQ])
        wo = sb("wo", [P, PAIRS, P])
        go = sb("go", [P, P])
        eii = sb("eii", [P, ST, 2])
        mx = sb("mx", [P, 2, ST], F32R)
        small = sb("small", [P, 4, ST * 2])
        scrap = sb("scrap", [P, P])
        Y = sb("Y", [P, ST, P])
        work = ln_work(sb, "l0o", ST)
        ring = [pb(f"ring{n}", [P, SEQ]) for n in range(2)]
        agg = [pb(f"agg{n}", [P, 512]) for n in range(2)]
        turn = pb("turn", [P, 4 * P])
        prod = pb("prod", [P, 4 * P])
        agg1 = [turn, prod, agg[0], agg[1]]
        W65 = DH + 1

        const_in, w_in, pool_step = sem("const_in"), sem("w_in"), sem("pool_step")
        cast_done, q_ready, k_ready, v_ready = sem("cast_done"), sem("q_ready"), sem("k_ready"), sem("v_ready")
        q_hi, k_hi, q_lo, k_lo, dup_in = sem("q_hi"), sem("k_hi"), sem("q_lo"), sem("k_lo"), sem("dup_in")
        vn_kept, vt_kept, vrow_ready, v_kept = sem("vn_kept"), sem("vt_kept"), sem("vrow_ready"), sem("v_kept")
        rowmax_ready, max_done = sem("rowmax_ready"), sem("max_done")
        mrow_ready, mrow_kept = sem("mrow_ready"), sem("mrow_kept")
        score_ready, exp_done, diag_done = sem("score_ready"), sem("exp_done"), sem("diag_done")
        agg1_ready, post1_done = sem("agg1_ready"), sem("post1_done")
        agg2_ready, post2_done, own_ready = sem("agg2_ready"), sem("post2_done"), sem("own_ready")
        turned, turn_kept = sem("turned"), sem("turn_kept")
        prod_ready, sum_done, gelu_done = sem("prod_ready"), sem("sum_done"), sem("gelu_done")
        ot_ready, ot_kept = sem("ot_ready"), sem("ot_kept")
        dve_step, dve_out, y_ready, y_kept = sem("dve_step"), sem("dve_out"), sem("y_ready"), sem("y_kept")
        ve_ready, root_ready = sem("ve_ready"), sem("root_ready")

        ecol = [sum(SEQ - P * k for k in range(jt)) for jt in range(ST)]

        def e_tile(h, jt, it):
            at = ecol[jt] + (it - jt) * P
            return E[:, h, at:at + P]

        def half(t, c):
            return t[:, c * 512:(c + 1) * 512]

        block = ctx.enter_context(nc.Block(no_gpsimd_drain=True))

        def for_units(eng, first, body, last):
            first()
            for b in range(NB):
                with eng.Fori(0, PAIRS - 1) as i:
                    body(i + b * PAIRS if b else i, b, i, b)
                if b < NB - 1:
                    body(PAIRS * (b + 1) - 1, b, PAIRS - 1, b + 1)
                else:
                    body(PAIRS * (b + 1) - 1, b, PAIRS - 1, None)
                last(b)

        NCONST = 16 * (3 + 2 * 6)
        NDUP = 16 * 4

        @block.sync
        def _(sp):
            for dst, src in ((maskf, d["cmask"]), (wo, d["wo"]), (go, d["gout"].partition_broadcast(P))):
                sp.dma_start(dst[:], src).then_inc(const_in, 16)
            sp.wait_ge(pool_step, 5)
            for h in range(2):
                r = slice(h * DH, (h + 1) * DH)
                for l in range(2):
                    sp.dma_start(gnn[l][r, r], d["gnn_w"][l]).then_inc(const_in, 16)
                    sp.dma_start(gnnb[l][r, :], d["gnn_bc"][l]).then_inc(const_in, 16)
                sp.dma_start(lin[r, r], d["lin_w"]).then_inc(const_in, 16)
                sp.dma_start(linb[r, :], d["lin_b"]).then_inc(const_in, 16)

            def duplicates(u):
                sp.wait_ge(k_hi, u * 2 + 2)
                sp.wait_ge(q_hi, u * 2 + 2)
                for h in range(2):
                    sp.dma_start(K1[DH:P, h, :].bitcast(F32), K1[0:DH, h, :].bitcast(F32)).then_inc(dup_in, 16)
                    sp.dma_start(Q2[0:DH, h, :].bitcast(F32), Q1[0:DH, h, :].bitcast(F32)).then_inc(dup_in, 16)

            def weights(rows, u):
                sp.wait_ge(v_ready, u)
                sp.dma_start(wp[:, :], d["wqkv"][rows, :]).then_inc(w_in, 16)

            sp.dma_start(wp[:, :], d["wqkv"][0:P, :]).then_inc(w_in, 16)
            duplicates(0)
            for b in range(NB):
                with sp.Fori(0, PAIRS - 1) as i:
                    g = i + b * PAIRS if b else i
                    weights(bass.ds((i + 1) * P, P), g + 1)
                    duplicates(g + 1)
                if b < NB - 1:
                    weights(slice(0, P), PAIRS * (b + 1))
                    duplicates(PAIRS * (b + 1))

        @block.gpsimd
        def _(pool):
            for t in gnn + [lin]:
                pool.memset(t[:, :], 0.0).then_inc(pool_step, 1)
            pool.memset(VH[:, :, DH:W65], 1.0).then_inc(pool_step, 1)
            pool.wait_ge(pool_step, 4)
            pool.memset(S[DH:W65, :], 1.0).then_inc(pool_step, 1)
            pool.wait_ge(pool_step, 5)
            pool.wait_ge(const_in, NCONST)

            def body(g, b, pair, nb):
                for q in range(4):
                    if q % 2 == 0:
                        pool.wait_ge(turn_kept, g * 6 + (3 + q // 2))
                    pool.tensor_tensor(T[:, 4 * q:4 * q + 4, :], F1[:, 4 * q:4 * q + 4, :],
                                       spread(small[:, 3, 4 * q:4 * q + 4], [P, 4, DH]), ALU.mult).then_inc(own_ready, 1)

            for_units(pool, lambda: None, body, lambda b: None)

        @block.scalar
        def _(act):
            def keep_hi(src, dst, ready, kept, scale, u):
                act.wait_ge(ready, u + 1)
                for h in range(2):
                    act.activation(dst[0:DH, h, :], src[h * DH:(h + 1) * DH, :], ACT.Copy, scale=scale).then_inc(kept, 1)

            def keep_mrows(u):
                for h in range(2):
                    act.wait_ge(mrow_ready, u * 2 + (h + 1))
                    act.activation(Q2[DH:W65, h, :], ring[h][0:1, :], ACT.Copy, scale=-1.0).then_inc(mrow_kept, 1)

            def keep_turned(g, k, dst):
                act.wait_ge(turned, g * 6 + (k + 1))
                act.activation(dst, turn[:, :], ACT.Copy).then_inc(turn_kept, 1)

            def rows4(t, c):
                return t[:, 8 * c:8 * c + 8, :].rearrange("p a b -> p (a b)")

            def first():
                keep_hi(ring[0], Q1, q_ready, q_hi, SCALE0, 0)
                keep_hi(ring[1], K1, k_ready, k_hi, 1.0, 0)
                keep_mrows(0)

            def body(g, b, pair, nb):
                for h in range(2):
                    for jt in range(ST):
                        n = ST * h + jt
                        act.wait_ge(score_ready, g * 16 + (n + 1))
                        w = SEQ - P * jt
                        act.activation(E[:, h, ecol[jt]:ecol[jt] + w], ring[n % 2][:, 0:w], ACT.Exp).then_inc(exp_done, 1)
                if nb is not None:
                    keep_hi(ring[0], Q1, q_ready, q_hi, SCALE0, g + 1)
                    keep_hi(ring[1], K1, k_ready, k_hi, 1.0, g + 1)
                keep_turned(g, 0, half(ZT, 0))
                keep_turned(g, 1, half(ZT, 1))
                for c in range(2):
                    act.wait_ge(sum_done, g * 4 + (c + 1))
                    act.activation(half(F1T, c), half(S, c), ACT.Gelu, bias=gnnb[0][:, :]).then_inc(gelu_done, 1)
                keep_turned(g, 2, rows4(F1, 0))
                keep_turned(g, 3, rows4(F1, 1))
                keep_turned(g, 4, half(ZT, 0))
                keep_turned(g, 5, half(ZT, 1))
                if nb is not None:
                    keep_mrows(g + 1)
                for c in range(2):
                    act.wait_ge(sum_done, g * 4 + (c + 3))
                    act.activation(half(S, c), half(S, c), ACT.Gelu, bias=gnnb[1][:, :]).then_inc(gelu_done, 1)

            def last(b):
                act.wait_ge(ve_ready, b + 1)
                act.activation(work["sd"][:, :], work["ve"][:, :], ACT.Sqrt).then_inc(root_ready, 1)

            for_units(act, first, body, last)

        @block.tensor
        def _(pe):
            pe.wait_ge(const_in, NCONST)
            pe.wait_ge(cast_done, 3)

            def project(dst, part, b, ready):
                for c in range(2):
                    mm = pe.matmul(half(dst, c), wp[:, part * P:(part + 1) * P],
                                   xnT[:, b * SEQ + c * 512:b * SEQ + (c + 1) * 512], start=True, stop=True)
                mm.then_inc(ready, 1)

            def v_rows(u):
                pe.wait_ge(vn_kept, u + 1)
                pe.wait_ge(k_lo, u * 2 + 2)
                for t in range(ST):
                    mm = pe.transpose(ring[1][:, t * P:(t + 1) * P], VN[:, t * P:(t + 1) * P], ident[:, :])
                mm.then_inc(vrow_ready, 1)

            def row_scores(u, n):
                it, h = n // 2, n % 2
                if n < 2:
                    pe.wait_ge(v_kept, u + 1)
                else:
                    pe.wait_ge(max_done, u * 16 + (n - 1))
                w = (it + 1) * P
                for c0 in range(0, w, 512):
                    c1 = min(w, c0 + 512)
                    pe.matmul(ring[n % 2][:, c0:c1], Q1[0:DH, h, it * P:(it + 1) * P], K1[0:DH, h, c0:c1],
                              start=True, stop=c1 < w)
                mm = pe.matmul(ring[n % 2][:, it * P:w], identb[:, :], mask[:, :], start=False, stop=True)
                mm.then_inc(rowmax_ready, 1)

            def max_rows(u):
                pe.wait_ge(max_done, u * 16 + 16)
                for h in range(2):
                    for it in range(ST):
                        mm = pe.matmul(ring[h][0:1, it * P:(it + 1) * P], mx[:, h, it:it + 1], identr[:, :],
                                       start=True, stop=True)
                    mm.then_inc(mrow_ready, 1)

            def first():
                pe.wait_ge(w_in, 16)
                project(ring[0], 0, 0, q_ready)
                project(ring[1], 1, 0, k_ready)
                pe.wait_ge(q_lo, 2)
                project(ring[0], 2, 0, v_ready)
                v_rows(0)
                for n in range(2 * ST):
                    row_scores(0, n)
                max_rows(0)
                score(0, 0)
                score(0, 1)

            def turn_rows(g, k, src, c):
                if k:
                    pe.wait_ge(turn_kept, g * 6 + k)
                for t in range(4):
                    mm = pe.transpose(turn[:, t * P:(t + 1) * P],
                                      src[:, 8 * c + 2 * t:8 * c + 2 * t + 2, :].rearrange("p a b -> p (a b)"), ident[:, :])
                mm.then_inc(turned, 1)

            def layer_product(g, l, c):
                pe.wait_ge(turn_kept, g * 6 + (4 * l + c + 1))
                if l or c:
                    pe.wait_ge(sum_done, g * 4 + (2 * l + c))
                pe.matmul(prod[:, :], gnn[l][:, :], half(ZT, c), start=True, stop=True).then_inc(prod_ready, 1)

            def score(u, n):
                h, jt = n // ST, n % ST
                if n < 2:
                    pe.wait_ge(mrow_kept, u * 2 + (n + 1))
                else:
                    pe.wait_ge(exp_done, u * 16 + (n - 1))
                if n == 0:
                    pe.wait_ge(mrow_kept, u * 2 + 2)
                    pe.wait_ge(dup_in, u * NDUP + NDUP)
                w = SEQ - P * jt
                keys = slice(jt * P, (jt + 1) * P)
                for c0 in range(0, w, 512):
                    c1 = min(w, c0 + 512)
                    out, at = ring[n % 2][:, c0:c1], slice(P * jt + c0, P * jt + c1)
                    pe.matmul(out, K1[:, h, keys], Q1[:, h, at], start=True, stop=False, skip_group_check=True)
                    mm = pe.matmul(out, K2[:, h, keys], Q2[:, h, at], start=False, stop=c0 > 0, skip_group_check=True)
                    if c0 == 0:
                        mm = pe.matmul(ring[n % 2][:, 0:P], mask[:, :], identb[:, :], start=False, stop=True,
                                       skip_group_check=True)
                mm.then_inc(score_ready, 1)

            def aggregate(out, it, h, feats, width, between=None):
                at = (2 * (it % 2) + h) * width
                for jt in range(it + 1):
                    mm = pe.matmul(out[:, at:at + width], e_tile(h, jt, it), feats[:, 2 * jt + h, :],
                                   start=(jt == 0), stop=(jt == it))
                    if between and (it, h, jt) != (it | 1, 1, it):
                        between()
                return mm

            def body(g, b, pair, nb):
                for n in range(2, 2 * ST):
                    score(g, n)
                    it = n - ST - 2
                    if it == 0:
                        if b:
                            pe.wait_ge(y_kept, ST * b)
                        pe.wait_ge(diag_done, g * 16 + 1)
                    if it >= 0:
                        pe.wait_ge(exp_done, g * 16 + (it + 1))
                        aggregate(agg1[it // 2], it, 0, VH, W65)
                if nb is not None:
                    pe.wait_ge(w_in, g * 16 + 32)
                    pe.wait_ge(exp_done, g * 16 + 15)
                    project(ring[0], 0, nb, q_ready)
                pe.wait_ge(exp_done, g * 16 + 16)
                if nb is not None:
                    project(ring[1], 1, nb, k_ready)
                for it in range(ST - 2, ST):
                    aggregate(agg1[it // 2], it, 0, VH, W65)
                for it in range(ST):
                    mm = aggregate(agg1[it // 2], it, 1, VH, W65)
                    if it % 2:
                        mm.then_inc(agg1_ready, 1)
                    if it == 5 and nb is not None:
                        pe.wait_ge(q_lo, g * 2 + 4)
                        project(ring[0], 2, nb, v_ready)
                pe.wait_ge(post1_done, g * 4 + 2)
                turn_rows(g, 0, Z, 0)
                if nb is not None:
                    v_rows(g + 1)
                layer_product(g, 0, 0)
                pe.wait_ge(post1_done, g * 4 + 4)
                turn_rows(g, 1, Z, 1)
                if nb is not None:
                    row_scores(g + 1, 0)
                    row_scores(g + 1, 1)
                layer_product(g, 0, 1)
                for c in range(2):
                    if nb is not None:
                        row_scores(g + 1, 2 * c + 2)
                        row_scores(g + 1, 2 * c + 3)
                    pe.wait_ge(gelu_done, g * 4 + (c + 1))
                    pe.wait_ge(turn_kept, g * 6 + (2 + c))
                    for t in range(4):
                        mm = pe.transpose(turn[:, t * P:(t + 1) * P], F1T[:, (4 * c + t) * P:(4 * c + t + 1) * P],
                                          ident[:, :])
                    mm.then_inc(turned, 1)
                if nb is not None:
                    row_scores(g + 1, 6)
                    row_scores(g + 1, 7)
                done = Passed()

                def between():
                    done.n += 1
                    if nb is not None and done.n % 8 == 0 and done.n <= 64:
                        row_scores(g + 1, 7 + done.n // 8)

                for it in range(ST):
                    q = it // 2
                    if it in (4, 6):
                        pe.wait_ge(post2_done, g * 4 + (q - 1))
                    if it in (0, 4):
                        pe.wait_ge(turn_kept, g * 6 + (3 + it // 4))
                    for h in range(2):
                        mm = aggregate(agg[q % 2], it, h, F1, DH, between)
                    if it % 2:
                        mm.then_inc(agg2_ready, 1)
                        done.n += 1
                    if it == 5:
                        pe.wait_ge(post2_done, g * 4 + 2)
                        turn_rows(g, 4, Z, 0)
                layer_product(g, 1, 0)
                pe.wait_ge(post2_done, g * 4 + 4)
                turn_rows(g, 5, Z, 1)
                if nb is not None:
                    max_rows(g + 1)
                layer_product(g, 1, 1)
                if nb is not None:
                    score(g + 1, 0)
                    score(g + 1, 1)
                mix(g, 0)
                mix(g, 1)

            def mix(g, c):
                if c == 0:
                    pe.wait_ge(sum_done, g * 4 + 4)
                else:
                    pe.wait_ge(ot_kept, g * 2 + 1)
                for t in range(4):
                    pe.matmul(prod[:, t * P:(t + 1) * P],
                              AO[:, 8 * c + 2 * t:8 * c + 2 * t + 2, :].rearrange("p a b -> p (a b)"), ident[:, :],
                              start=(t == 0), stop=False, skip_group_check=True)
                pe.wait_ge(gelu_done, g * 4 + (3 + c))
                mm = pe.matmul(prod[:, :], lin[:, :], half(S, c), start=False, stop=True, skip_group_check=True)
                mm.then_inc(ot_ready, 1)

            def last(b):
                pe.wait_ge(ot_kept, 2 * PAIRS * (b + 1))
                for it in range(ST):
                    if it >= 2:
                        pe.wait_ge(y_kept, ST * b + it - 1)
                    for q in range(PAIRS):
                        mm = pe.matmul(agg[it % 2][:, 0:P], OT[:, q, it * P:(it + 1) * P], wo[:, q, :],
                                       start=(q == 0), stop=(q == PAIRS - 1))
                    mm.then_inc(y_ready, 1)

            for_units(pe, first, body, last)

        LAST = 2 * ST + 5 + ST + 2
        UNIT = 7 * 4

        @block.vector
        def _(dve):
            step = Count(dve_step)
            dve.wait_ge(const_in, NCONST)
            dve.wait_ge(pool_step, 5)
            dve.tensor_copy(mask[:, :], maskf[:, :]).then_inc(cast_done, 1)
            dve.tensor_copy(identb[:, :], ident[:, :]).then_inc(cast_done, 1)
            dve.tensor_copy(identr[:, :], ident[:, :]).then_inc(cast_done, 1)
            for h in range(2):
                dve.tensor_copy(K2[DH:W65, h, :], S[DH:W65, :])

            def keep_lo(u):
                for h in range(2):
                    dve.wait_ge(q_hi, u * 2 + (h + 1))
                    dve.scalar_tensor_tensor(Q1[DH:P, h, :], ring[0][h * DH:(h + 1) * DH, :], SCALE0, Q1[0:DH, h, :],
                                             ALU.mult, ALU.subtract).then_inc(q_lo, 1)
                for h in range(2):
                    dve.wait_ge(k_hi, u * 2 + (h + 1))
                    dve.tensor_tensor(K2[0:DH, h, :], ring[1][h * DH:(h + 1) * DH, :], K1[0:DH, h, :],
                                      ALU.subtract).then_inc(k_lo, 1)

            def keep_v(u):
                dve.wait_ge(v_ready, u + 1)
                dve.tensor_copy(VN[:, :], ring[0][:, :]).then_inc(vn_kept, 1)

            def keep_vt(u):
                dve.wait_ge(vn_kept, u + 1)
                dve.tensor_copy(VT[:, :], VN[:, :]).then_inc(vt_kept, 1)

            def keep_v_rows(u):
                dve.wait_ge(vrow_ready, u + 1)
                dve.tensor_copy(VH[:, :, 0:DH], ring[1][:, :].rearrange("p (a w) -> p a w", w=DH)).then_inc(v_kept, 1)

            def row_max(u, n):
                it, h = n // 2, n % 2
                dve.wait_ge(rowmax_ready, u * 16 + (n + 1))
                dve.tensor_reduce(mx[:, h, it:it + 1], ring[n % 2][:, 0:(it + 1) * P], AX_X, ALU.max).then_inc(max_done, 1)

            def first():
                keep_lo(0)
                keep_v(0)
                keep_vt(0)
                keep_v_rows(0)
                for n in range(2 * ST):
                    row_max(0, n)

            def add_features(g, l, c, feats):
                dve.wait_ge(prod_ready, g * 4 + (2 * l + c + 1))
                dve.tensor_tensor(half(S, c), prod[:, :], half(feats, c), ALU.add).then_inc(sum_done, 1)

            def z_pair(q, bank, width, done):
                for k in range(4):
                    ins = dve.scalar_tensor_tensor(Z[:, 4 * q + k, :], bank[:, k * width:k * width + DH],
                                                   small[:, 0, 4 * q + k:4 * q + k + 1], T[:, 4 * q + k, :], ALU.mult, ALU.add)
                ins.then_inc(done, 1)

            def body(g, b, pair, nb):
                step = Count(dve_step, g * UNIT)
                for h in range(2):
                    for it in range(ST):
                        n = ST * h + it
                        dve.wait_ge(exp_done, g * 16 + (n + 1))
                        dve.scalar_tensor_tensor(scrap[:, :], e_tile(h, it, it), 1.0, ident[:, :], ALU.mult, ALU.mult,
                                                 accum_out=eii[:, it, h:h + 1]).then_inc(diag_done, 1)
                        dve.wait_ge(diag_done, g * 16 + (n + 1))
                if nb is not None:
                    keep_lo(g + 1)
                dve.wait_ge(vt_kept, g + 1)
                steps = 0
                for q in range(4):
                    dve.wait_ge(agg1_ready, g * 4 + (q + 1))
                    a = agg1[q][:, 0:4 * W65].rearrange("p (a w) -> p a w", w=W65)
                    four = slice(4 * q, 4 * q + 4)
                    s, e = a[:, :, DH], eii[:, 2 * q:2 * q + 2, :].rearrange("p a b -> p (a b)")
                    step.mark(dve.tensor_copy(small[:, 1, four], s))
                    step.then_wait(dve, dve.tensor_tensor(small[:, 2, four], s, e, ALU.subtract))
                    step.then_wait(dve, dve.tensor_tensor(small[:, 0, four], small[:, 1, four], small[:, 2, four], ALU.add))
                    step.then_wait(dve, dve.reciprocal(small[:, 0:2, four], small[:, 0:2, four]))
                    step.then_wait(dve, dve.tensor_tensor(small[:, 3, four], small[:, 2, four], small[:, 0, four], ALU.mult))
                    step.mark(dve.tensor_tensor(T[:, four, :], VH[:, four, 0:DH], spread(small[:, 3, four], [P, 4, DH]),
                                                ALU.mult))
                    step.mark(dve.tensor_tensor(AO[:, four, :], a[:, :, 0:DH], spread(small[:, 1, four], [P, 4, DH]),
                                                ALU.mult))
                    dve.wait_ge(step.sem, step.n)
                    steps += 7
                    z_pair(q, agg1[q], W65, post1_done)
                    if q == 2 and nb is not None:
                        keep_v(g + 1)
                assert steps == UNIT
                def row_maxima(*heads):
                    if nb is not None:
                        for n in heads:
                            row_max(g + 1, n)

                add_features(g, 0, 0, VT)
                if nb is not None:
                    keep_v_rows(g + 1)
                row_maxima(0, 1)
                add_features(g, 0, 1, VT)
                if nb is not None:
                    dve.wait_ge(sum_done, g * 4 + 2)
                    keep_vt(g + 1)
                row_maxima(2, 3, 4, 5, 6, 7)
                for q in range(4):
                    dve.wait_ge(agg2_ready, g * 4 + (q + 1))
                    dve.wait_ge(own_ready, g * 4 + (q + 1))
                    z_pair(q, agg[q % 2], DH, post2_done)
                    row_maxima(*((8, 9), (10, 11, 12), (13, 14, 15), ())[q])
                add_features(g, 1, 0, F1T)
                add_features(g, 1, 1, F1T)
                for c in range(2):
                    dve.wait_ge(ot_ready, g * 2 + (c + 1))
                    flat = OT[:, :, :].rearrange("p a b -> p (a b)")
                    dst = flat[:, bass.ds(pair * SEQ + c * 512, 512)]
                    dve.tensor_scalar(dst, prod[:, :], linb[:, :], None, ALU.add).then_inc(ot_kept, 1)

            def last(b):
                step = Count(dve_out)
                step.n = b * LAST
                start = step.n
                for it in range(ST):
                    dve.wait_ge(y_ready, ST * b + it + 1)
                    dve.tensor_copy(Y[:, it, :], agg[it % 2][:, 0:P]).then_inc(y_kept, 1)
                dve.wait_ge(y_kept, ST * (b + 1))
                ln_stats(dve, step, work, Y, ST).then_inc(ve_ready, 1)
                dve.wait_ge(root_ready, b + 1)
                ln_rstd(dve, step, work, ST)
                for it in range(ST):
                    step.mark(dve.tensor_scalar(Y[:, it, :], Y[:, it, :], work["mv"][:, it, 0:1],
                                                  work["rstd"][:, it:it + 1], ALU.subtract, ALU.mult))
                dve.wait_ge(step.sem, step.n)
                gam = go[:, :].unsqueeze(1).broadcast_to([P, ST, P])
                step.then_wait(dve, dve.tensor_tensor(Y[:, :, :], Y[:, :, :], gam, ALU.mult))
                xb = x[:, b * ST:(b + 1) * ST, :]
                step.then_wait(dve, dve.tensor_tensor(xb, xb, Y[:, :, :], ALU.add))
                assert step.n - start == LAST

            first()
            for b in range(NB):
                with dve.Fori(0, PAIRS - 1) as i:
                    body(i + b * PAIRS if b else i, b, i, b)
                body(PAIRS * (b + 1) - 1, b, PAIRS - 1, b + 1 if b < NB - 1 else None)
                last(b)
TWO_PI_PARTS = (6.28125, 0.0019350051879882812, 3.0199159819e-07)
ROUND = 1.5 * 2.0 ** 23
PI_IN = 3.1415925


def turns_removed(dve, step, y, m):
    step.then_wait(dve, dve.tensor_scalar(m, y, 0.15915494309189535, ROUND, ALU.mult, ALU.add))
    step.then_wait(dve, dve.tensor_scalar(m, m, ROUND, None, ALU.subtract))
    for part in TWO_PI_PARTS:
        step.then_wait(dve, dve.scalar_tensor_tensor(y, m, -part, y, ALU.mult, ALU.add))
    return dve.tensor_scalar(y, y, PI_IN, -PI_IN, ALU.min, ALU.max)


def l0_ffn(nc, d, x, xnT):
    F = d["f0_w1"].shape[1]
    FC = F // P
    with ExitStack() as ctx:
        sb, pb, sem = scope(nc, ctx, "l0f")
        w1, w2 = sb("w1", [P, F]), sb("w2", [P, FC, P])
        vec = sb("vec", [P, 4, FC])
        b2 = sb("b2", [P, P])
        coef, cosr, sinr, room = (sb(n, [P, FC]) for n in ("coef", "cosr", "sinr", "room"))
        h, y, m = sb("h", [P, 3, 512]), sb("y", [P, 3, 512]), sb("m", [P, 512])
        a = sb("a", [P, 2, FC, 512])
        hid = [pb(f"hid{n}", [P, 512]) for n in range(2)]
        outp = [pb(f"outp{n}", [P, 4, P]) for n in range(2)]
        w_in, bias_added = sem("w_in"), sem("bias_added")
        hid_ready, hid_kept, y_ready, sine_done = sem("hid_ready"), sem("hid_kept"), sem("y_ready"), sem("sine_done")
        q_ready, act_ready, out_ready, out_kept = sem("q_ready"), sem("act_ready"), sem("out_ready"), sem("out_kept")
        dve_step, angle_ready, trig_ready = sem("dve_step"), sem("angle_ready"), sem("trig_ready")
        items = [(g, c) for g in range(4) for c in range(FC)]
        block = ctx.enter_context(nc.Block(no_gpsimd_drain=True))

        @block.sync
        def _(sp):
            for dst, src in ((w1, d["f0_w1"]), (vec, d["f0_vec"]), (w2, d["f0_w2"]), (b2, d["f0_b2"].partition_broadcast(P))):
                sp.dma_start(dst[:], src).then_inc(w_in, 16)

        @block.gpsimd
        def _(pool):
            pool.wait_ge(w_in, 64)
            pool.tensor_tensor(x[:, :, :], x[:, :, :], b2[:, :].unsqueeze(1).broadcast_to([P, TT, P]),
                               ALU.add).then_inc(bias_added, 1)

        @block.scalar
        def _(act):
            act.wait_ge(angle_ready, 1)
            act.activation(sinr[:, :], vec[:, 1, :], ACT.Sin).then_inc(trig_ready, 1)
            act.activation(cosr[:, :], vec[:, 1, :], ACT.Sin, scale=0.5).then_inc(trig_ready, 1)

            def keep(n):
                g, c = items[n]
                act.wait_ge(hid_ready, n + 1)
                if n >= 3:
                    act.wait_ge(act_ready, n - 2)
                act.activation(h[:, n % 3, :], hid[n % 2][:, :], ACT.Identity, bias=vec[:, 0, c:c + 1]).then_inc(hid_kept, 1)

            def sine(n):
                act.wait_ge(y_ready, n + 1)
                act.activation(y[:, n % 3, :], y[:, n % 3, :], ACT.Sin).then_inc(sine_done, 1)

            def relu(n):
                g, c = items[n]
                act.wait_ge(q_ready, n + 1)
                if g >= 2:
                    act.wait_ge(out_ready, g - 1)
                act.activation(a[:, g % 2, c, :], h[:, n % 3, :], ACT.Relu).then_inc(act_ready, 1)

            keep(0)
            for n in range(len(items)):
                if n + 1 < len(items):
                    keep(n + 1)
                sine(n)
                if n >= 1:
                    relu(n - 1)
            relu(len(items) - 1)

        @block.vector
        def _(dve):
            step = Count(dve_step)
            dve.wait_ge(w_in, 64)
            turns_removed(dve, step, vec[:, 1, :], room[:, :]).then_inc(angle_ready, 1)
            dve.wait_ge(trig_ready, 2)
            step.then_wait(dve, dve.tensor_tensor(cosr[:, :], cosr[:, :], cosr[:, :], ALU.mult))
            step.then_wait(dve, dve.tensor_scalar(cosr[:, :], cosr[:, :], -2.0, 1.0, ALU.mult, ALU.add))
            step.then_wait(dve, dve.tensor_tensor(cosr[:, :], cosr[:, :], vec[:, 2, :], ALU.mult))
            step.then_wait(dve, dve.tensor_tensor(coef[:, :], sinr[:, :], vec[:, 3, :], ALU.mult))
            step.then_wait(dve, dve.tensor_tensor(coef[:, :], coef[:, :], cosr[:, :], ALU.add))
            step.then_wait(dve, dve.tensor_tensor(coef[:, :], coef[:, :], vec[:, 3, :], ALU.mult))
            step.then_wait(dve, dve.tensor_scalar(coef[:, :], coef[:, :], 0.1, None, ALU.mult))

            def angle(n):
                g, c = items[n]
                dve.wait_ge(hid_kept, n + 1)
                s = y[:, n % 3, :]
                step.then_wait(dve, dve.tensor_scalar(s, h[:, n % 3, :], 0.1, vec[:, 1, c:c + 1], ALU.mult, ALU.add))
                turns_removed(dve, step, s, m[:, :]).then_inc(y_ready, 1)

            def combine(n):
                g, c = items[n]
                dve.wait_ge(sine_done, n + 1)
                dve.scalar_tensor_tensor(h[:, n % 3, :], y[:, n % 3, :], coef[:, c:c + 1], h[:, n % 3, :],
                                         ALU.mult, ALU.add).then_inc(q_ready, 1)

            def add(g):
                dve.wait_ge(out_ready, g + 1)
                dve.wait_ge(bias_added, 1)
                s = x[:, 4 * g:4 * g + 4, :]
                dve.tensor_tensor(s, outp[g % 2][:, :, :], s, ALU.add).then_inc(out_kept, 1)

            for n in range(len(items)):
                angle(n)
                if n >= 1:
                    combine(n - 1)
                if n % FC == 1 and n > FC:
                    add(n // FC - 1)
            combine(len(items) - 1)
            add(3)

        @block.tensor
        def _(pe):
            pe.wait_ge(w_in, 64)

            def down(g):
                if g >= 2:
                    pe.wait_ge(out_kept, g - 1)
                for c in range(FC):
                    pe.wait_ge(act_ready, FC * g + c + 1)
                    for t in range(4):
                        mm = pe.matmul(outp[g % 2][:, t, :], a[:, g % 2, c, t * P:(t + 1) * P], w2[:, c, :],
                                       start=(c == 0 and t == 0), stop=(c == FC - 1), skip_group_check=True)
                mm.then_inc(out_ready, 1)

            for n, (g, c) in enumerate(items):
                if n >= 2:
                    pe.wait_ge(hid_kept, n - 1)
                pe.matmul(hid[n % 2][:, :], w1[:, c * P:(c + 1) * P], xnT[:, g * 512:(g + 1) * 512],
                          start=True, stop=True).then_inc(hid_ready, 1)
                if c == 1 and g >= 1:
                    down(g - 1)
            down(3)
def l1_attention(nc, d, x, xnT, ident):
    DI = d["a1_out"].shape[0]
    scale = DI ** -0.5
    with ExitStack() as ctx:
        sb, pb, sem = scope(nc, ctx, "l1a")
        wqkv, wout, bout = sb("wqkv", [P, 3 * DI]), sb("wout", [2 * DI, P]), sb("bout", [P, P])
        maskf, mask, identb = sb("maskf", [P, P]), sb("mask", [P, P], BF16), sb("identb", [P, P], BF16)
        qa, ka = sb("qa", [DI + 1, 2, SEQ]), sb("ka", [DI + 1, 2, SEQ])
        qr, kr = sb("qr", [DI, 2, SEQ], F32R), sb("kr", [DI, 2, SEQ], F32R)
        E = sb("E", [P, 2, 36 * P])
        V1 = sb("V1", [P, ST, 2, DI + 1])
        AO, AT = sb("AO", [P, ST, 2, DI]), sb("AT", [P, ST, P])
        mx, mh, ml = sb("mx", [P, 2, ST]), sb("mh", [P, 2, ST], BF16), sb("ml", [P, 2, ST], BF16)
        rs = sb("rs", [P, ST, 2])
        ring = [pb(f"ring{n}", [P, SEQ]) for n in range(2)]
        agg = [pb(f"agg{n}", [P, 512]) for n in range(4)]
        w_in, pool_step, dve_step, bf_ready = sem("w_in"), sem("pool_step"), sem("dve_step"), sem("bf_ready")
        q_ready, k_ready, v_ready = sem("q_ready"), sem("k_ready"), sem("v_ready")
        q_kept, k_kept, v_kept, rounded = sem("q_kept"), sem("k_kept"), sem("v_kept"), sem("rounded")
        rowmax_ready, max_done, mparts = sem("rowmax_ready"), sem("max_done"), sem("mparts")
        mrow_ready, mrow_kept = sem("mrow_ready"), sem("mrow_kept")
        score_ready, exp_done, masked = sem("score_ready"), sem("exp_done"), sem("masked")
        agg_ready, ao_ready, at_ready, at_kept = sem("agg_ready"), sem("ao_ready"), sem("at_ready"), sem("at_kept")
        y_ready, y_added = sem("y_ready"), sem("y_added")
        ecol = [sum(SEQ - P * k for k in range(jt)) for jt in range(ST)]

        def e_tile(b, jt, it):
            at = ecol[jt] + (it - jt) * P
            return E[:, b, at:at + P]

        block = ctx.enter_context(nc.Block(no_gpsimd_drain=True))

        @block.sync
        def _(sp):
            for dst, src in ((wqkv[:, :], d["a1_qkv"]), (maskf[:, :], d["cmask"]), (wout[0:DI, :], d["a1_out"]),
                             (wout[DI:2 * DI, :], d["a1_out"]), (bout[:, :], d["a1_bout"].partition_broadcast(P))):
                sp.dma_start(dst, src).then_inc(w_in, 16)

        @block.gpsimd
        def _(pool):
            pool.memset(V1[:, :, :, DI:DI + 1], 1.0).then_inc(pool_step, 1)
            pool.wait_ge(pool_step, 1)
            pool.memset(ka[DI:DI + 1, :, :], 1.0).then_inc(pool_step, 1)
            pool.wait_ge(pool_step, 2)
            pool.wait_ge(w_in, 80)
            pool.tensor_tensor(x[:, :, :], x[:, :, :], bout[:, :].unsqueeze(1).broadcast_to([P, TT, P]),
                               ALU.add).then_inc(pool_step, 1)
            for b in range(2):
                for jt in range(ST):
                    pool.wait_ge(exp_done, ST * b + jt + 1)
                    tile = e_tile(b, jt, jt)
                    pool.affine_select(out=tile, in_=tile, compare_op=ALU.is_ge, fill=0.0, base=0,
                                       pattern=[[1, P]], channel_multiplier=-1).then_inc(masked, 1)

        @block.scalar
        def _(act):
            for b in range(2):
                act.wait_ge(q_ready, b + 1)
                act.activation(qa[0:DI, b, :], ring[b][0:DI, :], ACT.Copy, scale=scale).then_inc(q_kept, 1)
            for b in range(2):
                act.wait_ge(mrow_ready, b + 1)
                act.activation(qa[DI:DI + 1, b, :], ring[b][0:1, :], ACT.Copy, scale=-1.0).then_inc(mrow_kept, 1)
            for n in range(2 * ST):
                b, jt = n // ST, n % ST
                act.wait_ge(score_ready, n + 1)
                w = SEQ - P * jt
                act.activation(E[:, b, ecol[jt]:ecol[jt] + w], ring[n % 2][:, 0:w], ACT.Exp).then_inc(exp_done, 1)
            for it in range(ST):
                act.wait_ge(at_ready, it + 1)
                act.activation(AT[:, it, :], agg[2 + it % 2][:, 0:P], ACT.Copy).then_inc(at_kept, 1)

        @block.tensor
        def _(pe):
            pe.wait_ge(w_in, 80)
            for b in range(2):
                for c in range(2):
                    mm = pe.matmul(ring[b][0:DI, c * 512:(c + 1) * 512], wqkv[:, 0:DI],
                                   xnT[:, b * SEQ + c * 512:b * SEQ + (c + 1) * 512], start=True, stop=True)
                mm.then_inc(q_ready, 1)
            for b in range(2):
                pe.wait_ge(q_kept, b + 1)
                for c in range(2):
                    mm = pe.matmul(ring[b][0:DI, c * 512:(c + 1) * 512], wqkv[:, DI:2 * DI],
                                   xnT[:, b * SEQ + c * 512:b * SEQ + (c + 1) * 512], start=True, stop=True)
                mm.then_inc(k_ready, 1)
            for b in range(2):
                for t in range(ST):
                    mm = pe.matmul(agg[b][:, t * DI:(t + 1) * DI], xnT[:, b * SEQ + t * P:b * SEQ + (t + 1) * P],
                                   wqkv[:, 2 * DI:3 * DI], start=True, stop=True)
                mm.then_inc(v_ready, 1)
            pe.wait_ge(bf_ready, 1)
            for n in range(2 * ST):
                it, b = n // 2, n % 2
                if n < 2:
                    pe.wait_ge(k_kept, n + 1)
                    pe.wait_ge(rounded, 2 * (n + 1))
                else:
                    pe.wait_ge(max_done, n - 1)
                w = (it + 1) * P
                for c0 in range(0, w, 512):
                    c1 = min(w, c0 + 512)
                    pe.matmul(ring[n % 2][:, c0:c1], qr[:, b, it * P:(it + 1) * P], kr[:, b, c0:c1],
                              start=True, stop=c1 < w)
                pe.matmul(ring[n % 2][:, it * P:w], identb[:, :], mask[:, :], start=False,
                          stop=True).then_inc(rowmax_ready, 1)
            for b in range(2):
                pe.wait_ge(mparts, b + 1)
                for it in range(ST):
                    pe.matmul(ring[b][0:1, it * P:(it + 1) * P], mh[:, b, it:it + 1], identb[:, :], start=True, stop=False)
                    mm = pe.matmul(ring[b][0:1, it * P:(it + 1) * P], ml[:, b, it:it + 1], identb[:, :],
                                   start=False, stop=True)
                mm.then_inc(mrow_ready, 1)
            for n in range(2 * ST):
                b, jt = n // ST, n % ST
                if n == 0:
                    pe.wait_ge(pool_step, 2)
                if n < 2:
                    pe.wait_ge(mrow_kept, n + 1)
                else:
                    pe.wait_ge(exp_done, n - 1)
                w = SEQ - P * jt
                for c0 in range(0, w, 512):
                    c1 = min(w, c0 + 512)
                    mm = pe.matmul(ring[n % 2][:, c0:c1], ka[:, b, jt * P:(jt + 1) * P],
                                   qa[:, b, P * jt + c0:P * jt + c1], start=True, stop=True)
                mm.then_inc(score_ready, 1)
            pe.wait_ge(v_kept, 2)

            def turn(it):
                pe.wait_ge(ao_ready, it + 1)
                if it >= 2:
                    pe.wait_ge(at_kept, it - 1)
                pe.transpose(agg[2 + it % 2][:, 0:P], AO[:, it, :, :].rearrange("p a b -> p (a b)"),
                             ident[:, :]).then_inc(at_ready, 1)

            for it in range(ST):
                if it >= 2:
                    pe.wait_ge(ao_ready, it - 1)
                pe.wait_ge(masked, ST + it + 1)
                for b in range(2):
                    for jt in range(it + 1):
                        mm = pe.matmul(agg[it % 2][:, b * 65:(b + 1) * 65], e_tile(b, jt, it), V1[:, jt, b, :],
                                       start=(jt == 0), stop=(jt == it))
                mm.then_inc(agg_ready, 1)
                if it >= 1:
                    turn(it - 1)
            turn(ST - 1)
            for g in range(4):
                b = g // 2
                if g < 2:
                    pe.wait_ge(at_kept, ST)
                    pe.wait_ge(ao_ready, ST)
                else:
                    pe.wait_ge(y_added, g - 1)
                for t in range(4):
                    mm = pe.matmul(agg[g % 2][:, t * P:(t + 1) * P], AT[b * DI:(b + 1) * DI, 4 * (g % 2) + t, :],
                                   wout[b * DI:(b + 1) * DI, :], start=True, stop=True)
                mm.then_inc(y_ready, 1)

        @block.vector
        def _(dve):
            step = Count(dve_step)
            dve.wait_ge(w_in, 80)
            step.then_wait(dve, dve.tensor_copy(mask[:, :], maskf[:, :]))
            dve.tensor_copy(identb[:, :], ident[:, :]).then_inc(bf_ready, 1)
            for b in range(2):
                dve.wait_ge(k_ready, b + 1)
                dve.tensor_copy(ka[0:DI, b, :], ring[b][0:DI, :]).then_inc(k_kept, 1)
            for b in range(2):
                dve.wait_ge(v_ready, b + 1)
                dve.tensor_copy(V1[:, :, b, 0:DI], agg[b][:, :].rearrange("p (t w) -> p t w", t=ST)).then_inc(v_kept, 1)
            for b in range(2):
                dve.wait_ge(q_kept, b + 1)
                dve.wait_ge(k_kept, b + 1)
                dve.tensor_copy(qr[:, b, :], qa[0:DI, b, :]).then_inc(rounded, 1)
                dve.tensor_copy(kr[:, b, :], ka[0:DI, b, :]).then_inc(rounded, 1)
            for n in range(2 * ST):
                it, b = n // 2, n % 2
                dve.wait_ge(rowmax_ready, n + 1)
                dve.tensor_reduce(mx[:, b, it:it + 1], ring[n % 2][:, 0:(it + 1) * P], AX_X, ALU.max).then_inc(max_done, 1)
            dve.wait_ge(max_done, 2 * ST)
            for b in range(2):
                step.then_wait(dve, dve.tensor_copy(mh[:, b, :], mx[:, b, :]))
                dve.tensor_tensor(ml[:, b, :], mx[:, b, :], mh[:, b, :], ALU.subtract).then_inc(mparts, 1)
            for it in range(ST):
                dve.wait_ge(agg_ready, it + 1)
                a = agg[it % 2][:, 0:130].rearrange("p (h w) -> p h w", h=2)
                step.then_wait(dve, dve.reciprocal(rs[:, it, :], a[:, :, DI]))
                dve.tensor_tensor(AO[:, it, :, :], a[:, :, 0:DI], spread(rs[:, it, :], [P, 2, DI]), ALU.mult).then_inc(ao_ready, 1)
            dve.wait_ge(pool_step, 3)
            for g in range(4):
                dve.wait_ge(y_ready, g + 1)
                s = x[:, 4 * g:4 * g + 4, :]
                dve.tensor_tensor(s, agg[g % 2][:, :].rearrange("p (t w) -> p t w", t=4), s, ALU.add).then_inc(y_added, 1)
NE = 8


def first_best(dve, step, pick, score, best, rank, prio, shape):
    step.then_wait(dve, dve.tensor_reduce(best, score, AX_X, ALU.max))
    step.then_wait(dve, dve.tensor_tensor(rank, score, spread(best, shape), ALU.is_ge))
    step.then_wait(dve, dve.tensor_tensor(rank, rank, prio, ALU.mult))
    step.then_wait(dve, dve.tensor_reduce(best, rank, AX_X, ALU.max))
    step.then_wait(dve, dve.tensor_tensor(pick, rank, spread(best, shape), ALU.is_equal))


def gate_top1(nc, name, d, keys, x, xnT, ident, pick):
    wkey, bkeys, b2key = keys
    with ExitStack() as ctx:
        sb, pb, sem = scope(nc, ctx, name)
        wg, b2 = sb("wg", [P, NE]), sb("b2", [NE, P])
        bias = [sb(f"bias{n}", [P, NE]) for n in range(len(bkeys))]
        prio = sb("prio", [P, NE])
        score, rank, best = sb("score", [P, TT, NE]), sb("rank", [P, TT, NE]), sb("best", [P, TT])
        pickT = sb("pickT", [NE, TT, P])
        lg = pb("lg", [P, TT, NE])
        pt = [pb(f"pt{n}", [NE, 4, P]) for n in range(2)]
        bb = [pb(f"bb{n}", [P, 4, P]) for n in range(2)]
        w_in, lg_ready, dve_step, pick_ready = sem("w_in"), sem("lg_ready"), sem("dve_step"), sem("pick_ready")
        pt_ready, pt_kept, bb_ready, bb_added = sem("pt_ready"), sem("pt_kept"), sem("bb_ready"), sem("bb_added")
        block = ctx.enter_context(nc.Block(no_gpsimd_drain=True))
        NW = 16 * (3 + len(bkeys))

        @block.sync
        def _(sp):
            sp.dma_start(wg[:, :], d[wkey]).then_inc(w_in, 16)
            sp.dma_start(b2[:, :], d[b2key]).then_inc(w_in, 16)
            sp.dma_start(prio[:, :], d["prio"].partition_broadcast(P)).then_inc(w_in, 16)
            for t, k in zip(bias, bkeys):
                sp.dma_start(t[:, :], d[k].partition_broadcast(P)).then_inc(w_in, 16)

        @block.tensor
        def _(pe):
            pe.wait_ge(w_in, NW)
            for t in range(TT):
                mm = pe.matmul(lg[:, t, :], xnT[:, t * P:(t + 1) * P], wg[:, :], start=True, stop=True)
            mm.then_inc(lg_ready, 1)
            pe.wait_ge(pick_ready, 1)
            for g in range(4):
                if g >= 2:
                    pe.wait_ge(pt_kept, g - 1)
                for t in range(4):
                    mm = pe.transpose(pt[g % 2][:, t, :], pick[:, 4 * g + t, :], ident[:, :])
                mm.then_inc(pt_ready, 1)
                pe.wait_ge(pt_kept, g + 1)
                if g >= 2:
                    pe.wait_ge(bb_added, g - 1)
                for t in range(4):
                    mm = pe.matmul(bb[g % 2][:, t, :], pickT[:, 4 * g + t, :], b2[:, :], start=True, stop=True)
                mm.then_inc(bb_ready, 1)

        @block.scalar
        def _(act):
            for g in range(4):
                act.wait_ge(pt_ready, g + 1)
                act.activation(pickT[:, 4 * g:4 * g + 4, :], pt[g % 2][:, :, :], ACT.Copy).then_inc(pt_kept, 1)

        @block.vector
        def _(dve):
            step = Count(dve_step)
            shape = [P, TT, NE]
            dve.wait_ge(lg_ready, 1)
            src = lg
            for t in bias:
                step.then_wait(dve, dve.tensor_tensor(score[:, :, :], src[:, :, :],
                                                      t[:, :].unsqueeze(1).broadcast_to(shape), ALU.add))
                src = score
            first_best(dve, step, pick[:, :, :], score[:, :, :], best[:, :], rank[:, :, :],
                       prio[:, :].unsqueeze(1).broadcast_to(shape), shape)
            dve.engine_nop().then_inc(pick_ready, 1)
            for g in range(4):
                dve.wait_ge(bb_ready, g + 1)
                s = x[:, 4 * g:4 * g + 4, :]
                dve.tensor_tensor(s, bb[g % 2][:, :, :], s, ALU.add).then_inc(bb_added, 1)


def experts_dense(nc, name, kind, d, keys, x, xnT, cw):
    upkeys, b1key, downkey = keys
    NU = len(upkeys)
    F = d[upkeys[0]].shape[1]
    FC = F // P
    with ExitStack() as ctx:
        sb, pb, sem = scope(nc, ctx, name)
        up = [[sb(f"up{j}_{u}", [P, F]) for u in range(NU)] for j in range(2)]
        down = [sb(f"down{j}", [P, FC, P]) for j in range(2)]
        b1 = [sb(f"b1_{j}", [P, FC]) for j in range(2)]
        a = sb("a", [P, 2, FC, 512])
        gate = sb("gate", [P, 2, 512])
        hid = [pb(f"hid{n}", [P, 512]) for n in range(2 * NU)]
        outp = [pb(f"outp{n}", [P, 4, P]) for n in range(2)]
        w_in = [sem("w_in0"), sem("w_in1")]
        hid_ready, gate_done, act_ready = sem("hid_ready"), sem("gate_done"), sem("act_ready")
        out_ready, out_added = sem("out_ready"), sem("out_added")
        per_w = 16 * (NU + 1 + (b1key is not None))
        func = {"gelu": ACT.Gelu, "relu": ACT.Relu, "silu": ACT.Silu}[kind]
        block = ctx.enter_context(nc.Block(no_gpsimd_drain=True))

        @block.sync
        def _(sp):
            def load(e, j):
                for u, k in enumerate(upkeys):
                    sp.dma_start(up[j][u][:, :], d[k][bass.ds(e * P, P), :]).then_inc(w_in[j], 16)
                sp.dma_start(down[j][:, :, :].rearrange("p a b -> p (a b)"), d[downkey][bass.ds(e * P, P), :]).then_inc(w_in[j], 16)
                if b1key is not None:
                    sp.dma_start(b1[j][:, :], d[b1key][bass.ds(e * P, P), :]).then_inc(w_in[j], 16)
            load(0, 0)
            load(1, 1)
            with sp.Fori(0, NE // 2 - 1) as i:
                for j in range(2):
                    sp.wait_ge(out_ready, i * 8 + 4 * (j + 1))
                    load(i * 2 + 2 + j, j)

        def experts(eng, body):
            for j in range(2):
                body(0, j)
            with eng.Fori(1, NE // 2) as i:
                for j in range(2):
                    body(i, j)

        def each(upf, downf):
            for g in range(4):
                upf(g)
                if g >= 1:
                    downf(g - 1)
            downf(3)

        @block.tensor
        def _(pe):
            def body(i, j):
                pe.wait_ge(w_in[j], (i + 1) * per_w)

                def upf(g):
                    for c in range(FC):
                        n = (4 * j + g) * FC + c
                        wait(pe, act_ready, i * 8 * FC + n - 1)
                        for u in range(NU):
                            mm = pe.matmul(hid[(n % 2) * NU + u][:, :], up[j][u][:, c * P:(c + 1) * P],
                                           xnT[:, g * 512:(g + 1) * 512], start=True, stop=True)
                        mm.then_inc(hid_ready, 1)

                def downf(g):
                    m = 4 * j + g
                    wait(pe, out_added, i * 8 + m - 1)
                    for c in range(FC):
                        pe.wait_ge(act_ready, i * 8 * FC + m * FC + c + 1)
                        for t in range(4):
                            mm = pe.matmul(outp[g % 2][:, t, :], a[:, g % 2, c, t * P:(t + 1) * P], down[j][:, c, :],
                                           start=(c == 0 and t == 0), stop=(c == FC - 1), skip_group_check=True)
                    mm.then_inc(out_ready, 1)

                each(upf, downf)

            experts(pe, body)

        @block.scalar
        def _(act):
            def body(i, j):
                if b1key is not None:
                    act.wait_ge(w_in[j], (i + 1) * per_w)
                for g in range(4):
                    for c in range(FC):
                        n = (4 * j + g) * FC + c
                        act.wait_ge(hid_ready, i * 8 * FC + n + 1)
                        m = 4 * j + g
                        if NU == 1:
                            wait(act, out_ready, i * 8 + m - 1)
                            act.activation(a[:, g % 2, c, :], hid[n % 2][:, :], func, bias=b1[j][:, c:c + 1]).then_inc(act_ready, 1)
                        else:
                            wait(act, act_ready, i * 8 * FC + n - 1)
                            act.activation(gate[:, n % 2, :], hid[(n % 2) * NU][:, :], func).then_inc(gate_done, 1)

            experts(act, body)

        @block.vector
        def _(dve):
            def body(i, j):
                def upf(g):
                    if NU == 1:
                        return
                    for c in range(FC):
                        n = (4 * j + g) * FC + c
                        m = 4 * j + g
                        dve.wait_ge(gate_done, i * 8 * FC + n + 1)
                        wait(dve, out_ready, i * 8 + m - 1)
                        dve.tensor_tensor(a[:, g % 2, c, :], gate[:, n % 2, :], hid[(n % 2) * NU + 1][:, :],
                                          ALU.mult).then_inc(act_ready, 1)

                def downf(g):
                    m = 4 * j + g
                    dve.wait_ge(out_ready, i * 8 + m + 1)
                    for t in range(4):
                        s = x[:, 4 * g + t, :]
                        w = cw[:, 4 * g + t, :][:, bass.ds(i * 2 + j, 1)]
                        ins = dve.scalar_tensor_tensor(s, outp[g % 2][:, t, :], w, s, ALU.mult, ALU.add)
                    ins.then_inc(out_added, 1)

                each(upf, downf)

            experts(dve, body)
def l2_attention(nc, d, x, xnT, ident):
    NH = 16
    W = 3 * P + 1
    with ExitStack() as ctx:
        sb, pb, sem = scope(nc, ctx, "l2a")
        wkgv, wq, wo = sb("wkgv", [P, 3 * P]), sb("wq", [P, P]), sb("wo", [P, P])
        bkgv, bq, bo = sb("bkgv", [P, 3 * P]), sb("bq", [P, 1]), sb("bo", [P, P])
        heads = sb("heads", [P, P + NH])
        KGV = sb("KGV", [P, TT, W])
        room = sb("room", [P, ST, P])
        QT, qroom = sb("QT", [P, TOK]), sb("qroom", [P, TOK])
        RK = sb("RK", [P, NB, P + NH])
        z = sb("z", [P, TT, NH])
        O, OT = sb("O", [P, TT, P]), sb("OT", [P, TT, P])
        ring = [pb(f"ring{n}", [P, 512]) for n in range(2)]
        qp = [pb(f"qp{n}", [P, 512]) for n in range(2)]
        kv = pb("kv", [P, NB, 256])
        outp = [pb(f"outp{n}", [P, 4, P]) for n in range(2)]
        w_in, one_set, bo_added = sem("w_in"), sem("one_set"), sem("bo_added")
        kgv_ready, kgv_kept, q_ready, q_kept = sem("kgv_ready"), sem("kgv_kept"), sem("q_ready"), sem("q_kept")
        low_ready, exp_done, k_ready, g_exp, g_ready = (sem(n) for n in ("low_ready", "exp_done", "k_ready", "g_exp", "g_ready"))
        qlow_ready, qexp_done, qT_ready = sem("qlow_ready"), sem("qexp_done"), sem("qT_ready")
        kv_ready, rk_ready, num_ready, o_ready = sem("kv_ready"), sem("rk_ready"), sem("num_ready"), sem("o_ready")
        ot_ready, ot_kept, out_ready, out_added = sem("ot_ready"), sem("ot_kept"), sem("out_ready"), sem("out_added")
        dve_step = sem("dve_step")
        block = ctx.enter_context(nc.Block(no_gpsimd_drain=True))

        @block.sync
        def _(sp):
            for dst, src in ((wkgv, d["a2_wkgv"]), (bkgv, d["a2_bkgv"].partition_broadcast(P)), (wq, d["a2_wq"]),
                             (bq, d["a2_bq"]), (heads, d["heads"]), (wo, d["a2_wo"]), (bo, d["a2_bo"].partition_broadcast(P))):
                sp.dma_start(dst[:], src).then_inc(w_in, 16)

        @block.gpsimd
        def _(pool):
            pool.memset(KGV[:, :, 3 * P:W], 1.0).then_inc(one_set, 1)
            pool.wait_ge(w_in, 7 * 16)
            pool.tensor_tensor(x[:, :, :], x[:, :, :], bo[:, :].unsqueeze(1).broadcast_to([P, TT, P]),
                               ALU.add).then_inc(bo_added, 1)

        @block.tensor
        def _(pe):
            pe.wait_ge(w_in, 7 * 16)
            for t in range(TT):
                if t >= 2:
                    pe.wait_ge(kgv_kept, t - 1)
                pe.matmul(ring[t % 2][:, 0:3 * P], xnT[:, t * P:(t + 1) * P], wkgv[:, :], start=True,
                          stop=True).then_inc(kgv_ready, 1)
                if t % 4 == 3:
                    g = t // 4
                    if g >= 2:
                        pe.wait_ge(q_kept, g - 1)
                    pe.matmul(qp[g % 2][:, :], wq[:, :], xnT[:, g * 512:(g + 1) * 512], start=True,
                              stop=True).then_inc(q_ready, 1)
            for b in range(NB):
                pe.wait_ge(k_ready, b + 1)
                pe.wait_ge(one_set, 1)
                for t in range(b * ST, (b + 1) * ST):
                    mm = pe.matmul(kv[:, b, 0:P + 1], KGV[:, t, 0:P], KGV[:, t, 2 * P:W],
                                   start=(t == b * ST), stop=(t == (b + 1) * ST - 1))
                mm.then_inc(kv_ready, 1)

            def turn(g):
                pe.wait_ge(o_ready, 2 * (g + 1))
                if g >= 2:
                    pe.wait_ge(ot_kept, g - 1)
                for t in range(4):
                    mm = pe.transpose(qp[g % 2][:, t * P:(t + 1) * P], O[:, 4 * g + t, :], ident[:, :])
                mm.then_inc(ot_ready, 1)

            def project(g):
                pe.wait_ge(ot_kept, g + 1)
                if g >= 2:
                    pe.wait_ge(out_added, g - 1)
                for t in range(4):
                    mm = pe.matmul(outp[g % 2][:, t, :], OT[:, 4 * g + t, :], wo[:, :], start=True, stop=True)
                mm.then_inc(out_ready, 1)

            pe.wait_ge(qT_ready, 1)
            pe.wait_ge(q_kept, 4)
            for n in range(TT // 2):
                if n * 2 % ST == 0:
                    pe.wait_ge(rk_ready, n * 2 // ST + 1)
                if n >= 2:
                    pe.wait_ge(o_ready, n - 1)
                for j in range(2):
                    t = 2 * n + j
                    mm = pe.matmul(ring[n % 2][:, j * (P + NH):(j + 1) * (P + NH)], QT[:, t * P:(t + 1) * P],
                                   RK[:, t // ST, :], start=True, stop=True)
                mm.then_inc(num_ready, 1)
                if n % 2 == 0 and n >= 2:
                    turn(n // 2 - 1)
                if n % 2 == 1 and n >= 3:
                    project(n // 2 - 1)
            turn(3)
            project(3)

        @block.scalar
        def _(act):
            act.wait_ge(w_in, 7 * 16)
            for b in range(NB):
                for g in (2 * b, 2 * b + 1):
                    act.wait_ge(q_ready, g + 1)
                    act.activation(QT[:, g * 512:(g + 1) * 512], qp[g % 2][:, :], ACT.Identity, bias=bq[:, :]).then_inc(q_kept, 1)
                s = slice(b * ST, (b + 1) * ST)
                act.wait_ge(low_ready, b + 1)
                act.activation(room[:, :, :], room[:, :, :], ACT.Exp).then_inc(exp_done, 1)
                act.activation(KGV[:, s, P:2 * P], KGV[:, s, P:2 * P], ACT.Exp, scale=-1.0).then_inc(g_exp, 1)
            act.wait_ge(qlow_ready, 1)
            act.activation(qroom[:, :], qroom[:, :], ACT.Exp).then_inc(qexp_done, 1)
            for g in range(4):
                act.wait_ge(ot_ready, g + 1)
                act.activation(OT[:, 4 * g:4 * g + 4, :], qp[g % 2][:, :].rearrange("p (t w) -> p t w", t=4),
                               ACT.Copy).then_inc(ot_kept, 1)

        @block.vector
        def _(dve):
            step = Count(dve_step)
            dve.wait_ge(w_in, 7 * 16)
            for b in range(NB):
                s = slice(b * ST, (b + 1) * ST)
                for t in range(b * ST, (b + 1) * ST):
                    dve.wait_ge(kgv_ready, t + 1)
                    dve.tensor_tensor(KGV[:, t, 0:3 * P], ring[t % 2][:, 0:3 * P], bkgv[:, :], ALU.add).then_inc(kgv_kept, 1)
                dve.wait_ge(kgv_kept, (b + 1) * ST)
                dve.tensor_scalar(room[:, :, :], KGV[:, s, 0:P], 0.0, None, ALU.min).then_inc(low_ready, 1)
                dve.wait_ge(exp_done, b + 1)
                dve.scalar_tensor_tensor(KGV[:, s, 0:P], KGV[:, s, 0:P], 0.0, room[:, :, :], ALU.max, ALU.add).then_inc(k_ready, 1)
                dve.wait_ge(k_ready, b + 1)
                if b == NB - 1:
                    dve.wait_ge(q_kept, 4)
                    dve.tensor_scalar(qroom[:, :], QT[:, :], 0.0, None, ALU.min).then_inc(qlow_ready, 1)
                dve.wait_ge(g_exp, b + 1)
                step.then_wait(dve, dve.tensor_scalar(KGV[:, s, P:2 * P], KGV[:, s, P:2 * P], 1.0, None, ALU.add))
                step.then_wait(dve, dve.reciprocal(KGV[:, s, P:2 * P], KGV[:, s, P:2 * P]))
            dve.wait_ge(qexp_done, 1)
            dve.scalar_tensor_tensor(QT[:, :], QT[:, :], 0.0, qroom[:, :], ALU.max, ALU.add).then_inc(qT_ready, 1)
            for b in range(NB):
                dve.wait_ge(kv_ready, 2)
                dve.tensor_tensor(RK[:, b, 0:P], kv[:, b, 0:P], heads[:, 0:P], ALU.mult)
                dve.tensor_scalar(RK[:, b, P:P + NH], heads[:, P:P + NH], kv[:, b, P:P + 1], None, ALU.mult).then_inc(rk_ready, 1)

            def add(g):
                dve.wait_ge(out_ready, g + 1)
                s = x[:, 4 * g:4 * g + 4, :]
                dve.tensor_tensor(s, outp[g % 2][:, :, :], s, ALU.add).then_inc(out_added, 1)

            dve.wait_ge(bo_added, 1)
            for n in range(TT // 2):
                dve.wait_ge(num_ready, n + 1)
                ps = ring[n % 2][:, 0:2 * (P + NH)].rearrange("p (j w) -> p j w", j=2)
                s = slice(2 * n, 2 * n + 2)
                step.then_wait(dve, dve.tensor_scalar(z[:, s, :], ps[:, :, P:P + NH], 1e-6, None, ALU.add))
                step.then_wait(dve, dve.reciprocal(z[:, s, :], z[:, s, :]))
                for t in range(2):
                    ins = dve.tensor_tensor(O[:, 2 * n + t, :].rearrange("p (h w) -> p h w", h=NH),
                                            ps[:, t, 0:P].rearrange("p (h w) -> p h w", h=NH),
                                            spread(z[:, 2 * n + t, :], [P, NH, P // NH]), ALU.mult)
                    step.mark(ins)
                dve.wait_ge(step.sem, step.n)
                dve.tensor_tensor(O[:, s, :], O[:, s, :], KGV[:, s, P:2 * P], ALU.mult).then_inc(o_ready, 1)
                if n % 2 == 1 and n >= 5:
                    add(n // 2 - 2)
            add(2)
            add(3)
def route_top2(nc, d, x, xnT, ident, cw):
    CAP = int(1.25 * TOK / NE)
    R = P // NE
    DIGITS = 8
    with ExitStack() as ctx:
        sb, pb, sem = scope(nc, ctx, "rt")
        wr, prio = sb("wr", [P, NE]), sb("prio", [P, NE])
        digits = sb("digits", [P, DIGITS], I32)
        same = sb("same", [P, P])
        pickrow = sb("pickrow", [P, NE])
        prob, rank, one, two = (sb(n, [P, TT, NE]) for n in ("prob", "rank", "one", "two"))
        best, tot = sb("best", [P, TT]), sb("tot", [P, TT])
        wide = sb("wide", [P, TT, P])
        WR, keep, eq, cum = (sb(n, [P, TOK]) for n in ("WR", "keep", "eq", "cum"))
        zeros = sb("zeros", [P, TOK])
        T, cand, inc = sb("T", [P, 1], I32), sb("cand", [P, 1], I32), sb("inc", [P, 1], I32)
        cnt, flag, need = sb("cnt", [P, 1]), sb("flag", [P, 1]), sb("need", [P, 1])
        lg = pb("lg", [P, TT, NE])
        wt = [pb(f"wt{n}", [P, 512]) for n in range(4)]
        votes = pb("votes", [P, 512])
        cwp = pb("cwp", [P, TT, NE])
        w_in, lg_ready, exp_in, exp_done, wide_ready = (sem(n) for n in ("w_in", "lg_ready", "exp_in", "exp_done", "wide_ready"))
        wt_ready, wr_kept, flag_ready, votes_ready = sem("wt_ready"), sem("wr_kept"), sem("flag_ready"), sem("votes_ready")
        kept_ready, cwp_ready, dve_step, zero_set = sem("kept_ready"), sem("cwp_ready"), sem("dve_step"), sem("zero_set")
        block = ctx.enter_context(nc.Block(no_gpsimd_drain=True))

        @block.sync
        def _(sp):
            for dst, src in ((wr, d["f2_router"]), (prio, d["prio"].partition_broadcast(P)), (digits, d["digits"]),
                             (same, d["same16"]), (pickrow, d["pickrow"])):
                sp.dma_start(dst[:], src).then_inc(w_in, 16)

        @block.gpsimd
        def _(pool):
            pool.memset(zeros[:, :], 0.0).then_inc(zero_set, 1)
            pool.memset(T[:, :], 0).then_inc(zero_set, 1)

        @block.tensor
        def _(pe):
            pe.wait_ge(w_in, 80)
            for t in range(TT):
                mm = pe.matmul(lg[:, t, :], xnT[:, t * P:(t + 1) * P], wr[:, :], start=True, stop=True)
            mm.then_inc(lg_ready, 1)
            pe.wait_ge(wide_ready, 1)
            for g in range(4):
                for t in range(4):
                    mm = pe.transpose(wt[g][:, t * P:(t + 1) * P], wide[:, 4 * g + t, :], ident[:, :])
                mm.then_inc(wt_ready, 1)
            for k in range(DIGITS):
                pe.wait_ge(flag_ready, k + 1)
                pe.matmul(votes[:, 0:1], same[:, :], flag[:, :], start=True, stop=True).then_inc(votes_ready, 1)
            pe.wait_ge(kept_ready, 1)
            for t in range(TT):
                mm = pe.matmul(cwp[:, t, :], keep[:, t * P:(t + 1) * P], pickrow[:, :], start=True, stop=True)
            mm.then_inc(cwp_ready, 1)

        @block.scalar
        def _(act):
            act.wait_ge(exp_in, 1)
            act.activation(prob[:, :, :], prob[:, :, :], ACT.Exp).then_inc(exp_done, 1)
            for g in range(4):
                act.wait_ge(wt_ready, g + 1)
                act.activation(WR[:, g * 512:(g + 1) * 512], wt[g][:, :], ACT.Copy).then_inc(wr_kept, 1)

        @block.vector
        def _(dve):
            step = Count(dve_step)
            shape = [P, TT, NE]
            dve.wait_ge(w_in, 80)
            pr = prio[:, :].unsqueeze(1).broadcast_to(shape)
            dve.wait_ge(lg_ready, 1)
            step.then_wait(dve, dve.tensor_reduce(best[:, :], lg[:, :, :], AX_X, ALU.max))
            dve.tensor_tensor(prob[:, :, :], lg[:, :, :], spread(best[:, :], shape), ALU.subtract).then_inc(exp_in, 1)
            dve.wait_ge(exp_done, 1)
            step.then_wait(dve, dve.tensor_reduce(tot[:, :], prob[:, :, :], AX_X, ALU.add))
            step.then_wait(dve, dve.reciprocal(tot[:, :], tot[:, :]))
            step.then_wait(dve, dve.tensor_tensor(prob[:, :, :], prob[:, :, :], spread(tot[:, :], shape), ALU.mult))
            first_best(dve, step, one[:, :, :], prob[:, :, :], best[:, :], rank[:, :, :], pr, shape)
            step.then_wait(dve, dve.scalar_tensor_tensor(two[:, :, :], one[:, :, :], -2.0, prob[:, :, :], ALU.mult, ALU.add))
            first_best(dve, step, two[:, :, :], two[:, :, :], best[:, :], rank[:, :, :], pr, shape)
            step.then_wait(dve, dve.tensor_tensor(one[:, :, :], one[:, :, :], two[:, :, :], ALU.add))
            step.then_wait(dve, dve.tensor_tensor(prob[:, :, :], prob[:, :, :], one[:, :, :], ALU.mult))
            step.then_wait(dve, dve.tensor_reduce(tot[:, :], prob[:, :, :], AX_X, ALU.add))
            step.then_wait(dve, dve.tensor_scalar(tot[:, :], tot[:, :], 1e-6, None, ALU.add))
            step.then_wait(dve, dve.reciprocal(tot[:, :], tot[:, :]))
            step.then_wait(dve, dve.tensor_tensor(prob[:, :, :], prob[:, :, :], spread(tot[:, :], shape), ALU.mult))
            dve.tensor_copy(wide[:, :, :].rearrange("p t (e r) -> p (t e) r", r=R),
                            spread(prob[:, :, :].rearrange("p t e -> p (t e)"), [P, TT * NE, R])).then_inc(wide_ready, 1)
            dve.wait_ge(wr_kept, 4)
            dve.wait_ge(zero_set, 2)
            for k in range(DIGITS):
                step.then_wait(dve, dve.tensor_tensor(cand[:, :], T[:, :], digits[:, k:k + 1], ALU.bitwise_or))
                step.then_wait(dve, dve.tensor_scalar(keep[:, :], WR[:, :], cand[:, :].bitcast(F32), 0.0, ALU.is_ge,
                                                      ALU.add, accum_out=cnt[:, :]))
                dve.tensor_scalar(flag[:, :], cnt[:, :], CAP - 0.5, None, ALU.is_ge).then_inc(flag_ready, 1)
                dve.wait_ge(votes_ready, k + 1)
                step.then_wait(dve, dve.tensor_scalar(inc[:, :], votes[:, 0:1], 1.0, float(2 ** (28 - 4 * k)),
                                                      ALU.subtract, ALU.mult))
                step.then_wait(dve, dve.tensor_tensor(T[:, :], T[:, :], inc[:, :], ALU.bitwise_or))
            cut = T[:, :].bitcast(F32)
            step.then_wait(dve, dve.tensor_scalar(keep[:, :], WR[:, :], cut, 0.0, ALU.is_gt, ALU.add, accum_out=cnt[:, :]))
            step.then_wait(dve, dve.tensor_scalar(need[:, :], cnt[:, :], -1.0, CAP + 0.5, ALU.mult, ALU.add))
            step.then_wait(dve, dve.tensor_scalar(eq[:, :], WR[:, :], cut, None, ALU.is_equal))
            step.then_wait(dve, dve.tensor_tensor_scan(cum[:, :], eq[:, :], zeros[:, :], 0.0, ALU.add, ALU.add))
            step.then_wait(dve, dve.scalar_tensor_tensor(eq[:, :], cum[:, :], need[:, :], eq[:, :], ALU.is_le, ALU.mult))
            step.then_wait(dve, dve.tensor_tensor(keep[:, :], keep[:, :], eq[:, :], ALU.add))
            dve.tensor_tensor(keep[:, :], keep[:, :], WR[:, :], ALU.mult).then_inc(kept_ready, 1)
            dve.wait_ge(cwp_ready, 1)
            dve.tensor_copy(cw[:, :, :], cwp[:, :, :]).then_inc(dve_step, 1)
def l3_mixer(nc, d, x, xnT, ident):
    DI = d["m_conv"].shape[0]
    HALF = DI // P
    NS = d["m_alog"].shape[1]
    RK = d["m_wdt"].shape[0]
    KC = d["m_conv"].shape[1]
    PAD = KC - 1
    with ExitStack() as ctx:
        sb, pb, sem = scope(nc, ctx, "mx")
        win = sb("win", [P, 2 * DI])
        conv, convb = sb("conv", [P, HALF, KC]), sb("convb", [P, HALF])
        wdt8, wbc = sb("wdt8", [P, HALF, RK]), sb("wbc", [P, HALF, 2 * NS])
        wdt = sb("wdt", [RK, DI])
        bdt, A, Dp = sb("bdt", [P, HALF]), sb("A", [P, HALF, NS]), sb("Dp", [P, HALF])
        wout = sb("wout", [P, HALF, P])
        sel1 = sb("sel1", [96, 2 * NS])
        sel = sb("sel", [96, 2 * NS, P], BF16)
        XI = sb("XI", [P, HALF, NB, PAD + SEQ])
        XC, SZ, DT = (sb(n, [P, HALF, TOK]) for n in ("XC", "SZ", "DT"))
        V, Ex = sb("V", [P, TOK]), sb("Ex", [P, TOK])
        dt8 = sb("dt8", [RK, TOK])
        bc, rest = sb("bc", [96, TOK], BF16), sb("rest", [32, TOK])
        dA, dBu, hst = sb("dA", [P, 2, HALF, SEQ]), sb("dBu", [P, 2, HALF, SEQ]), sb("hst", [P, 2, HALF, SEQ])
        BB = sb("BB", [P, 2, SEQ])
        Bp, Cp = pb("Bp", [P, SEQ]), pb("Cp", [P, SEQ])
        ysum = [pb(f"ysum{h}", [P, SEQ]) for h in range(HALF)]
        work = [Bp, Cp, ysum[0], ysum[1]]
        w_in, pads, proj_ready, proj_kept = sem("w_in"), sem("pads"), sem("proj_ready"), sem("proj_kept")
        tap_done, conv_ready, xc_ready = sem("tap_done"), sem("conv_ready"), sem("xc_ready")
        dbl_ready, dbl_kept, step_ready, v_kept = sem("dbl_ready"), sem("dbl_kept"), sem("step_ready"), sem("v_kept")
        abs_ready, e_ready, u_ready, ln_ready, dt_ready = (sem(n) for n in ("abs_ready", "e_ready", "u_ready", "ln_ready", "dt_ready"))
        a_exp, a_ready, du_ready, dve_step = sem("a_exp"), sem("a_ready"), sem("du_ready"), sem("dve_step")
        b_ready, b_kept, c_ready, dA_ready, dBu_ready = (sem(n) for n in ("b_ready", "b_kept", "c_ready", "dA_ready", "dBu_ready"))
        scanned, hc_ready, summed, y_ready = sem("scanned"), sem("hc_ready"), sem("summed"), sem("y_ready")
        rest_kept = sem("rest_kept")
        out_ready, out_added, bc_ready, ysum_ready = sem("out_ready"), sem("out_added"), sem("bc_ready"), sem("ysum_ready")
        block = ctx.enter_context(nc.Block(no_gpsimd_drain=True))
        loads = ((win, "m_win"), (conv, "m_conv3"), (convb, "m_convb"), (wdt8, "m_wx_dt"), (wbc, "m_wx_bc"), (wdt, "m_wdt"),
                 (bdt, "m_bdt"), (A, "m_alog3"), (Dp, "m_D"), (wout, "m_wout"), (sel1, "sel32"))
        NW = 16 * len(loads)
        du = XI

        def du_of(h, b):
            return du[:, h, b, 0:SEQ]

        @block.sync
        def _(sp):
            for dst, k in loads:
                sp.dma_start(dst[:], d[k]).then_inc(w_in, 16)

        @block.tensor
        def _(pe):
            pe.wait_ge(w_in, NW)
            items = [(p, h, b) for p in range(2) for h in range(HALF) for b in range(NB)]
            for n, (p, h, b) in enumerate(items):
                if n >= 4:
                    pe.wait_ge(proj_kept, n - 3)
                for c in range(2):
                    mm = pe.matmul(work[n % 4][:, c * 512:(c + 1) * 512], win[:, p * DI + h * P:p * DI + (h + 1) * P],
                                   xnT[:, b * SEQ + c * 512:b * SEQ + (c + 1) * 512], start=True, stop=True)
                mm.then_inc(proj_ready, 1)
            for b in range(NB):
                pe.wait_ge(proj_kept, 8)
                pe.wait_ge(xc_ready, HALF * NB)
                for m, (wt, rows) in enumerate(((wbc, 2 * NS), (wdt8, RK))):
                    for c in range(2):
                        for h in range(HALF):
                            mm = pe.matmul(work[2 * b + m][0:rows, c * 512:(c + 1) * 512], wt[:, h, :],
                                           XC[:, h, b * SEQ + c * 512:b * SEQ + (c + 1) * 512],
                                           start=(h == 0), stop=(h == HALF - 1))
                    mm.then_inc(dbl_ready, 1)
            for n, (h, b) in enumerate((h, b) for h in range(HALF) for b in range(NB)):
                pe.wait_ge(dbl_kept, NB)
                pe.wait_ge(rest_kept, NB)
                for c in range(2):
                    mm = pe.matmul(work[n][:, c * 512:(c + 1) * 512], wdt[:, h * P:(h + 1) * P],
                                   dt8[:, b * SEQ + c * 512:b * SEQ + (c + 1) * 512], start=True, stop=True)
                mm.then_inc(step_ready, 1)
            pe.wait_ge(bc_ready, 1)
            pe.wait_ge(v_kept, 4)

            def rows(out, r, b, ready):
                for c in range(2):
                    mm = pe.matmul(out[:, c * 512:(c + 1) * 512], sel[:, r, :],
                                   bc[:, b * SEQ + c * 512:b * SEQ + (c + 1) * 512], start=True, stop=True)
                mm.then_inc(ready, 1)

            def total(b, i, j, first, last):
                for h in range(HALF):
                    pe.wait_ge(hc_ready, NS * HALF * b + i * 2 * HALF + j * HALF + h + 1)
                    for c in range(2):
                        mm = pe.matmul(ysum[h][:, c * 512:(c + 1) * 512], ident[:, :],
                                       hst[:, j, h, c * 512:(c + 1) * 512], start=first, stop=last,
                                       skip_group_check=True)
                mm.then_inc(summed, 1)

            def row_b(n, r, b):
                wait(pe, b_kept, n)
                rows(Bp, r, b, b_ready)

            row_b(0, 0, 0)
            for b in range(NB):
                def state(i, j, last, head=False):
                    n = NS * b + i * 2 + j
                    if not last:
                        row_b(n + 1, i * 2 + j + 1, b)
                    elif b + 1 < NB:
                        row_b(n + 1, 0, b + 1)
                    if head:
                        pe.wait_ge(hc_ready, n * HALF)
                        pe.wait_ge(y_ready, HALF * b)
                    else:
                        wait(pe, hc_ready, n * HALF)
                    rows(Cp, i * 2 + j + NS, b, c_ready)

                state(0, 0, False, head=b > 0)
                state(0, 1, False)
                total(b, 0, 0, True, False)
                with pe.Fori(1, NS // 2 - 1) as i:
                    state(i, 0, False)
                    total(b, i - 1, 1, False, False)
                    state(i, 1, False)
                    total(b, i, 0, False, False)
                state(NS // 2 - 1, 0, False)
                total(b, NS // 2 - 2, 1, False, False)
                state(NS // 2 - 1, 1, True)
                total(b, NS // 2 - 1, 0, False, False)
                total(b, NS // 2 - 1, 1, False, True)
                pe.wait_ge(ysum_ready, HALF * (b + 1))
                for g in range(2):
                    for t in range(4):
                        for h in range(HALF):
                            tok = b * SEQ + (4 * g + t) * P
                            mm = pe.matmul(ysum[g][:, t * P:(t + 1) * P], XC[:, h, tok:tok + P], wout[:, h, :],
                                           start=(h == 0), stop=(h == HALF - 1))
                    mm.then_inc(out_ready, 1)

        @block.scalar
        def _(act):
            act.wait_ge(w_in, NW)
            items = [(p, h, b) for p in range(2) for h in range(HALF) for b in range(NB)]
            for n, (p, h, b) in enumerate(items):
                act.wait_ge(proj_ready, n + 1)
                if p == 0:
                    act.wait_ge(pads, 1)
                    act.activation(XI[:, h, b, PAD:PAD + SEQ], work[n % 4][:, :], ACT.Copy).then_inc(proj_kept, 1)
                else:
                    act.activation(SZ[:, h, b * SEQ:(b + 1) * SEQ], work[n % 4][:, :], ACT.Silu).then_inc(proj_kept, 1)
            for n, (h, b) in enumerate((h, b) for h in range(HALF) for b in range(NB)):
                s = XC[:, h, b * SEQ:(b + 1) * SEQ]
                act.wait_ge(conv_ready, n + 1)
                act.activation(s, s, ACT.Silu, bias=convb[:, h:h + 1]).then_inc(xc_ready, 1)
            for b in range(NB):
                act.wait_ge(dbl_ready, 2 * b + 2)
                act.activation(dt8[:, b * SEQ:(b + 1) * SEQ], work[2 * b + 1][0:RK, :], ACT.Copy).then_inc(dbl_kept, 1)
            act.activation(A[:, :, :], A[:, :, :], ACT.Exp).then_inc(a_exp, 1)
            for h in range(HALF):
                if h:
                    act.wait_ge(dt_ready, h)
                for b in range(NB):
                    act.wait_ge(step_ready, NB * h + b + 1)
                    act.activation(Ex[:, b * SEQ:(b + 1) * SEQ], work[NB * h + b][:, :], ACT.Abs,
                                   bias=bdt[:, h:h + 1]).then_inc(abs_ready, 1)
                    act.activation(V[:, b * SEQ:(b + 1) * SEQ], work[NB * h + b][:, :], ACT.Identity,
                                   bias=bdt[:, h:h + 1]).then_inc(v_kept, 1)
                act.wait_ge(abs_ready, NB * (h + 1))
                act.activation(Ex[:, :], Ex[:, :], ACT.Exp, scale=-1.0).then_inc(e_ready, 1)
                act.wait_ge(u_ready, h + 1)
                act.activation(DT[:, h, :], DT[:, h, :], ACT.Ln).then_inc(ln_ready, 1)
            act.wait_ge(a_ready, 1)
            act.wait_ge(dt_ready, HALF)
            for b in range(NB):
                def states(i):
                    for j in range(2):
                        n = i * 2 + j + NS * b
                        act.wait_ge(b_ready, n + 1)
                        wait(act, dBu_ready, (n - 1) * HALF)
                        act.activation(BB[:, j, :], Bp[:, :], ACT.Copy).then_inc(b_kept, 1)
                        for h in range(HALF):
                            wait(act, scanned, (n - 1) * HALF)
                            act.activation(dA[:, j, h, :], DT[:, h, b * SEQ:(b + 1) * SEQ], ACT.Exp,
                                           scale=A[:, h, :][:, bass.ds(i * 2 + j, 1)]).then_inc(dA_ready, 1)

                states(0)
                with act.Fori(1, NS // 2) as i:
                    states(i)

        @block.gpsimd
        def _(pool):
            pool.memset(XI[:, :, :, 0:PAD], 0.0).then_inc(pads, 1)
            pool.wait_ge(du_ready, HALF * NB)
            for b in range(NB):
                def states(i):
                    for j in range(2):
                        n = i * 2 + j + NS * b
                        pool.wait_ge(b_kept, n + 1)
                        for h in range(HALF):
                            wait(pool, scanned, (n - 1) * HALF)
                            pool.tensor_tensor(dBu[:, j, h, :], du_of(h, b), BB[:, j, :], ALU.mult).then_inc(dBu_ready, 1)

                states(0)
                with pool.Fori(1, NS // 2) as i:
                    states(i)

        @block.vector
        def _(dve):
            step = Count(dve_step)
            dve.wait_ge(w_in, NW)
            dve.wait_ge(pads, 1)
            step.then_wait(dve, dve.tensor_copy(sel[:, :, :], spread(sel1[:, :], [96, 2 * NS, P])))
            for n, (h, b) in enumerate((h, b) for h in range(HALF) for b in range(NB)):
                dve.wait_ge(proj_kept, n + 1)
                s = XC[:, h, b * SEQ:(b + 1) * SEQ]
                step.then_wait(dve, dve.tensor_scalar(s, XI[:, h, b, 0:SEQ], conv[:, h, 0:1], None, ALU.mult))
                for k in range(1, KC):
                    ins = dve.scalar_tensor_tensor(s, XI[:, h, b, k:k + SEQ], conv[:, h, k:k + 1], s, ALU.mult, ALU.add)
                    if k < KC - 1:
                        step.then_wait(dve, ins)
                ins.then_inc(conv_ready, 1)
            for b in range(NB):
                c = slice(b * SEQ, (b + 1) * SEQ)
                dve.wait_ge(dbl_ready, 2 * b + 1)
                dve.tensor_copy(rest[:, c], work[2 * b][0:32, :]).then_inc(rest_kept, 1)
            dve.wait_ge(rest_kept, NB)
            for b in range(NB):
                c = slice(b * SEQ, (b + 1) * SEQ)
                step.then_wait(dve, dve.tensor_copy(bc[0:32, c], rest[:, c]))
                step.then_wait(dve, dve.tensor_tensor(rest[:, c], rest[:, c], bc[0:32, c], ALU.subtract))
                step.then_wait(dve, dve.tensor_copy(bc[32:64, c], rest[:, c]))
                step.then_wait(dve, dve.tensor_copy(bc[64:96, c], bc[32:64, c]))
                step.then_wait(dve, dve.tensor_tensor(rest[:, c], rest[:, c], bc[32:64, c], ALU.subtract))
                ins = dve.tensor_copy(bc[64:96, c], rest[:, c])
                if b == NB - 1:
                    ins.then_inc(bc_ready, 1)
                else:
                    step.then_wait(dve, ins)
            dve.wait_ge(a_exp, 1)
            dve.tensor_scalar(A[:, :, :], A[:, :, :], -1.0, None, ALU.mult).then_inc(a_ready, 1)
            for h in range(HALF):
                dve.wait_ge(v_kept, NB * (h + 1))
                dve.wait_ge(e_ready, h + 1)
                dve.tensor_scalar(DT[:, h, :], Ex[:, :], 1.0, None, ALU.add).then_inc(u_ready, 1)
                dve.wait_ge(u_ready, h + 1)
                step.then_wait(dve, dve.tensor_scalar(hst[:, 0, :, :].rearrange("p a b -> p (a b)"), Ex[:, :], 1.0, 1.0, ALU.add, ALU.subtract))
                step.then_wait(dve, dve.tensor_tensor(Ex[:, :], Ex[:, :], hst[:, 0, :, :].rearrange("p a b -> p (a b)"), ALU.subtract))
                step.then_wait(dve, dve.scalar_tensor_tensor(Ex[:, :], V[:, :], 0.0, Ex[:, :], ALU.max, ALU.add))
                dve.wait_ge(ln_ready, h + 1)
                dve.tensor_tensor(DT[:, h, :], DT[:, h, :], Ex[:, :], ALU.add).then_inc(dt_ready, 1)
            dve.wait_ge(dt_ready, HALF)
            dve.wait_ge(xc_ready, HALF * NB)
            for h in range(HALF):
                for b in range(NB):
                    c = slice(b * SEQ, (b + 1) * SEQ)
                    dve.tensor_tensor(du_of(h, b), DT[:, h, c], XC[:, h, c], ALU.mult).then_inc(du_ready, 1)

            def add(b):
                for g in range(2):
                    dve.wait_ge(out_ready, NB * b + g + 1)
                    s = x[:, b * ST + 4 * g:b * ST + 4 * g + 4, :]
                    dve.tensor_tensor(s, ysum[g][:, 0:512].rearrange("p (t w) -> p t w", t=4), s, ALU.add).then_inc(y_ready, 1)

            for b in range(NB):
                c = slice(b * SEQ, (b + 1) * SEQ)
                def states(i):
                    for j in range(2):
                        n = i * 2 + j + NS * b
                        wait(dve, summed, n - 1)
                        for h in range(HALF):
                            dve.wait_ge(dA_ready, n * HALF + h + 1)
                            dve.wait_ge(dBu_ready, n * HALF + h + 1)
                            dve.tensor_tensor_scan(hst[:, j, h, :], dA[:, j, h, :], dBu[:, j, h, :], 0.0,
                                                   ALU.mult, ALU.add).then_inc(scanned, 1)
                        dve.wait_ge(c_ready, n + 1)
                        for h in range(HALF):
                            dve.wait_ge(scanned, n * HALF + h + 1)
                            dve.tensor_tensor(hst[:, j, h, :], hst[:, j, h, :], Cp[:, :], ALU.mult).then_inc(hc_ready, 1)

                states(0)
                with dve.Fori(1, NS // 2) as i:
                    states(i)
                dve.wait_ge(summed, NS * (b + 1))
                for h in range(HALF):
                    step.then_wait(dve, dve.scalar_tensor_tensor(XC[:, h, c], XC[:, h, c], Dp[:, h:h + 1], ysum[h][:, :],
                                                                 ALU.mult, ALU.add))
                    dve.tensor_tensor(XC[:, h, c], XC[:, h, c], SZ[:, h, c], ALU.mult).then_inc(ysum_ready, 1)
                add(b)
def more_layouts(a, out):
    import numpy as np

    def chunks(w):
        return w.reshape(-1, P, w.shape[-1]).transpose(1, 0, 2)

    def experts(w):
        e, r, c = w.shape
        return w.reshape(e, r // P, P, c).transpose(0, 2, 1, 3).reshape(e * P, r // P * c)

    out["f0_w1"], out["f0_w2"] = a["L0_ffn_W1"], chunks(a["L0_ffn_W2"])
    vec = np.stack([a["L0_ffn_b1"], a["L0_ffn_quantum_phases"], a["L0_ffn_quantum_weights_real"],
                    a["L0_ffn_quantum_weights_imag"]])
    out["f0_vec"] = vec.reshape(4, -1, P).transpose(2, 0, 1)
    out["f0_b2"] = a["L0_ffn_b2"].reshape(1, P)
    out["a1_qkv"], out["a1_out"] = a["L1_attn_w_qkv"].T, a["L1_attn_w_out"].T
    out["a1_bout"] = a["L1_attn_b_out"].reshape(1, P)
    out["f1_wg"], out["f1_bg"] = a["L1_ffn_Wg"], a["L1_ffn_bg"].reshape(1, NE)
    out["f1_w1"], out["f1_w2"], out["f1_b2"] = experts(a["L1_ffn_W1"]), experts(a["L1_ffn_W2"]), a["L1_ffn_b2"]
    out["f1_b1"] = experts(a["L1_ffn_b1"][:, :, None])
    kgv = ("wk", "wg", "wv")
    out["a2_wkgv"] = np.concatenate([a[f"L2_attn_{n}_w"] for n in kgv], 1)
    out["a2_bkgv"] = np.concatenate([a[f"L2_attn_{n}_b"] for n in kgv]).reshape(1, 3 * P)
    out["a2_wq"], out["a2_bq"] = a["L2_attn_wq_w"], a["L2_attn_wq_b"].reshape(P, 1)
    out["a2_wo"], out["a2_bo"] = a["L2_attn_out_w"], a["L2_attn_out_b"].reshape(1, P)
    out["f2_router"] = a["L2_ffn_router_w"].T
    for n in ("wg", "wu", "wd"):
        out["f2_" + n] = experts(a["L2_ffn_" + n])
    out["m_win"], out["m_conv"], out["m_wdt"] = a["L3_attn_W_in"], a["L3_attn_conv_w"], a["L3_attn_W_dt"]
    out["m_conv3"] = chunks(a["L3_attn_conv_w"])
    for n, k in (("convb", "conv_b"), ("bdt", "b_dt"), ("D", "D")):
        out["m_" + n] = a["L3_attn_" + k].reshape(-1, P).T
    rk = a["L3_attn_W_dt"].shape[0]
    out["m_wx_dt"], out["m_wx_bc"] = chunks(a["L3_attn_W_x"][:, :rk]), chunks(a["L3_attn_W_x"][:, rk:])
    out["m_alog"], out["m_alog3"] = a["L3_attn_A_log"], chunks(a["L3_attn_A_log"])
    out["m_wout"] = chunks(a["L3_attn_W_out"])
    out["f3_wg"] = a["L3_ffn_gate_w"].T
    out["f3_bg"], out["f3_be"] = a["L3_ffn_gate_b"].reshape(1, NE), a["L3_ffn_expert_bias"].reshape(1, NE)
    out["f3_w1"], out["f3_w2"], out["f3_b2"] = experts(a["L3_ffn_w1"]), experts(a["L3_ffn_w2"]), a["L3_ffn_b2"]
    out["f3_b1"] = experts(a["L3_ffn_b1"][:, :, None])
    i = np.arange(P)
    f = np.float32
    out["heads"] = np.concatenate([i[:, None] // 8 == i[None] // 8, i[:, None] // 8 == np.arange(16)[None]], 1).astype(f)
    out["prio"] = np.arange(NE, 0, -1).reshape(1, NE).astype(f)
    out["same16"] = (i[:, None] // 16 == i[None] // 16).astype(f)
    out["pickrow"] = (i[:, None] == 16 * np.arange(NE)[None]).astype(f)
    dig = (i[:, None] % 16) << (28 - 4 * np.arange(8))[None]
    dig[:, 0] = np.minimum(i % 16, 7) << 28
    out["digits"] = dig.astype(np.int32)
    out["sel32"] = (np.arange(96)[:, None] % 32 == np.arange(32)[None]).astype(f)


def program(nc, d, out, upto=99, start=0):
    with ExitStack() as ctx:
        sb, pb, sem = scope(nc, ctx, "main")
        x = sb("x", [P, TT, P])
        xnT = sb("xnT", [P, TOK])
        ident = sb("ident", [P, P])
        gin = sb("gin", [P, 1])
        pick = sb("pick", [P, TT, NE])
        first_in, out_done = sem("first_in"), sem("out_done")
        with nc.Block(no_gpsimd_drain=True) as block:
            @block.sync
            def _(sp):
                sp.dma_start(ident[:, :], d["eye"]).then_inc(first_in, 16)
                sp.dma_start(gin[:, :], d["gin"]).then_inc(first_in, 16)
                for t in range(4):
                    sp.dma_start(x[:, 4 * t:4 * t + 4, :], d["x"][:, 4 * t:4 * t + 4, :]).then_inc(first_in, 16)
                sp.wait_ge(first_in, 6 * 16)

        def layer(n, name, f, **k):
            if start <= n < upto:
                prenorm(nc, "n" + name, x, xnT, ident, **k)
                f()

        layer(0, "0", lambda: l0_attention(nc, d, x, xnT, ident, None), rounds=2, gamma=gin[:, :])
        layer(1, "1", lambda: l0_ffn(nc, d, x, xnT))
        layer(2, "2", lambda: l1_attention(nc, d, x, xnT, ident))

        def l1_ffn():
            gate_top1(nc, "g1", d, ("f1_wg", ("f1_bg",), "f1_b2"), x, xnT, ident, pick)
            experts_dense(nc, "e1", "gelu", d, (("f1_w1",), "f1_b1", "f1_w2"), x, xnT, pick)

        def l2_ffn():
            route_top2(nc, d, x, xnT, ident, pick)
            experts_dense(nc, "e2", "silu", d, (("f2_wg", "f2_wu"), None, "f2_wd"), x, xnT, pick)

        def l3_ffn():
            gate_top1(nc, "g3", d, ("f3_wg", ("f3_bg", "f3_be"), "f3_b2"), x, xnT, ident, pick)
            experts_dense(nc, "e3", "relu", d, (("f3_w1",), "f3_b1", "f3_w2"), x, xnT, pick)

        layer(3, "3", l1_ffn)
        layer(4, "4", lambda: l2_attention(nc, d, x, xnT, ident))
        layer(5, "5", l2_ffn)
        layer(6, "6", lambda: l3_mixer(nc, d, x, xnT, ident))
        layer(7, "7", l3_ffn)
        with nc.Block(no_gpsimd_drain=True) as block:
            @block.sync
            def _(sp):
                for t in range(4):
                    sp.dma_start(out[:, 4 * t:4 * t + 4, :], x[:, 4 * t:4 * t + 4, :]).then_inc(out_done, 16)
                sp.wait_ge(out_done, 4 * 16)


def layouts(inputs):
    import numpy as np

    a = {k: np.ascontiguousarray(np.asarray(v)) for k, v in inputs.items()}
    out = {}
    out["x"] = a["L0_attn_x"].reshape(TT, P, P).transpose(1, 0, 2)
    wq, wk, wv = (a["L0_attn_" + n].reshape(P, PAIRS, P) for n in ("Wq", "Wk", "Wv"))
    out["wqkv"] = np.stack([wq, wk, wv], 2).transpose(1, 0, 2, 3).reshape(PAIRS * P, 3 * P)
    out["wo"] = a["L0_attn_Wo"].reshape(PAIRS, P, P).transpose(1, 0, 2)
    out["gnn_w"], out["gnn_bc"] = a["L0_attn_gnn_w"], a["L0_attn_gnn_b"].reshape(-1, DH, 1)
    out["lin_w"], out["lin_b"] = a["L0_attn_lin_w"], a["L0_attn_lin_b"].reshape(DH, 1)
    out["gin"], out["gout"] = a["L0_attn_gamma_in"].reshape(P, 1), a["L0_attn_gamma_out"].reshape(1, P)
    more_layouts(a, out)
    out["eye"] = np.eye(P, dtype=np.float32)
    out["cmask"] = np.triu(np.full((P, P), -1e38, np.float32), 1)
    return {k: np.ascontiguousarray(v) for k, v in out.items()}


def kernel(**inputs):
    import numpy as np
    import concourse.bacc as bacc
    from concourse.bass_utils import run_bass_kernel_spmd

    arrays = layouts(inputs)
    nc = bacc.Bacc("TRN2", target_bir_lowering=False, num_devices=1)
    d = {n: nc.dram_tensor(f"in_{n}", v.shape, mybir.dt.from_np(v.dtype), kind="ExternalInput").ap()
         for n, v in arrays.items()}
    out = nc.dram_tensor("out_x", (P, TT, P), F32, kind="ExternalOutput").ap()
    program(nc, d, out)
    r = run_bass_kernel_spmd(nc, [{f"in_{n}": v for n, v in arrays.items()}], core_ids=[0])
    got = np.asarray(r.results[0]["out_x"])
    return got.transpose(1, 0, 2).reshape(NB, SEQ, P)
```
